# Optimizing a Trainium2 kernel written in Bass

```python
import numpy as np
import jax
import jax.numpy as jnp

def _softmax(x, axis=-1):
    return jax.nn.softmax(x, axis=axis)

def _gelu(x):
    return jax.nn.gelu(x, approximate=True)

def _silu(x):
    return jax.nn.silu(x)

def _sigmoid(x):
    return jax.nn.sigmoid(x)

def _layernorm(x, axis=-1, eps=1e-05):
    m = jnp.mean(x, axis=axis, keepdims=True)
    v = jnp.var(x, axis=axis, keepdims=True)
    return (x - m) / jnp.sqrt(v + eps)

def _scatter_add(tgt, idx, src, axis=0):
    return tgt.at[idx].add(src)

def _segment_sum(src, seg, n):
    return jax.ops.segment_sum(src, seg, n)
kernel_name = 'mk_flamingo_gated_d4_seqx_r8_95bb12'

def setup_inputs(seed: int=0):
    np.random.seed(seed)
    _w = jnp.asarray

    def _rec_inputs():
        import jax
        import jax.numpy as jnp
        _rk = jax.random.key(seed)
        x = 7.22e-05 + 1 * jax.random.normal(jax.random.fold_in(_rk, 1), (4, 256, 128), jnp.float32)
        _lenS = 256 - jax.random.randint(jax.random.fold_in(_rk, 7), (4,), 0, max(1, 256 // 4) + 1, jnp.int32)
        _lenS2 = 256 - jax.random.randint(jax.random.fold_in(_rk, 8), (4,), 0, max(1, 256 // 4) + 1, jnp.int32)
        _ctx_1024P = jax.random.normal(jax.random.fold_in(_rk, 11), (4, 16, 128), jnp.float32)
        _ctx_1024c = jax.random.dirichlet(jax.random.fold_in(_rk, 511), 0.3 * jnp.ones((16,), jnp.float32), (4, 256))
        _ctx_1024t = jnp.einsum('bsk,bkd->bsd', _ctx_1024c, _ctx_1024P)
        _ctx_1024t = _ctx_1024t * jax.lax.rsqrt(jnp.mean(jnp.square(_ctx_1024t)) + 1e-12) * 0.953939
        ctx_1024 = 4.13588e-05 + 0.999923 * (_ctx_1024t + 0.3 * jax.random.normal(jax.random.fold_in(_rk, 611), (4, 256, 128), jnp.float32))
        _validS = jnp.arange(256)[None, :] < _lenS[:, None]
        _validS2 = jnp.arange(256)[None, :] < _lenS2[:, None]
        _causal = jnp.tril(jnp.ones((256, 256), dtype=bool))
        mask_BxSxS2_ik1 = jnp.where(jnp.broadcast_to(_validS2[:, None, :], (4, 256, 256)), 1, 0).astype(jnp.int32)
        mask_Bx1xSxS2_ik0 = jnp.where(jnp.broadcast_to(_validS2[:, None, None, :], (4, 1, 256, 256)), 0, 1).astype(jnp.int32)
        _g = jax.random.normal(jax.random.fold_in(_rk, 9001), (2, 4), jnp.float32)
        _g = jnp.sign(_g) * jnp.maximum(jnp.abs(_g), 1.0) + (_g == 0) * 1.0
        g_xattn = _g[0]
        g_ffn = _g[1]
        return (x, ctx_1024, mask_BxSxS2_ik1, mask_Bx1xSxS2_ik0, g_xattn, g_ffn)
    x, ctx_1024, mask_BxSxS2_ik1, mask_Bx1xSxS2_ik0, g_xattn, g_ffn = _rec_inputs()

    def _L0_xattn_setup():
        import jax, jax.numpy as jnp
        import numpy as np
        INPUT_DIM = 128
        HEADS = 16
        D_K = INPUT_DIM // HEADS
        B, S = (4, 256)
        key = jax.random.key(seed)
        ks = jax.random.split(key, 12)
        scale = 1.0 / np.sqrt(INPUT_DIM)
        inp = {'q': jax.random.normal(ks[0], (B, S, INPUT_DIM), jnp.float32), 'k': jax.random.normal(ks[1], (B, S, INPUT_DIM), jnp.float32), 'v': jax.random.normal(ks[2], (B, S, INPUT_DIM), jnp.float32), 'mask': jax.random.randint(ks[3], (B, S, S), 0, 2, jnp.int32), 'Wq': jax.random.normal(ks[4], (INPUT_DIM, INPUT_DIM), jnp.float32) * scale, 'bq': jnp.zeros((INPUT_DIM,), jnp.float32), 'Wk': jax.random.normal(ks[5], (INPUT_DIM, INPUT_DIM), jnp.float32) * scale, 'bk': jnp.zeros((INPUT_DIM,), jnp.float32), 'Wv': jax.random.normal(ks[6], (INPUT_DIM, INPUT_DIM), jnp.float32) * scale, 'bv': jnp.zeros((INPUT_DIM,), jnp.float32), 'Wo': jax.random.normal(ks[7], (INPUT_DIM, INPUT_DIM), jnp.float32) * scale, 'bo': jnp.zeros((INPUT_DIM,), jnp.float32)}
        return inp
    _L0_xattn_all = _L0_xattn_setup()
    _L0_xattn_in = {k: v for k, v in _L0_xattn_all.items() if k in ('Wq', 'bq', 'Wk', 'bk', 'Wv', 'bv', 'Wo', 'bo')}
    del _L0_xattn_all

    def _L0_ffn_setup():
        import jax, jax.numpy as jnp
        import numpy as np
        B, S, H, E, F = (2, 256, 128, 8, 512)
        key = jax.random.key(seed)
        k1, k2, k3, k4 = jax.random.split(key, 4)
        h = jax.random.normal(k1, (B, S, H), dtype=jnp.float32)
        Wr = jax.random.normal(k2, (H, E), dtype=jnp.float32) / np.sqrt(H)
        W1 = jax.random.normal(k3, (E, H, F), dtype=jnp.float32) / np.sqrt(H)
        W2 = jax.random.normal(k4, (E, F, H), dtype=jnp.float32) / np.sqrt(F)
        return {'h': h, 'Wr': Wr, 'W1': W1, 'W2': W2}
    _L0_ffn_all = _L0_ffn_setup()
    _L0_ffn_in = {k: v for k, v in _L0_ffn_all.items() if k in ('Wr', 'W1', 'W2')}
    del _L0_ffn_all

    def _L1_xattn_setup():
        import jax, jax.numpy as jnp
        import numpy as np
        EMBED = 128
        HEADS = 16
        HEAD_DIM = EMBED // HEADS
        key = jax.random.key(seed)
        ks = jax.random.split(key, 7)
        B, S = (4, 256)
        q = jax.random.normal(ks[0], (B, S, EMBED), dtype=jnp.float32)
        k = jax.random.normal(ks[1], (B, S, EMBED), dtype=jnp.float32)
        v = jax.random.normal(ks[2], (B, S, EMBED), dtype=jnp.float32)
        mask = jnp.broadcast_to(jnp.tril(jnp.ones((S, S), dtype=jnp.int32))[None, None], (B, 1, S, S))
        scale = 1.0 / np.sqrt(EMBED)
        w_q = jax.random.normal(ks[3], (EMBED, EMBED), dtype=jnp.float32) * scale
        w_k = jax.random.normal(ks[4], (EMBED, EMBED), dtype=jnp.float32) * scale
        w_v = jax.random.normal(ks[5], (EMBED, EMBED), dtype=jnp.float32) * scale
        w_o = jax.random.normal(ks[6], (EMBED, EMBED), dtype=jnp.float32) * scale
        return {'q': q, 'k': k, 'v': v, 'mask': mask, 'w_q': w_q, 'w_k': w_k, 'w_v': w_v, 'w_o': w_o}
    _L1_xattn_all = _L1_xattn_setup()
    _L1_xattn_in = {k: v for k, v in _L1_xattn_all.items() if k in ('w_q', 'w_k', 'w_v', 'w_o')}
    del _L1_xattn_all

    def _L1_ffn_setup():
        import math
        import jax, jax.numpy as jnp
        import numpy as np
        TOP_K = 2
        _GELU_C = math.sqrt(2.0 / math.pi)

        def gelu_new(x):
            return 0.5 * x * (1.0 + jnp.tanh(_GELU_C * (x + 0.044715 * x * x * x)))
        key = jax.random.key(seed)
        ks = jax.random.split(key, 6)
        B, T, C, E, H = (2, 256, 128, 8, 512)
        s_in = 1.0 / math.sqrt(C)
        s_hid = 1.0 / math.sqrt(H)
        return {'x': jax.random.normal(ks[0], (B, T, C), dtype=jnp.float32), 'router_w': jax.random.normal(ks[1], (E, C), dtype=jnp.float32) * s_in, 'w_fc': jax.random.normal(ks[2], (E, C, H), dtype=jnp.float32) * s_in, 'b_fc': jax.random.normal(ks[3], (E, H), dtype=jnp.float32) * 0.02, 'w_proj': jax.random.normal(ks[4], (E, H, C), dtype=jnp.float32) * s_hid, 'b_proj': jax.random.normal(ks[5], (E, C), dtype=jnp.float32) * 0.02}
    _L1_ffn_all = _L1_ffn_setup()
    _L1_ffn_in = {k: v for k, v in _L1_ffn_all.items() if k in ('router_w', 'w_fc', 'b_fc', 'w_proj', 'b_proj')}
    del _L1_ffn_all

    def _L2_xattn_setup():
        import jax, jax.numpy as jnp
        import numpy as np
        N_HEADS = 16
        WINDOW = 4
        NEG = -1000000000.0

        def local_mask(seq_len):
            i = jnp.arange(seq_len)
            return jnp.abs(i[:, None] - i[None, :]) <= WINDOW
        key = jax.random.key(seed)
        ks = jax.random.split(key, 8)
        B, S, D = (2, 256, 128)
        sc = 1.0 / np.sqrt(D)
        return {'query': jax.random.normal(ks[0], (B, S, D), jnp.float32), 'key': jax.random.normal(ks[1], (B, S, D), jnp.float32), 'value': jax.random.normal(ks[2], (B, S, D), jnp.float32), 'Wq': jax.random.normal(ks[3], (D, D), jnp.float32) * sc, 'Wk': jax.random.normal(ks[4], (D, D), jnp.float32) * sc, 'Wv': jax.random.normal(ks[5], (D, D), jnp.float32) * sc, 'Wo': jax.random.normal(ks[6], (D, D), jnp.float32) * sc, 'bo': jax.random.normal(ks[7], (D,), jnp.float32) * 0.01}
    _L2_xattn_all = _L2_xattn_setup()
    _L2_xattn_in = {k: v for k, v in _L2_xattn_all.items() if k in ('Wq', 'Wk', 'Wv', 'Wo', 'bo')}
    del _L2_xattn_all

    def _L2_ffn_setup():
        import jax, jax.numpy as jnp
        import numpy as np
        NUM_EXPERTS = 8
        TOP_K = 2

        def _swiglu(x, w1, w2, w3):
            return jax.nn.silu(x @ w1) * (x @ w3) @ w2
        key = jax.random.key(seed)
        ks = jax.random.split(key, 9)
        B, S, D, H, E = (1, 128, 128, 128, NUM_EXPERTS)
        std = 0.02
        return {'x': jax.random.normal(ks[0], (B, S, D), jnp.float32), 'router_w': jax.random.normal(ks[1], (D, E), jnp.float32) * std, 'expert_bias': jnp.zeros((E,), jnp.float32), 'w1': jax.random.normal(ks[2], (E, D, H), jnp.float32) * std, 'w2': jax.random.normal(ks[3], (E, H, D), jnp.float32) * std, 'w3': jax.random.normal(ks[4], (E, D, H), jnp.float32) * std, 'sw1': jax.random.normal(ks[5], (D, H), jnp.float32) * std, 'sw2': jax.random.normal(ks[6], (H, D), jnp.float32) * std, 'sw3': jax.random.normal(ks[7], (D, H), jnp.float32) * std}
    _L2_ffn_all = _L2_ffn_setup()
    _L2_ffn_in = {k: v for k, v in _L2_ffn_all.items() if k in ('router_w', 'expert_bias', 'w1', 'w2', 'w3', 'sw1', 'sw2', 'sw3')}
    del _L2_ffn_all

    def _L3_xattn_setup():
        import jax, jax.numpy as jnp
        import numpy as np
        D_MODEL = 128
        N_HEADS = 16
        D_K = D_MODEL // N_HEADS
        key = jax.random.key(seed)
        ks = jax.random.split(key, 12)
        B, S, D = (2, 256, D_MODEL)
        lim = 1.0 / np.sqrt(D)

        def lin(k):
            kw, kb = jax.random.split(k)
            W = jax.random.uniform(kw, (D, D), jnp.float32, -lim, lim)
            b = jax.random.uniform(kb, (D,), jnp.float32, -lim, lim)
            return (W, b)
        wq, bq = lin(ks[0])
        wk, bk = lin(ks[1])
        wv, bv = lin(ks[2])
        wo, bo = lin(ks[3])
        return {'query': jax.random.normal(ks[4], (B, S, D), jnp.float32), 'key': jax.random.normal(ks[5], (B, S, D), jnp.float32), 'value': jax.random.normal(ks[6], (B, S, D), jnp.float32), 'wq': wq, 'bq': bq, 'wk': wk, 'bk': bk, 'wv': wv, 'bv': bv, 'wo': wo, 'bo': bo, 'time_decay': jnp.float32(0.1)}
    _L3_xattn_all = _L3_xattn_setup()
    _L3_xattn_in = {k: v for k, v in _L3_xattn_all.items() if k in ('wq', 'bq', 'wk', 'bk', 'wv', 'bv', 'wo', 'bo', 'time_decay')}
    del _L3_xattn_all

    def _L3_ffn_setup():
        import jax, jax.numpy as jnp
        import numpy as np
        H, E, DFF = (128, 8, 512)
        key = jax.random.key(seed)
        ks = jax.random.split(key, 7)
        s = lambda *shape: 1.0 / np.sqrt(shape[-2] if len(shape) > 1 else shape[-1])
        x = jax.random.normal(ks[0], (2, 256, H), dtype=jnp.float32)
        Wr = jax.random.normal(ks[1], (H, E), dtype=jnp.float32) * (1.0 / np.sqrt(H))
        br = jnp.zeros((E,), dtype=jnp.float32)
        W1 = jax.random.normal(ks[2], (E, H, DFF), dtype=jnp.float32) * (1.0 / np.sqrt(H))
        b1 = jnp.zeros((E, DFF), dtype=jnp.float32)
        W2 = jax.random.normal(ks[3], (E, DFF, H), dtype=jnp.float32) * (1.0 / np.sqrt(DFF))
        b2 = jnp.zeros((E, H), dtype=jnp.float32)
        return {'x': x, 'Wr': Wr, 'br': br, 'W1': W1, 'b1': b1, 'W2': W2, 'b2': b2}
    _L3_ffn_all = _L3_ffn_setup()
    _L3_ffn_in = {k: v for k, v in _L3_ffn_all.items() if k in ('Wr', 'br', 'W1', 'b1', 'W2', 'b2')}
    del _L3_ffn_all
    return {'x': x, 'ctx_1024': ctx_1024, 'mask_BxSxS2_ik1': mask_BxSxS2_ik1, 'mask_Bx1xSxS2_ik0': mask_Bx1xSxS2_ik0, 'g_xattn': g_xattn, 'g_ffn': g_ffn, 'L0_xattn_Wq': _L0_xattn_in['Wq'], 'L0_xattn_bq': _L0_xattn_in['bq'], 'L0_xattn_Wk': _L0_xattn_in['Wk'], 'L0_xattn_bk': _L0_xattn_in['bk'], 'L0_xattn_Wv': _L0_xattn_in['Wv'], 'L0_xattn_bv': _L0_xattn_in['bv'], 'L0_xattn_Wo': _L0_xattn_in['Wo'], 'L0_xattn_bo': _L0_xattn_in['bo'], 'L0_ffn_Wr': _L0_ffn_in['Wr'], 'L0_ffn_W1': _L0_ffn_in['W1'], 'L0_ffn_W2': _L0_ffn_in['W2'], 'L1_xattn_w_q': _L1_xattn_in['w_q'], 'L1_xattn_w_k': _L1_xattn_in['w_k'], 'L1_xattn_w_v': _L1_xattn_in['w_v'], 'L1_xattn_w_o': _L1_xattn_in['w_o'], 'L1_ffn_router_w': _L1_ffn_in['router_w'], 'L1_ffn_w_fc': _L1_ffn_in['w_fc'], 'L1_ffn_b_fc': _L1_ffn_in['b_fc'], 'L1_ffn_w_proj': _L1_ffn_in['w_proj'], 'L1_ffn_b_proj': _L1_ffn_in['b_proj'], 'L2_xattn_Wq': _L2_xattn_in['Wq'], 'L2_xattn_Wk': _L2_xattn_in['Wk'], 'L2_xattn_Wv': _L2_xattn_in['Wv'], 'L2_xattn_Wo': _L2_xattn_in['Wo'], 'L2_xattn_bo': _L2_xattn_in['bo'], 'L2_ffn_router_w': _L2_ffn_in['router_w'], 'L2_ffn_expert_bias': _L2_ffn_in['expert_bias'], 'L2_ffn_w1': _L2_ffn_in['w1'], 'L2_ffn_w2': _L2_ffn_in['w2'], 'L2_ffn_w3': _L2_ffn_in['w3'], 'L2_ffn_sw1': _L2_ffn_in['sw1'], 'L2_ffn_sw2': _L2_ffn_in['sw2'], 'L2_ffn_sw3': _L2_ffn_in['sw3'], 'L3_xattn_wq': _L3_xattn_in['wq'], 'L3_xattn_bq': _L3_xattn_in['bq'], 'L3_xattn_wk': _L3_xattn_in['wk'], 'L3_xattn_bk': _L3_xattn_in['bk'], 'L3_xattn_wv': _L3_xattn_in['wv'], 'L3_xattn_bv': _L3_xattn_in['bv'], 'L3_xattn_wo': _L3_xattn_in['wo'], 'L3_xattn_bo': _L3_xattn_in['bo'], 'L3_xattn_time_decay': _L3_xattn_in['time_decay'], 'L3_ffn_Wr': _L3_ffn_in['Wr'], 'L3_ffn_br': _L3_ffn_in['br'], 'L3_ffn_W1': _L3_ffn_in['W1'], 'L3_ffn_b1': _L3_ffn_in['b1'], 'L3_ffn_W2': _L3_ffn_in['W2'], 'L3_ffn_b2': _L3_ffn_in['b2']}

def reference(x, ctx_1024, mask_BxSxS2_ik1, mask_Bx1xSxS2_ik0, g_xattn, g_ffn, L0_xattn_Wq, L0_xattn_bq, L0_xattn_Wk, L0_xattn_bk, L0_xattn_Wv, L0_xattn_bv, L0_xattn_Wo, L0_xattn_bo, L0_ffn_Wr, L0_ffn_W1, L0_ffn_W2, L1_xattn_w_q, L1_xattn_w_k, L1_xattn_w_v, L1_xattn_w_o, L1_ffn_router_w, L1_ffn_w_fc, L1_ffn_b_fc, L1_ffn_w_proj, L1_ffn_b_proj, L2_xattn_Wq, L2_xattn_Wk, L2_xattn_Wv, L2_xattn_Wo, L2_xattn_bo, L2_ffn_router_w, L2_ffn_expert_bias, L2_ffn_w1, L2_ffn_w2, L2_ffn_w3, L2_ffn_sw1, L2_ffn_sw2, L2_ffn_sw3, L3_xattn_wq, L3_xattn_bq, L3_xattn_wk, L3_xattn_bk, L3_xattn_wv, L3_xattn_bv, L3_xattn_wo, L3_xattn_bo, L3_xattn_time_decay, L3_ffn_Wr, L3_ffn_br, L3_ffn_W1, L3_ffn_b1, L3_ffn_W2, L3_ffn_b2):
    import jax
    import jax.numpy as jnp

    def _L0_xattn_ref(q, k, v, mask, Wq, bq, Wk, bk, Wv, bv, Wo, bo):
        import jax, jax.numpy as jnp
        import numpy as np
        INPUT_DIM = 128
        HEADS = 16
        D_K = INPUT_DIM // HEADS
        B, S = (4, 256)
        bs = q.shape[0]

        def proj(x, W, b):
            return (x @ W.T + b).reshape(bs, -1, HEADS, D_K).transpose(0, 2, 1, 3)
        qh, kh, vh = (proj(q, Wq, bq), proj(k, Wk, bk), proj(v, Wv, bv))
        scores = jnp.einsum('bhqd,bhkd->bhqk', qh, kh) / jnp.sqrt(jnp.float32(D_K))
        scores = jnp.where(mask[:, None] == 0, jnp.float32(-1000000000.0), scores)
        attn = jax.nn.softmax(scores, axis=-1)
        ctx = jnp.einsum('bhqk,bhkd->bhqd', attn, vh)
        concat = ctx.transpose(0, 2, 1, 3).reshape(bs, -1, INPUT_DIM)
        return concat @ Wo.T + bo

    def _L0_ffn_ref(h, Wr, W1, W2):
        import jax, jax.numpy as jnp
        import numpy as np
        B, S, H, E, F = (2, 256, 128, 8, 512)
        g = jax.nn.softmax(h @ Wr, axis=-1)
        top2_w, top2_idx = jax.lax.top_k(g, 2)
        top2_w = top2_w / jnp.sum(top2_w, axis=-1, keepdims=True)
        hid = jax.nn.relu(jnp.einsum('bsh,ehf->bsef', h, W1))
        expert_out = jnp.einsum('bsef,efh->bseh', hid, W2)
        top2_out = jnp.take_along_axis(expert_out, top2_idx[..., None], axis=2)
        return jnp.sum(top2_out * top2_w[..., None], axis=2)

    def _L1_xattn_ref(q, k, v, mask, w_q, w_k, w_v, w_o):
        import jax, jax.numpy as jnp
        import numpy as np
        EMBED = 128
        HEADS = 16
        HEAD_DIM = EMBED // HEADS
        B, S, _ = q.shape

        def proj(x, w):
            return (x @ w.T).reshape(B, -1, HEADS, HEAD_DIM).transpose(0, 2, 1, 3)
        qh, kh, vh = (proj(q, w_q), proj(k, w_k), proj(v, w_v))
        scores = jnp.einsum('bhqd,bhkd->bhqk', qh, kh) / jnp.sqrt(jnp.float32(HEAD_DIM))
        scores = jnp.where(mask == 0, jnp.float32(-1000000000.0), scores)
        attn = jax.nn.softmax(scores, axis=-1)
        x = jnp.einsum('bhqk,bhkd->bhqd', attn, vh)
        x = x.transpose(0, 2, 1, 3).reshape(B, S, HEADS * HEAD_DIM)
        return x @ w_o.T

    def _L1_ffn_ref(x, router_w, w_fc, b_fc, w_proj, b_proj):
        import math
        import jax, jax.numpy as jnp
        import numpy as np
        TOP_K = 2
        _GELU_C = math.sqrt(2.0 / math.pi)

        def gelu_new(x):
            return 0.5 * x * (1.0 + jnp.tanh(_GELU_C * (x + 0.044715 * x * x * x)))
        B, T, C = x.shape
        E = router_w.shape[0]
        N = B * T
        xf = x.reshape(N, C)
        logits = xf @ router_w.T
        probs = jax.nn.softmax(logits, axis=-1)
        topk_probs, topk_idx = jax.lax.top_k(probs, TOP_K)
        topk_probs = topk_probs / jnp.sum(topk_probs, axis=-1, keepdims=True)
        combine = jnp.zeros((N, E), dtype=x.dtype).at[jnp.arange(N)[:, None], topk_idx].add(topk_probs)
        h = gelu_new(jnp.einsum('nc,ech->neh', xf, w_fc) + b_fc)
        out = jnp.einsum('neh,ehc->nec', h, w_proj) + b_proj
        y = jnp.einsum('nec,ne->nc', out, combine)
        return y.reshape(B, T, C)

    def _L2_xattn_ref(query, key, value, Wq, Wk, Wv, Wo, bo):
        import jax, jax.numpy as jnp
        import numpy as np
        N_HEADS = 16
        WINDOW = 4
        NEG = -1000000000.0

        def local_mask(seq_len):
            i = jnp.arange(seq_len)
            return jnp.abs(i[:, None] - i[None, :]) <= WINDOW
        B, S, D = query.shape
        H = N_HEADS
        dk = D // H
        Q = (query @ Wq.T).reshape(B, S, H, dk).transpose(0, 2, 1, 3)
        K = (key @ Wk.T).reshape(B, S, H, dk).transpose(0, 2, 1, 3)
        V = (value @ Wv.T).reshape(B, S, H, dk).transpose(0, 2, 1, 3)
        scores = jnp.einsum('bhqd,bhkd->bhqk', Q, K) / jnp.sqrt(jnp.asarray(dk, Q.dtype))
        mask = local_mask(S)
        scores = jnp.where(mask[None, None, :, :], scores, NEG)
        attn = jax.nn.softmax(scores, axis=-1)
        out = jnp.einsum('bhqk,bhkd->bhqd', attn, V)
        out = out.transpose(0, 2, 1, 3).reshape(B, S, D)
        return out @ Wo.T + bo

    def _L2_ffn_ref(x, router_w, expert_bias, w1, w2, w3, sw1, sw2, sw3):
        import jax, jax.numpy as jnp
        import numpy as np
        NUM_EXPERTS = 8
        TOP_K = 2

        def _swiglu(x, w1, w2, w3):
            return jax.nn.silu(x @ w1) * (x @ w3) @ w2
        B, S, D = x.shape
        E, K = (NUM_EXPERTS, TOP_K)
        N = B * S
        x_flat = x.reshape(N, D)
        logits = x_flat @ router_w
        scores = jax.nn.softmax(logits.astype(jnp.float32), axis=-1)
        _, sel = jax.lax.top_k(scores + expert_bias[None, :], K)
        top_scores = jnp.take_along_axis(scores, sel, axis=-1)
        flat_exp = sel.reshape(-1)
        order = jnp.argsort(flat_exp)
        exp_sorted = flat_exp[order]
        routed_input = x_flat[order // K]
        routed_output = jnp.zeros_like(routed_input)
        for e in range(E):
            mask = (exp_sorted == e)[:, None]
            y_e = _swiglu(routed_input, w1[e], w2[e], w3[e])
            routed_output = routed_output + jnp.where(mask, y_e, 0.0)
        unsorted = jnp.zeros((N * K, D), routed_output.dtype).at[order].set(routed_output)
        unsorted = unsorted.reshape(N, K, D)
        out_experts = jnp.einsum('nk,nkd->nd', top_scores, unsorted)
        shared_out = _swiglu(x_flat, sw1, sw2, sw3)
        return (shared_out + out_experts).reshape(B, S, D)

    def _L3_xattn_ref(query, key, value, wq, bq, wk, bk, wv, bv, wo, bo, time_decay):
        import jax, jax.numpy as jnp
        import numpy as np
        D_MODEL = 128
        N_HEADS = 16
        D_K = D_MODEL // N_HEADS
        B, S, D = query.shape
        H, Dk = (N_HEADS, D_K)

        def proj(x, W, b):
            y = jnp.einsum('bsd,ed->bse', x, W) + b
            return y.reshape(B, S, H, Dk).transpose(0, 2, 1, 3)
        Q = proj(query, wq, bq)
        K = proj(key, wk, bk)
        V = proj(value, wv, bv)
        scores = jnp.einsum('bhqd,bhkd->bhqk', Q, K) / jnp.sqrt(jnp.float32(Dk))
        pos = jnp.arange(S, dtype=jnp.float32)
        decay = -time_decay * jnp.abs(pos[:, None] - pos[None, :])
        scores = scores + decay[None, None, :, :]
        attn = jax.nn.softmax(scores, axis=-1)
        ctx = jnp.einsum('bhqk,bhkd->bhqd', attn, V)
        ctx = ctx.transpose(0, 2, 1, 3).reshape(B, S, D)
        out = jnp.einsum('bsd,ed->bse', ctx, wo) + bo
        return out

    def _L3_ffn_ref(x, Wr, br, W1, b1, W2, b2):
        import jax, jax.numpy as jnp
        import numpy as np
        H, E, DFF = (128, 8, 512)
        B, S, Hd = x.shape
        n_exp = W1.shape[0]
        xt = x.reshape(-1, Hd)
        logits = xt @ Wr + br
        probs = jax.nn.softmax(logits, axis=-1)
        gate = jnp.max(probs, axis=-1)
        idx = jnp.argmax(probs, axis=-1)
        h1 = jnp.maximum(jnp.einsum('th,ehf->etf', xt, W1) + b1[:, None, :], 0.0)
        ye = jnp.einsum('etf,efh->eth', h1, W2) + b2[:, None, :]
        onehot = jax.nn.one_hot(idx, n_exp, dtype=xt.dtype)
        y = jnp.einsum('te,eth->th', onehot, ye) * gate[:, None]
        return y.reshape(B, S, Hd)
    x = x + jnp.tanh(g_xattn[0]) * _L0_xattn_ref(_layernorm(x, axis=-1), ctx_1024, ctx_1024, mask_BxSxS2_ik1, L0_xattn_Wq, L0_xattn_bq, L0_xattn_Wk, L0_xattn_bk, L0_xattn_Wv, L0_xattn_bv, L0_xattn_Wo, L0_xattn_bo)
    x = x + jnp.tanh(g_ffn[0]) * _L0_ffn_ref(_layernorm(x, axis=-1), L0_ffn_Wr, L0_ffn_W1, L0_ffn_W2)
    x = x + jnp.tanh(g_xattn[1]) * _L1_xattn_ref(_layernorm(x, axis=-1), ctx_1024, ctx_1024, mask_Bx1xSxS2_ik0, L1_xattn_w_q, L1_xattn_w_k, L1_xattn_w_v, L1_xattn_w_o)
    x = x + jnp.tanh(g_ffn[1]) * _L1_ffn_ref(_layernorm(x, axis=-1), L1_ffn_router_w, L1_ffn_w_fc, L1_ffn_b_fc, L1_ffn_w_proj, L1_ffn_b_proj)
    x = x + jnp.tanh(g_xattn[2]) * _L2_xattn_ref(_layernorm(x, axis=-1), ctx_1024, ctx_1024, L2_xattn_Wq, L2_xattn_Wk, L2_xattn_Wv, L2_xattn_Wo, L2_xattn_bo)
    x = x + jnp.tanh(g_ffn[2]) * _L2_ffn_ref(_layernorm(x, axis=-1), L2_ffn_router_w, L2_ffn_expert_bias, L2_ffn_w1, L2_ffn_w2, L2_ffn_w3, L2_ffn_sw1, L2_ffn_sw2, L2_ffn_sw3)
    x = x + jnp.tanh(g_xattn[3]) * _L3_xattn_ref(_layernorm(x, axis=-1), ctx_1024, ctx_1024, L3_xattn_wq, L3_xattn_bq, L3_xattn_wk, L3_xattn_bk, L3_xattn_wv, L3_xattn_bv, L3_xattn_wo, L3_xattn_bo, L3_xattn_time_decay)
    x = x + jnp.tanh(g_ffn[3]) * _L3_ffn_ref(_layernorm(x, axis=-1), L3_ffn_Wr, L3_ffn_br, L3_ffn_W1, L3_ffn_b1, L3_ffn_W2, L3_ffn_b2)
    return x

_drawn_inputs = setup_inputs


def setup_inputs(seed=0):
    import zlib

    import numpy as np

    out = dict(_drawn_inputs(seed))
    spreads = {'L0_xattn_bq': (0.0, 0.1),
     'L0_xattn_bk': (0.0, 2.0),
     'L0_xattn_bv': (0.0, 0.1),
     'L0_xattn_bo': (0.0, 0.1),
     'L2_ffn_expert_bias': (0.0, 0.8),
     'L3_ffn_br': (0.0, 0.351),
     'L3_ffn_b1': (0.0, 0.519),
     'L3_ffn_b2': (0.0, 0.381)}
    factors = {'L1_ffn_b_fc': 5.445,
     'L1_ffn_b_proj': 4.057,
     'L2_xattn_bo': 7.536,
     'L2_ffn_router_w': 8.0,
     'L2_ffn_w1': 8.0,
     'L2_ffn_w2': 8.0,
     'L2_ffn_w3': 8.0,
     'L2_ffn_sw1': 6.962,
     'L2_ffn_sw2': 8.0,
     'L2_ffn_sw3': 7.953,
     'L3_xattn_wq': 3.185,
     'L3_xattn_bq': 31.51,
     'L3_xattn_wk': 3.3,
     'L3_xattn_bk': 64.0,
     'L3_xattn_bv': 8.821,
     'L3_xattn_bo': 4.285}
    for name, (base, spread) in spreads.items():
        noise = np.random.default_rng([zlib.crc32(name.encode()), seed]).standard_normal(out[name].shape)
        drawn = base * np.exp(spread * noise) if base else spread * noise
        out[name] = jnp.asarray(drawn.astype(out[name].dtype))
    for name, factor in factors.items():
        out[name] = (out[name] * factor).astype(out[name].dtype)
    return out
```

```python
import concourse.bass as bass
from concourse import mybir
from contextlib import ExitStack

F32 = mybir.dt.float32
F32R = mybir.dt.float32r
BF16 = mybir.dt.bfloat16
I32 = mybir.dt.int32
U32 = mybir.dt.uint32
ALU = mybir.AluOpType
ACT = mybir.ActivationFunctionType
AX = mybir.AxisListType.X

P = 128
LAYERS, BATCH, S, D = 4, 4, 256, 128
LANES = 2
PAIRS = BATCH // LANES
TT = S // P
HEADS, DK = 16, 8
GROUPS, GH = 4, 4
STEPS = HEADS // 2
EXPERTS, FF = 8, 512
CH = FF // P
PHASES = LAYERS * LANES
BIG = float(2 ** 100)
EPS = 1e-5
WINDOW = 4
BAND = P + WINDOW
GELU_A = 0.044715
GELU_C = 0.7978845608028654
GATE_LINKS = (12, 12, 10, 8)
VW = P + DK


def window(layer, tile):
    return (tile * (S - BAND), BAND) if layer == 2 else (0, S)


def experts(layer):
    return EXPERTS + 1 if layer == 2 else EXPERTS


def experts_before(n):
    return sum(experts(m // LANES) for m in range(n))


def flamingo_layers(nc, ins, out):
    ctx = ExitStack()
    with ctx:
        def sb(name, shape, dt=F32):
            return ctx.enter_context(nc.sbuf_tensor(name, shape, dt))

        def pb(name, shape, dt=F32):
            return ctx.enter_context(nc.psum_tensor(name, shape, dt))

        def sem(name):
            return ctx.enter_context(nc.semaphore(name))

        wq = sb("wq", [P, LAYERS, D])
        wk = sb("wk", [P, LAYERS, D])
        wv = sb("wv", [P, LAYERS, D])
        wo = sb("wo", [P, LAYERS, D])
        up_w = {l: sb(f"up_w{l}", [P, EXPERTS, FF]) for l in (0, 1, 3)}
        down_w = {l: sb(f"down_w{l}", [P, EXPERTS, CH, D]) for l in (0, 1, 3)}
        glu_w1 = sb("glu_w1", [P, EXPERTS + 1, D])
        glu_w3 = sb("glu_w3", [P, EXPERTS + 1, D])
        glu_w2 = sb("glu_w2", [P, EXPERTS + 1, D])
        router = sb("router", [P, LAYERS, EXPERTS])
        col_bias = {n: sb(n, [P, 1]) for n in ("bq0", "bk0", "bq3", "bk3")}
        bv = {l: sb(f"bv{l}", [P, D]) for l in (0, 3)}
        bo = {l: sb(f"bo{l}", [P, D]) for l in (0, 2, 3)}
        hid_bias = {l: sb(f"hid_bias{l}", [P, EXPERTS, CH]) for l in (1, 3)}
        out_bias = {l: sb(f"out_bias{l}", [P, D]) for l in (1, 3)}
        route_bias = {l: sb(f"route_bias{l}", [P, EXPERTS]) for l in (2, 3)}
        gates = sb("gates", [P, 2 * LAYERS])
        tanh_g = sb("tanh_g", [P, 2 * LAYERS])
        time_decay = sb("time_decay", [P, 1])

        ident = sb("ident", [P, P])
        ident_r = sb("ident_r", [P, P], F32R)
        ident_b = sb("ident_b", [P, P], BF16)
        spread_two = {"q": sb("spread_q_high", [P, GROUPS, P], F32R), "k": sb("spread_k_high", [P, GROUPS, P], F32R)}
        spread_one = {"q": sb("spread_q_low", [P, GROUPS, P], F32R), "k": sb("spread_k_low", [P, GROUPS, P], F32R)}
        ones_rows = sb("ones_rows", [P, 1])
        minus_half = sb("minus_half", [P, TT])
        iota8 = sb("iota8", [P, EXPERTS])
        decay_hi = sb("decay_hi", [P, TT, S], F32R)
        decay_lo = sb("decay_lo", [P, TT, S], F32R)
        band = sb("band", [P, TT, BAND], BF16)

        x = [sb(f"x{b}", [P, TT, D]) for b in range(LANES)]
        ctx_t = [sb(f"ctx_t{b}", [P, S]) for b in range(LANES)]
        mask = [[[sb(f"mask{b}{m}{o}", [P, TT, S], BF16) for o in range(2)] for m in range(2)] for b in range(LANES)]

        q_stack = sb("q_stack", [P, GROUPS, S], F32R)
        k_stack = sb("k_stack", [P, GROUPS, S], F32R)
        qm_stack = sb("qm_stack", [P, 2, S], F32R)
        qkv_hi = {"q": qm_stack[:, 0, :], "k": q_stack[:, 0, :]}
        qkv_lo = {"q": qm_stack[:, 1, :], "k": q_stack[:, 1, :]}
        v_cols = sb("v_cols", [P, TT, 2, (HEADS // 2) * VW])
        row_max = sb("row_max", [P, HEADS, TT])
        max_parts = sb("max_parts", [P, TT, GH, 32], F32R)
        probs = sb("probs", [P, 2, 2, TT, S])
        inv_sum = probs[0:P // 2, 0, 0, :, :].rearrange("p t n -> p (t n)")
        heads_t = probs[:, 1, 0, 0, :]
        iota_i = probs[:, 0, 0, :, :].bitcast(I32)
        dist, dist_neg = probs[:, 0, 1, :, :], probs[:, 1, 0, :, :]

        hidden = sb("hidden", [P, 2, CH, S])
        pre_act = sb("pre_act", [P, 2, 2, S])
        gelu_t = sb("gelu_t", [P, 2, 2, S])
        acc = sb("acc", [P, TT, D])
        logit = sb("logit", [P, TT, EXPERTS])
        logit_max = sb("logit_max", [P, TT])
        shifted = sb("shifted", [P, TT, EXPERTS])
        exp_l = sb("exp_l", [P, TT, EXPERTS])
        exp_sum = sb("exp_sum", [P, TT])
        exp_inv = sb("exp_inv", [P, TT])
        prob = sb("prob", [P, TT, EXPERTS])
        choice = sb("choice", [P, TT, EXPERTS])
        top8 = sb("top8", [P, TT, 8])
        top_idx = sb("top_idx", [P, TT, 8], U32)
        top_f = sb("top_f", [P, TT, 8])
        pick1 = sb("pick1", [P, TT, EXPERTS])
        pick2 = sb("pick2", [P, TT, EXPERTS])
        picked = sb("picked", [P, TT, EXPERTS])
        gate_raw = sb("gate_raw", [P, TT, EXPERTS])
        gate_sum = sb("gate_sum", [P, TT])
        gate_inv = sb("gate_inv", [P, TT])
        gate_pad = sb("gate_pad", [P, TT, P])
        gate_use = sb("gate_use", [P, TT, EXPERTS])
        gate_t = gelu_t[:, 0, 0, :]
        mask_in = [pre_act[:, i, :, :].bitcast(I32) for i in range(2)]

        smax = pb("smax", [P, 2, 512])
        sexp = pb("sexp", [P, 2, 512])
        cbank = pb("cbank", [P, 512])
        ybank = pb("ybank", [P, 512])
        hbank = pb("hbank", [P, 2, 512])

        w_attn, w_small = sem("w_attn"), sem("w_small")
        w_up = {l: sem(f"w_up{l}") for l in range(LAYERS)}
        w_down = {l: sem(f"w_down{l}") for l in range(LAYERS)}
        zeroed, ident_made, spread_made, const_made = sem("zeroed"), sem("ident_made"), sem("spread_made"), sem("const_made")
        iota_made, dist_made, decay_made, tanh_made, v_set = (
            sem("iota_made"), sem("dist_made"), sem("decay_made"), sem("tanh_made"), sem("v_set"))

        class Norm:

            def __init__(self, tag):
                self.stats = sb(f"{tag}_stats", [P, TT, 6])
                self.mean_var = sb(f"{tag}_mean_var", [P, TT, 2])
                self.var_eps = sb(f"{tag}_var_eps", [P, TT])
                self.rstd = sb(f"{tag}_rstd", [P, TT])
                self.normed = sb(f"{tag}_normed", [P, TT, D])
                self.normed_t = sb(f"{tag}_normed_t", [P, S])
                self.stats_done = sem(f"{tag}_stats_done")
                self.aggr_done = sem(f"{tag}_aggr_done")
                self.eps_added = sem(f"{tag}_eps_added")
                self.rstd_done = sem(f"{tag}_rstd_done")
                self.normed_done = sem(f"{tag}_normed_done")
                self.turned = sem(f"{tag}_turned")
                self.turned_sb = sem(f"{tag}_turned_sb")

        first_loop_sem = sem("loop_first")
        an, fn = Norm("attn"), Norm("ffn")
        x_res = an.normed
        x_loaded = [sem(f"x_loaded{b}") for b in range(LANES)]
        ctx_loaded = [sem(f"ctx_loaded{b}") for b in range(LANES)]
        x_new = [sem(f"x_new{b}") for b in range(LANES)]
        mask_loaded = [sem("mask_loaded0"), sem("mask_loaded1")]
        mask_made, stored = sem("mask_made"), sem("stored")
        k_proj, v_proj, q_proj = sem("k_proj"), sem("v_proj"), sem("q_proj")
        k_hi, k_lo, q_hi, q_lo, v_ready = sem("k_hi_s"), sem("k_lo_s"), sem("q_hi_s"), sem("q_lo_s"), sem("v_ready")
        k_spread, q_spread, k_ready, q_ready = sem("k_spread"), sem("q_spread"), sem("k_ready"), sem("q_ready")
        max_psum, max_red, max_hi, max_lo = sem("max_psum"), sem("max_red"), sem("max_hi"), sem("max_lo")
        max_turned, qm_ready, exp_psum, exp_done, pv_done = (
            sem("max_turned"), sem("qm_ready"), sem("exp_psum"), sem("exp_done"), sem("pv_done"))
        inv_done, heads_ready, attn_out, res_ready = sem("inv_done"), sem("heads_ready"), sem("attn_out"), sem("res_ready")
        logits_psum, gate_step, gate_max, gate_shifted = (
            sem("logits_psum"), sem("gate_step"), sem("gate_max"), sem("gate_shifted"))
        exp_l_done, gate_chain, gate_ready = sem("exp_l_done"), sem("gate_chain"), sem("gate_ready")
        up_psum, hid_ready, y_psum, y_acc = sem("up_psum"), sem("hid_ready"), sem("y_psum"), sem("y_acc")
        pre_ready, sq_ready, inner_ready, tanh_ready = sem("pre_ready"), sem("sq_ready"), sem("inner_ready"), sem("tanh_ready")
        glu_tanh, glu_silu = sem("glu_tanh"), sem("glu_silu")
        gate_turned, gate_t_ready, bias_psum, bias_added = (
            sem("gate_turned"), sem("gate_t_ready"), sem("bias_psum"), sem("bias_added"))
        last_loop_sem = sem("loop_last")

        def v_view(lo):
            return v_cols[:, :, :, :].rearrange("p t u (j c) -> p t u j c", c=VW)[:, :, :, :, lo:lo + DK]

        def score_bias(eng_mm, bank, lane, layer, orient):
            if layer == 3:
                eng_mm(bank, ident_r[:, :], decay_hi[:, :, :].rearrange("p t n -> p (t n)"), start=True, stop=False,
                       skip_group_check=True)
                eng_mm(bank, ident_r[:, :], decay_lo[:, :, :].rearrange("p t n -> p (t n)"), start=False, stop=False,
                       skip_group_check=True)
            elif layer == 2:
                eng_mm(bank.rearrange("p (t n) -> p t n", t=TT)[:, :, 0:BAND], ident_b[:, :], band[:, :, :],
                       start=True, stop=False, skip_group_check=True)
            else:
                m = mask[lane][layer][orient]
                eng_mm(bank, ident_b[:, :], m[:, :, :].rearrange("p t n -> p (t n)"), start=True, stop=False,
                       skip_group_check=True)

        small = [
            (router[:, :, :], ins["router"].rearrange("l p e -> p l e")),
            (gates[:, :], ins["gates"].partition_broadcast(P)),
            (time_decay[:, :], ins["time_decay"].partition_broadcast(P)),
        ]
        for n in ("bq0", "bk0", "bq3", "bk3"):
            small.append((col_bias[n][:, :], ins[n].rearrange("(p a) -> p a", a=1)))
        for l in (0, 3):
            small.append((bv[l][:, :], ins[f"bv{l}"].partition_broadcast(P)))
        for l in (0, 2, 3):
            small.append((bo[l][:, :], ins[f"bo{l}"].partition_broadcast(P)))
        for l in (2, 3):
            small.append((route_bias[l][:, :], ins[f"route_bias{l}"].partition_broadcast(P)))
        for l in (1, 3):
            small.append((hid_bias[l][:, :, :], ins[f"hid_bias{l}"].rearrange("p (e c) -> p e c", c=CH)))
            small.append((out_bias[l][0:EXPERTS, :], ins[f"out_bias{l}"]))
        SMALL = 16 * len(small)

        with nc.Block(no_gpsimd_drain=True) as block:
            @block.sync
            def _(sp):
                for w, name in ((wk, "wk"), (wv, "wv"), (wq, "wq"), (wo, "wo")):
                    sp.dma_start(w[:, :, :], ins[name].rearrange("l p n -> p l n")).then_inc(w_attn, 16)
                sp.wait_ge(zeroed, 2)
                for dst, src in small:
                    sp.dma_start(dst, src).then_inc(w_small, 16)

            @block.scalar
            def _(act):
                for l in range(LAYERS):
                    if l == 2:
                        for w, name in ((glu_w1, "glu_w1"), (glu_w3, "glu_w3")):
                            act.dma_start(w[:, 0:EXPERTS, :], ins[name].rearrange("e p n -> p e n")).then_inc(w_up[l], 16)
                            act.dma_start(w[:, EXPERTS, :], ins["s" + name]).then_inc(w_up[l], 16)
                        act.dma_start(glu_w2[:, 0:EXPERTS, :], ins["glu_w2"].rearrange("e p n -> p e n")).then_inc(w_down[l], 16)
                        act.dma_start(glu_w2[:, EXPERTS, :], ins["sglu_w2"]).then_inc(w_down[l], 16)
                        continue
                    act.dma_start(up_w[l][:, :, :], ins[f"up_w{l}"].rearrange("e p n -> p e n")).then_inc(w_up[l], 16)
                    act.dma_start(down_w[l][:, :, :, :], ins[f"down_w{l}"].rearrange("e (c p) n -> p e c n", p=P))\
                       .then_inc(w_down[l], 16)
                act.wait_ge(w_small, SMALL)
                act.activation(tanh_g[:, :], gates[:, :], ACT.Tanh).then_inc(tanh_made, 1)

            @block.gpsimd
            def _(pool):
                for l in (1, 3):
                    pool.memset(out_bias[l][:, :], 0.0).then_inc(zeroed, 1)
                pool.memset(ident[:, :], 1.0).then_inc(ident_made, 1)
                pool.wait_ge(ident_made, 1)
                pool.affine_select(out=ident[:, :], in_=ident[:, :], compare_op=ALU.is_equal, fill=0.0, base=0,
                                   pattern=[[-1, P]], channel_multiplier=1).then_inc(ident_made, 1)
                pool.iota(iota_i, [[P, TT], [-1, S]], base=0, channel_multiplier=1).then_inc(iota_made, 1)
                pool.wait_ge(ident_made, 2)
                pool.tensor_copy(ident_r[:, :], ident[:, :]).then_inc(ident_made, 1)
                pool.tensor_copy(ident_b[:, :], ident[:, :]).then_inc(ident_made, 1)
                pool.memset(minus_half[:, :], -0.5).then_inc(const_made, 1)
                for e in range(EXPERTS):
                    pool.memset(iota8[:, e:e + 1], float(e)).then_inc(const_made, 1)
                pool.memset(gate_pad[:, :, :], 0.0).then_inc(const_made, 1)
                pool.wait_ge(w_attn, 64)
                pool.wait_ge(w_small, SMALL)
                pool.tensor_scalar(wq[:, :, :], wq[:, :, :], DK ** -0.5, None, ALU.mult).then_inc(const_made, 1)
                for n in ("bq0", "bq3"):
                    pool.tensor_scalar(col_bias[n][:, :], col_bias[n][:, :], DK ** -0.5, None, ALU.mult)\
                        .then_inc(const_made, 1)
                pool.wait_ge(tanh_made, 1)
                for l in (0, 2, 3):
                    pool.tensor_scalar(bo[l][:, :], bo[l][:, :], tanh_g[:, l:l + 1], None, ALU.mult)\
                        .then_inc(const_made, 1)

            @block.vector
            def _(dve):
                for t in (spread_two["q"], spread_two["k"], spread_one["q"], spread_one["k"]):
                    dve.memset(t[:, :, :].bitcast(F32), 0.0).then_inc(v_set, 1)
                dve.memset(max_parts[:, :, :, :].bitcast(F32), 0.0).then_inc(v_set, 1)
                dve.memset(v_cols[:, :, :, :], 0.0).then_inc(v_set, 1)
                dve.wait_ge(v_set, 6)
                dve.memset(v_view(P // 2)[:, 0, :, :, :], 1.0).then_inc(v_set, 1)
                dve.memset(v_view(P // 2)[:, 1, :, :, :], 1.0).then_inc(v_set, 1)
                dve.wait_ge(ident_made, 3)
                for g in range(GROUPS):
                    src = ident[:, g * 32:(g + 1) * 32].rearrange("p (h d) -> p h d", d=DK)
                    for t, copies in ((spread_two["q"], (0, 1)), (spread_one["q"], (2,)),
                                      (spread_two["k"], (0, 2)), (spread_one["k"], (1,))):
                        for c in copies:
                            dst = t[:, g, :].rearrange("p (h r) -> p h r", r=32)[:, :, c * DK:(c + 1) * DK]
                            dve.tensor_copy(dst, src).then_inc(spread_made, 1)
                rows = ident[:, :].rearrange("p (h r) -> p h r", r=32)[:, :, 3 * DK:3 * DK + 2]
                dve.tensor_reduce(ones_rows[:, :], rows, mybir.AxisListType.XY, ALU.add).then_inc(spread_made, 1)
                dve.wait_ge(iota_made, 1)
                dve.tensor_copy(dist, iota_i).then_inc(dist_made, 1)
                dve.wait_ge(dist_made, 1)
                dve.tensor_scalar(dist_neg, dist, -1.0, None, ALU.mult).then_inc(dist_made, 1)
                dve.wait_ge(dist_made, 2)
                dve.tensor_tensor(dist, dist, dist_neg, ALU.max).then_inc(dist_made, 1)
                dve.wait_ge(dist_made, 3)
                for t in range(TT):
                    lo, n = window(2, t)
                    dve.tensor_scalar(band[:, t, :], dist[:, t, lo:lo + n], float(WINDOW), -BIG, ALU.is_gt, ALU.mult)\
                       .then_inc(decay_made, 1)
                dve.wait_ge(w_small, SMALL)
                dve.tensor_scalar(dist_neg, dist, time_decay[:, 0:1], -1.0, ALU.mult, ALU.mult)\
                   .then_inc(dist_made, 1)
                dve.wait_ge(dist_made, 4)
                dve.tensor_copy(decay_hi[:, :, :], dist_neg).then_inc(dist_made, 1)
                dve.wait_ge(dist_made, 5)
                dve.tensor_tensor(decay_lo[:, :, :], dist_neg, decay_hi[:, :, :].bitcast(F32), ALU.subtract)\
                   .then_inc(decay_made, 1)

        with nc.Fori(0, PAIRS) as pair:
            with nc.Block(no_gpsimd_drain=True) as block:
                @block.sync
                def _(sp):
                    row = pair * LANES
                    n_mask = 0
                    for b in range(LANES):
                        sp.dma_start(ctx_t[b][:, :], ins["ctx_t"][bass.ds(row + b, 1)].rearrange("b p n -> (b p) n"))\
                          .then_inc(ctx_loaded[b], 16)
                        sp.dma_start(x[b][:, :, :], ins["x"][bass.ds(row + b, 1)].rearrange("b (t p) n -> p (b t) n", p=P))\
                          .then_inc(x_loaded[b], 16)
                        for m in range(2):
                            for o in range(2):
                                src = ins[f"mask{m}{o}"][bass.ds(row + b, 1)]
                                if n_mask >= 2:
                                    sp.wait_ge(mask_made, n_mask - 1)
                                sp.dma_start(mask_in[n_mask % 2], src.rearrange("b (t p) n -> p (b t) n", p=P))\
                                  .then_inc(mask_loaded[n_mask % 2], 16)
                                n_mask += 1
                    for b in range(LANES):
                        sp.wait_ge(x_new[b], PHASES)
                        sp.dma_start(out[bass.ds(row + b, 1)].rearrange("b (t p) n -> p (b t) n", p=P), x[b][:, :, :])\
                          .then_inc(stored, 16)
                    sp.wait_ge(stored, 16 * LANES)

                @block.gpsimd
                def _(pool):
                    def make_masks(b):
                        for m in range(2):
                            for o in range(2):
                                i = (b * 2 + m) * 2 + o
                                pool.wait_ge(mask_loaded[i % 2], 16 * (i // 2 + 1))
                                pool.tensor_scalar(mask[b][m][o][:, :, :], mask_in[i % 2], 0.0, -BIG,
                                                   ALU.is_equal, ALU.mult).then_inc(mask_made, 1)

                    def rstd(ln, n):
                        pool.wait_ge(ln.aggr_done, TT * (n + 1))
                        pool.tensor_scalar(ln.var_eps[:, :], ln.mean_var[:, :, 1], EPS, None, ALU.add)\
                            .then_inc(ln.eps_added, 1)
                        pool.wait_ge(ln.eps_added, n + 1)
                        pool.tensor_tensor(ln.rstd[:, :], ln.var_eps[:, :], minus_half[:, :], ALU.pow)\
                            .then_inc(ln.rstd_done, 1)

                    def residual_with_bias(n):
                        layer, b = n // LANES, n % LANES
                        if layer == 1:
                            return
                        pool.wait_ge(an.turned, n + 1)
                        if layer == 0:
                            pool.wait_ge(x_loaded[b], 16)
                        else:
                            pool.wait_ge(x_new[b], 2 * layer)
                        for t in range(TT):
                            last = pool.tensor_tensor(x_res[:, t, :], x[b][:, t, :], bo[layer][:, :], ALU.add)
                        last.then_inc(res_ready, 1)

                    def gelu_square(n, e):
                        for u in range(2):
                            c = 2 * (EXPERTS * (n - LANES) + e) + u + 1
                            pool.wait_ge(pre_ready, c)
                            if c > 2:
                                pool.wait_ge(hid_ready, 2 * (experts_before(n) + e - 1) + u + 1)
                            pool.tensor_tensor(gelu_t[:, u, :, :], pre_act[:, u, :, :], pre_act[:, u, :, :], ALU.mult)\
                                .then_inc(sq_ready, 1)

                    for slot in range(PHASES + 1):
                        a, f = slot if slot < PHASES else None, slot - 1 if slot else None
                        if slot == 0:
                            rstd(an, 0)
                            make_masks(0)
                            make_masks(1)
                        else:
                            rstd(fn, f)
                            if a is not None:
                                rstd(an, a)
                        if a is not None:
                            residual_with_bias(a)
                        if f is not None and f // LANES == 1:
                            for e in range(EXPERTS):
                                gelu_square(f, e)

                @block.tensor
                def _(pe):
                    def mm(o, lhs, rhs, **kw):
                        return nc.tensor.matmul(o, lhs, rhs, **kw)

                    def kv_project(n):
                        layer, b = n // LANES, n % LANES
                        pe.wait_ge(w_attn, 64)
                        pe.wait_ge(ctx_loaded[b], 16)
                        if n:
                            pe.wait_ge(qm_ready, GROUPS * n)
                            pe.wait_ge(exp_done, STEPS * n)
                        mm(smax[:, 1, 0:S], wk[:, layer, :], ctx_t[b][:, :], start=True, stop=True).then_inc(k_proj, 1)
                        for t in range(TT):
                            last = mm(sexp[:, 0, t * D:(t + 1) * D], ctx_t[b][:, t * P:(t + 1) * P], wv[:, layer, :],
                                      start=True, stop=True)
                        last.then_inc(v_proj, 1)

                    def turn(ln, n, bank):
                        pe.wait_ge(ident_made, 2)
                        pe.wait_ge(ln.normed_done, TT * (n + 1))
                        for t in range(TT):
                            last = nc.tensor.transpose(bank[:, t * P:(t + 1) * P], ln.normed[:, t, :], ident[:, :])
                        last.then_inc(ln.turned, 1)

                    def q_project(n):
                        pe.wait_ge(an.turned_sb, n + 1)
                        mm(cbank[:, S:2 * S], wq[:, n // LANES, :], an.normed_t[:, :], start=True, stop=True)\
                            .then_inc(q_proj, 1)

                    def spread(n, which, bank, parts_done, done):
                        pe.wait_ge(parts_done, n + 1)
                        flat = bank[:, :, :].rearrange("p a n -> p (a n)")
                        for g in range(GROUPS):
                            o = flat[:, g * S:(g + 1) * S]
                            mm(o, spread_two[which][:, g, :], qkv_hi[which], start=True, stop=False)
                            last = mm(o, spread_one[which][:, g, :], qkv_lo[which], start=False, stop=True)
                        last.then_inc(done, 1)

                    def strip(h):
                        return slice(32 * (h % GH), 32 * (h % GH) + 32)

                    def max_scores(n, s):
                        layer, b = n // LANES, n % LANES
                        if s == 0:
                            pe.wait_ge(k_ready, n + 1)
                            pe.wait_ge(q_ready, n + 1)
                            pe.wait_ge(mask_made, 4 * (b + 1))
                        else:
                            pe.wait_ge(max_red, STEPS * n + s)
                            if s % 2 == 0:
                                pe.wait_ge(qm_ready, GROUPS * n + s // 2)
                        for j in range(2):
                            h = 2 * s + j
                            score_bias(mm, smax[:, j, :], b, layer, 0)
                            for t in range(TT):
                                lo, w = window(layer, t)
                                last = mm(smax[:, j, t * S:t * S + w], q_stack[strip(h), h // GH, t * P:(t + 1) * P],
                                          k_stack[strip(h), h // GH, lo:lo + w], start=False, stop=(t == TT - 1),
                                          skip_group_check=True)
                        last.then_inc(max_psum, 1)

                    def turn_max(n, g):
                        pe.wait_ge(max_lo, GROUPS * n + g + 1)
                        for t in range(TT):
                            last = mm(smax[:, 0, t * P:(t + 1) * P], max_parts[:, t, :, :].rearrange("p h r -> p (h r)"),
                                      ident_r[:, :], start=True, stop=True)
                        last.then_inc(max_turned, 1)

                    def exp_scores(n, s):
                        layer, b = n // LANES, n % LANES
                        pe.wait_ge(qm_ready, GROUPS * n + s // 2 + 1)
                        if s:
                            pe.wait_ge(exp_done, STEPS * n + s)
                        for j in range(2):
                            h = 2 * s + j
                            score_bias(mm, sexp[:, j, :], b, layer, 1)
                            for t in range(TT):
                                lo, w = window(layer, t)
                                last = mm(sexp[:, j, t * S:t * S + w], k_stack[strip(h), h // GH, t * P:(t + 1) * P],
                                          qm_stack[strip(h), h // GH % 2, lo:lo + w], start=False, stop=(t == TT - 1),
                                          skip_group_check=True)
                        last.then_inc(exp_psum, 1)

                    def times_v(n, s):
                        layer = n // LANES
                        pe.wait_ge(exp_done, STEPS * n + s + 1)
                        pe.wait_ge(v_ready, TT * (n + 1))
                        for j in range(2):
                            h = 2 * s + j
                            u, hj = h // (HEADS // 2), h % (HEADS // 2)
                            for t in range(TT):
                                lo, w = window(layer, t)
                                last = mm(cbank[:, u * S + lo:u * S + lo + w], v_cols[:, t, u, hj * P:(hj + 1) * P],
                                          probs[:, s % 2, j, t, 0:w], start=(hj == 0 and t == 0),
                                          stop=(hj == HEADS // 2 - 1 and t == TT - 1), skip_group_check=True)
                        last.then_inc(pv_done, 1)

                    def out_project(n):
                        pe.wait_ge(heads_ready, 2 * (n + 1))
                        for t in range(TT):
                            last = mm(cbank[:, t * D:(t + 1) * D], heads_t[:, t * P:(t + 1) * P], wo[:, n // LANES, :],
                                      start=True, stop=True)
                        last.then_inc(attn_out, 1)

                    def logits(n):
                        pe.wait_ge(fn.turned_sb, n + 1)
                        pe.wait_ge(w_small, SMALL)
                        for t in range(TT):
                            last = mm(ybank[:, S + t * EXPERTS:S + (t + 1) * EXPERTS], fn.normed_t[:, t * P:(t + 1) * P],
                                      router[:, n // LANES, :], start=True, stop=True)
                        last.then_inc(logits_psum, 1)

                    def up(n, e):
                        layer, done = n // LANES, experts_before(n) + e
                        pe.wait_ge(w_up[layer], 64 if layer == 2 else 16)
                        for u in range(2):
                            if done:
                                if layer == 1 and e:
                                    pe.wait_ge(pre_ready, 2 * (EXPERTS * (n - LANES) + e - 1) + u + 1)
                                else:
                                    pe.wait_ge(hid_ready, 2 * done if layer == 2 or e == 0 else 2 * (done - 1) + u + 1)
                            if e == 0 and n and (n - 1) // LANES in (1, 3):
                                pe.wait_ge(gate_t_ready, (n - 1) - LANES + 1 if n <= 2 * LANES else LANES + n - 3 * LANES)
                            if layer == 2:
                                last = mm(hbank[:, u, 0:S], (glu_w1, glu_w3)[u][:, e, :], fn.normed_t[:, :],
                                          start=True, stop=True)
                            else:
                                for c in range(2):
                                    cc = 2 * u + c
                                    last = mm(hbank[:, u, c * S:(c + 1) * S], up_w[layer][:, e, cc * P:(cc + 1) * P],
                                              fn.normed_t[:, :], start=True, stop=True)
                            last.then_inc(up_psum, 1)

                    def down(n, e):
                        layer, done = n // LANES, experts_before(n) + e
                        pe.wait_ge(w_down[layer], 32 if layer == 2 else 16)
                        pe.wait_ge(hid_ready, 2 * (done + 1))
                        if e == 0:
                            pe.wait_ge(gate_step, n + 1)
                        else:
                            pe.wait_ge(y_acc, done)
                        for t in range(TT):
                            o = ybank[:, t * D:(t + 1) * D]
                            if layer == 2:
                                last = mm(o, hidden[:, done % 2, 0, t * P:(t + 1) * P], glu_w2[:, e, :], start=True, stop=True)
                            else:
                                for c in range(CH):
                                    last = mm(o, hidden[:, done % 2, c, t * P:(t + 1) * P], down_w[layer][:, e, c, :],
                                              start=(c == 0), stop=(c == CH - 1))
                        last.then_inc(y_psum, 1)

                    def biased(n):
                        return sum(m // LANES in (1, 3) for m in range(n))

                    def output_bias(n):
                        layer = n // LANES
                        pe.wait_ge(gate_ready, n + 1)
                        pe.wait_ge(hid_ready, 2 * experts_before(n + 1))
                        for t in range(TT):
                            last = nc.tensor.transpose(hbank[:, 0, t * P:(t + 1) * P], gate_pad[:, t, :], ident[:, :])
                        last.then_inc(gate_turned, 1)
                        pe.wait_ge(gate_t_ready, biased(n) + 1)
                        pe.wait_ge(y_acc, experts_before(n + 1))
                        for t in range(TT):
                            last = mm(ybank[:, t * D:(t + 1) * D], gate_t[:, t * P:(t + 1) * P], out_bias[layer][:, :],
                                      start=True, stop=True)
                        last.then_inc(bias_psum, 1)

                    for slot in range(PHASES + 1):
                        a, f = slot if slot < PHASES else None, slot - 1 if slot else None
                        if a is not None:
                            kv_project(a)
                        if f is not None:
                            if f:
                                pe.wait_ge(x_new[(f - 1) % LANES], 2 * ((f - 1) // LANES) + 2)
                            turn(fn, f, ybank)
                        if a is not None:
                            if a:
                                pe.wait_ge(x_new[(a - 1) % LANES], 2 * ((a - 1) // LANES) + 1)
                            turn(an, a, cbank)
                        if f is not None:
                            logits(f)
                            up(f, 0)
                        if a is not None:
                            q_project(a)
                            spread(a, "k", smax, k_lo, k_spread)
                            pe.wait_ge(v_ready, TT * (a + 1))
                            spread(a, "q", sexp, q_lo, q_spread)
                        for s in range(STEPS + 3):
                            if a is not None and s < STEPS:
                                max_scores(a, s)
                            if f is not None and s + 1 < experts(f // LANES):
                                up(f, s + 1)
                            if a is not None and s < STEPS and s % 2:
                                turn_max(a, s // 2)
                            if a is not None and 2 <= s < STEPS + 2:
                                exp_scores(a, s - 2)
                            if f is not None and s < experts(f // LANES):
                                down(f, s)
                            if f is not None and s == EXPERTS and f // LANES in (1, 3):
                                output_bias(f)
                            if a is not None and s >= 3:
                                times_v(a, s - 3)
                        if a is not None:
                            out_project(a)

                @block.scalar
                def _(act):
                    def high_part(n, which, proj, done, src):
                        layer = n // LANES
                        act.wait_ge(proj, n + 1)
                        if layer in (0, 3):
                            i = act.activation(qkv_hi[which], src, ACT.Identity, bias=col_bias[f"b{which}{layer}"][:, :])
                        else:
                            i = act.activation(qkv_hi[which], src, ACT.Copy)
                        i.then_inc(done, 1)

                    def copy_turned(ln, n, bank):
                        act.wait_ge(ln.turned, n + 1)
                        act.activation(ln.normed_t[:, :], bank[:, 0:S], ACT.Copy).then_inc(ln.turned_sb, 1)

                    def copy_q_stack(n):
                        act.wait_ge(q_spread, n + 1)
                        act.wait_ge(k_spread, n + 1)
                        act.activation(q_stack[:, :, :].rearrange("p g n -> p (g n)"),
                                       sexp[:, :, :].rearrange("p a n -> p (a n)"), ACT.Copy).then_inc(q_ready, 1)

                    def exp_logits(n):
                        act.wait_ge(gate_step, n + 1)
                        act.wait_ge(gate_shifted, n + 1)
                        act.activation(exp_l[:, :, :], shifted[:, :, :], ACT.Exp).then_inc(exp_l_done, 1)

                    def exponentials(n, s):
                        layer = n // LANES
                        act.wait_ge(exp_psum, STEPS * n + s + 1)
                        if STEPS * n + s >= 2:
                            act.wait_ge(pv_done, STEPS * n + s - 1)
                        w = window(layer, 0)[1]
                        act.activation(probs[:, s % 2, :, :, 0:w].rearrange("p j t n -> p (j t) n"),
                                       sexp[:, :, :].rearrange("p j (t n) -> p (j t) n", n=S)[:, :, 0:w],
                                       ACT.Exp).then_inc(exp_done, 1)

                    def hidden_units(n, e):
                        layer, done = n // LANES, experts_before(n) + e
                        for u in range(2):
                            act.wait_ge(up_psum, 2 * done + u + 1)
                            if layer == 0:
                                if done >= 2:
                                    act.wait_ge(y_psum, done - 1)
                                act.activation(hidden[:, done % 2, 2 * u:2 * u + 2, :].rearrange("p c n -> p (c n)"),
                                               hbank[:, u, :], ACT.Relu).then_inc(hid_ready, 1)
                            elif layer == 3:
                                act.wait_ge(y_psum, done - 1)
                                for c in range(2):
                                    last = act.activation(hidden[:, done % 2, 2 * u + c, :], hbank[:, u, c * S:(c + 1) * S],
                                                          ACT.Relu, bias=hid_bias[3][:, e, 2 * u + c:2 * u + c + 1])
                                last.then_inc(hid_ready, 1)
                            elif layer == 1:
                                if e or n > LANES:
                                    act.wait_ge(hid_ready, 2 * (done - 1) + u + 1)
                                for c in range(2):
                                    last = act.activation(pre_act[:, u, c, :], hbank[:, u, c * S:(c + 1) * S],
                                                          ACT.Identity, bias=hid_bias[1][:, e, 2 * u + c:2 * u + c + 1])
                                last.then_inc(pre_ready, 1)
                            elif u == 0:
                                if done > experts_before(2 * LANES):
                                    act.wait_ge(hid_ready, 2 * done)
                                act.activation(pre_act[:, 0, 0, :], hbank[:, 0, 0:S], ACT.Tanh, scale=0.5)\
                                   .then_inc(glu_tanh, 1)

                    def gelu_tanh(n, e):
                        for u in range(2):
                            act.wait_ge(inner_ready, 2 * (EXPERTS * (n - LANES) + e) + u + 1)
                            act.activation(gelu_t[:, u, :, :], gelu_t[:, u, :, :], ACT.Tanh, scale=GELU_C * GELU_A)\
                               .then_inc(tanh_ready, 1)

                    def copy_gates(n):
                        act.wait_ge(gate_turned, sum(m // LANES in (1, 3) for m in range(n)) + 1)
                        act.activation(gate_t, hbank[:, 0, 0:S], ACT.Copy).then_inc(gate_t_ready, 1)

                    for slot in range(PHASES + 1):
                        a, f = slot if slot < PHASES else None, slot - 1 if slot else None
                        if a is not None:
                            high_part(a, "k", k_proj, k_hi, smax[:, 1, 0:S])
                        if f is not None:
                            copy_turned(fn, f, ybank)
                        if a is not None:
                            copy_turned(an, a, cbank)
                        if f is not None:
                            hidden_units(f, 0)
                        if a is not None:
                            high_part(a, "q", q_proj, q_hi, cbank[:, S:2 * S])
                            copy_q_stack(a)
                        if f is not None:
                            if f // LANES == 1:
                                gelu_tanh(f, 0)
                            exp_logits(f)
                        for s in range(STEPS + 3):
                            more = f is not None and s + 1 < experts(f // LANES)
                            if more:
                                hidden_units(f, s + 1)
                            if a is not None and 2 <= s < STEPS + 2:
                                exponentials(a, s - 2)
                            if more and f // LANES == 1:
                                gelu_tanh(f, s + 1)
                            if f is not None and s == EXPERTS and f // LANES in (1, 3):
                                copy_gates(f)

                @block.vector
                def _(dve):
                    def statistics(ln, n, b, layer, kind):
                        if layer == 0 and kind == 0:
                            dve.wait_ge(x_loaded[b], 16)
                        else:
                            dve.wait_ge(x_new[b], 2 * layer + kind)
                        for t in range(TT):
                            dve.bn_stats(ln.stats[:, t, :], x[b][:, t, :]).then_inc(ln.stats_done, 1)
                        dve.wait_ge(ln.stats_done, TT * (n + 1))
                        for t in range(TT):
                            dve.bn_aggr(ln.mean_var[:, t, :], ln.stats[:, t, :]).then_inc(ln.aggr_done, 1)

                    def normalise(ln, n, b):
                        dve.wait_ge(ln.rstd_done, n + 1)
                        for t in range(TT):
                            dve.tensor_scalar(ln.normed[:, t, :], x[b][:, t, :], ln.mean_var[:, t, 0:1], ln.rstd[:, t:t + 1],
                                              ALU.subtract, ALU.mult).then_inc(ln.normed_done, 1)

                    def low_part(n, which, hi_done, done, src):
                        layer = n // LANES
                        dve.wait_ge(hi_done, n + 1)
                        bias = col_bias[f"b{which}{layer}"][:, :] if layer in (0, 3) else 0.0
                        dve.scalar_tensor_tensor(out=qkv_lo[which], in0=src, scalar=bias,
                                                 in1=qkv_hi[which].bitcast(F32), op0=ALU.add, op1=ALU.subtract)\
                           .then_inc(done, 1)

                    def place_v(n):
                        layer = n // LANES
                        dve.wait_ge(v_proj, n + 1)
                        for t in range(TT):
                            src = sexp[:, 0, t * D:(t + 1) * D].rearrange("p (u j d) -> p u j d", u=2, d=DK)
                            dst = v_view(0)[:, t, :, :, :]
                            if layer in (0, 3):
                                bias = bv[layer][:, :].rearrange("p (u j d) -> p u j d", u=2, d=DK)
                                i = dve.tensor_tensor(dst, src, bias, ALU.add)
                            else:
                                i = dve.tensor_copy(dst, src)
                            i.then_inc(v_ready, 1)

                    def copy_k_stack(n):
                        dve.wait_ge(k_spread, n + 1)
                        dve.tensor_scalar(k_stack[:, :, :].rearrange("p g n -> p (g n)"),
                                          smax[:, :, :].rearrange("p a n -> p (a n)"), ones_rows[:, 0:1], None,
                                          ALU.add).then_inc(k_ready, 1)

                    def reduce_max(n, s):
                        w = window(n // LANES, 0)[1]
                        dve.wait_ge(max_psum, STEPS * n + s + 1)
                        dve.tensor_reduce(row_max[:, 2 * s:2 * s + 2, :].rearrange("p h t -> p (h t)"),
                                          smax[:, :, :].rearrange("p j (t n) -> p (j t) n", n=S)[:, :, 0:w],
                                          AX, ALU.max).then_inc(max_red, 1)

                    def split_max(n, g):
                        dve.wait_ge(max_red, STEPS * n + 2 * g + 2)
                        if GROUPS * n + g:
                            dve.wait_ge(max_turned, GROUPS * n + g)
                        src = row_max[:, GH * g:GH * g + GH, :].rearrange("p h t -> p t h")
                        hi, lo = max_parts[:, :, :, 3 * DK], max_parts[:, :, :, 3 * DK + 1]
                        dve.tensor_scalar(hi, src, -1.0, None, ALU.mult).then_inc(max_hi, 1)
                        dve.wait_ge(max_hi, GROUPS * n + g + 1)
                        dve.scalar_tensor_tensor(out=lo, in0=src, scalar=-1.0, in1=hi.bitcast(F32),
                                                 op0=ALU.mult, op1=ALU.subtract).then_inc(max_lo, 1)

                    def add_max(n, g):
                        dve.wait_ge(max_turned, GROUPS * n + g + 1)
                        if GROUPS * n + g >= 2:
                            dve.wait_ge(exp_psum, STEPS * n + 2 * g - 2)
                        dve.tensor_tensor(qm_stack[:, g % 2, :], smax[:, 0, 0:S], q_stack[:, g, :].bitcast(F32), ALU.add)\
                           .then_inc(qm_ready, 1)

                    def heads_out(n):
                        dve.wait_ge(pv_done, STEPS * (n + 1))
                        dve.reciprocal(inv_sum, cbank[P // 2:P, :]).then_inc(inv_done, 1)
                        dve.wait_ge(inv_done, n + 1)
                        for u in range(2):
                            dve.tensor_tensor(heads_t[u * P // 2:(u + 1) * P // 2, :], cbank[0:P // 2, u * S:(u + 1) * S],
                                              inv_sum[:, u * S:(u + 1) * S], ALU.mult).then_inc(heads_ready, 1)

                    def attention_sum(n):
                        layer, b = n // LANES, n % LANES
                        dve.wait_ge(attn_out, n + 1)
                        src = x[b]
                        if layer != 1:
                            dve.wait_ge(res_ready, n + 1 if n < LANES else n + 1 - LANES)
                            src = x_res
                        dve.scalar_tensor_tensor(out=x[b][:, :, :].rearrange("p t n -> p (t n)"), in0=cbank[:, 0:S],
                                                 scalar=tanh_g[:, layer:layer + 1],
                                                 in1=src[:, :, :].rearrange("p t n -> p (t n)"),
                                                 op0=ALU.mult, op1=ALU.add).then_inc(x_new[b], 1)

                    def bc(ap):
                        return ap.unsqueeze(2).broadcast_to([P, TT, EXPERTS])

                    def read_logits(n):
                        layer = n // LANES
                        dve.wait_ge(logits_psum, n + 1)
                        src = ybank[:, S:S + TT * EXPERTS].rearrange("p (t e) -> p t e", t=TT)
                        if layer == 3:
                            b3 = route_bias[3][:, :].unsqueeze(1).broadcast_to([P, TT, EXPERTS])
                            i = dve.tensor_tensor(logit[:, :, :], src, b3, ALU.add)
                        else:
                            i = dve.tensor_copy(logit[:, :, :], src)
                        i.then_inc(gate_step, 1)
                        dve.wait_ge(gate_step, n + 1)
                        dve.tensor_reduce(logit_max[:, :], logit[:, :, :], AX, ALU.max).then_inc(gate_max, 1)
                        dve.wait_ge(gate_max, n + 1)
                        dve.tensor_tensor(shifted[:, :, :], logit[:, :, :], bc(logit_max[:, :]), ALU.subtract)\
                           .then_inc(gate_shifted, 1)

                    def make_gates(n):
                        layer = n // LANES
                        steps = [sum(GATE_LINKS[m // LANES] for m in range(n))]

                        def done(i):
                            i.then_inc(gate_chain, 1)
                            steps[0] += 1
                            dve.wait_ge(gate_chain, steps[0])

                        dve.wait_ge(exp_l_done, n + 1)
                        done(dve.tensor_reduce(exp_sum[:, :], exp_l[:, :, :], AX, ALU.add))
                        done(dve.reciprocal(exp_inv[:, :], exp_sum[:, :]))
                        done(dve.tensor_tensor(prob[:, :, :], exp_l[:, :, :], bc(exp_inv[:, :]), ALU.mult))
                        if layer == 2:
                            b2 = route_bias[2][:, :].unsqueeze(1).broadcast_to([P, TT, EXPERTS])
                            done(dve.tensor_tensor(choice[:, :, :], prob[:, :, :], b2, ALU.add))
                        key = choice if layer == 2 else prob
                        dve.max(top8[:, 0, :], key[:, 0, :])
                        done(dve.max(top8[:, 1, :], key[:, 1, :]))
                        dve.max_index(top_idx[:, 0, :], top8[:, 0, :], key[:, 0, :])
                        done(dve.max_index(top_idx[:, 1, :], top8[:, 1, :], key[:, 1, :]))
                        done(dve.tensor_copy(top_f[:, :, :], top_idx[:, :, :]))
                        i8 = iota8[:, :].unsqueeze(1).broadcast_to([P, TT, EXPERTS])
                        if layer == 3:
                            done(dve.tensor_tensor(picked[:, :, :], i8, bc(top_f[:, :, 0]), ALU.is_equal))
                        else:
                            dve.tensor_tensor(pick1[:, :, :], i8, bc(top_f[:, :, 0]), ALU.is_equal)
                            done(dve.tensor_tensor(pick2[:, :, :], i8, bc(top_f[:, :, 1]), ALU.is_equal))
                            done(dve.tensor_tensor(picked[:, :, :], pick1[:, :, :], pick2[:, :, :], ALU.add))
                        gate = gate_pad[:, :, 0:EXPERTS]
                        if layer >= 2:
                            done(dve.tensor_tensor(gate, picked[:, :, :], prob[:, :, :], ALU.mult))
                        else:
                            done(dve.tensor_tensor(gate_raw[:, :, :], picked[:, :, :], prob[:, :, :], ALU.mult))
                            done(dve.tensor_reduce(gate_sum[:, :], gate_raw[:, :, :], AX, ALU.add))
                            done(dve.reciprocal(gate_inv[:, :], gate_sum[:, :]))
                            done(dve.tensor_tensor(gate, gate_raw[:, :, :], bc(gate_inv[:, :]), ALU.mult))
                        dve.tensor_scalar(gate_use[:, :, :], gate, 0.5 if layer in (1, 2) else 1.0, None, ALU.mult)\
                           .then_inc(gate_ready, 1)
                        assert steps[0] == sum(GATE_LINKS[m // LANES] for m in range(n + 1))

                    def gelu_inner(n, e):
                        for u in range(2):
                            dve.wait_ge(sq_ready, 2 * (EXPERTS * (n - LANES) + e) + u + 1)
                            dve.scalar_tensor_tensor(out=gelu_t[:, u, :, :], in0=gelu_t[:, u, :, :], scalar=1.0 / GELU_A,
                                                     in1=pre_act[:, u, :, :], op0=ALU.add, op1=ALU.mult)\
                               .then_inc(inner_ready, 1)

                    def gelu_out(n, e):
                        done = experts_before(n) + e
                        for u in range(2):
                            dve.wait_ge(tanh_ready, 2 * (EXPERTS * (n - LANES) + e) + u + 1)
                            dve.wait_ge(y_psum, done - 1)
                            dve.scalar_tensor_tensor(out=hidden[:, done % 2, 2 * u:2 * u + 2, :], in0=gelu_t[:, u, :, :],
                                                     scalar=1.0, in1=pre_act[:, u, :, :], op0=ALU.add, op1=ALU.mult)\
                               .then_inc(hid_ready, 1)

                    def glu_hidden(n, e):
                        done = experts_before(n) + e
                        dve.wait_ge(glu_tanh, done - experts_before(2 * LANES) + 1)
                        dve.scalar_tensor_tensor(out=gelu_t[:, 0, 0, :], in0=pre_act[:, 0, 0, :], scalar=1.0,
                                                 in1=hbank[:, 0, 0:S], op0=ALU.add, op1=ALU.mult).then_inc(hid_ready, 1)
                        dve.wait_ge(hid_ready, 2 * done + 1)
                        dve.wait_ge(up_psum, 2 * done + 2)
                        dve.wait_ge(y_psum, done - 1)
                        dve.tensor_tensor(hidden[:, done % 2, 0, :], hbank[:, 1, 0:S], gelu_t[:, 0, 0, :], ALU.mult)\
                           .then_inc(hid_ready, 1)

                    def add_expert(n, e):
                        layer, done = n // LANES, experts_before(n) + e
                        dve.wait_ge(y_psum, done + 1)
                        if e == 0:
                            dve.wait_ge(gate_ready, n + 1)
                        else:
                            dve.wait_ge(y_acc, done)
                        for t in range(TT):
                            o, y = acc[:, t, :], ybank[:, t * D:(t + 1) * D]
                            g = 0.5 if e == EXPERTS else gate_use[:, t, e:e + 1]
                            if e == 0:
                                last = dve.tensor_scalar(o, y, g, None, ALU.mult)
                            else:
                                last = dve.scalar_tensor_tensor(out=o, in0=y, scalar=g, in1=o, op0=ALU.mult, op1=ALU.add)
                        last.then_inc(y_acc, 1)

                    def add_output_bias(n):
                        k = sum(m // LANES in (1, 3) for m in range(n)) + 1
                        dve.wait_ge(bias_psum, k)
                        dve.wait_ge(y_acc, experts_before(n + 1))
                        dve.tensor_tensor(acc[:, :, :].rearrange("p t n -> p (t n)"), ybank[:, 0:S],
                                          acc[:, :, :].rearrange("p t n -> p (t n)"), ALU.add).then_inc(bias_added, 1)
                        dve.wait_ge(bias_added, k)

                    def expert_sum(n):
                        layer, b = n // LANES, n % LANES
                        dve.wait_ge(y_acc, experts_before(n + 1))
                        dve.scalar_tensor_tensor(out=x[b][:, :, :], in0=acc[:, :, :],
                                                 scalar=tanh_g[:, LAYERS + layer:LAYERS + layer + 1], in1=x[b][:, :, :],
                                                 op0=ALU.mult, op1=ALU.add).then_inc(x_new[b], 1)

                    for slot in range(PHASES + 1):
                        a, f = slot if slot < PHASES else None, slot - 1 if slot else None
                        fl = f // LANES if f is not None else None
                        if f is not None:
                            statistics(fn, f, f % LANES, fl, 1)
                        if a is not None:
                            statistics(an, a, a % LANES, a // LANES, 0)
                            low_part(a, "k", k_hi, k_lo, smax[:, 1, 0:S])
                            place_v(a)
                        if f is not None:
                            normalise(fn, f, f % LANES)
                        if a is not None:
                            normalise(an, a, a % LANES)
                        if f is not None:
                            read_logits(f)
                        if a is not None:
                            low_part(a, "q", q_hi, q_lo, cbank[:, S:2 * S])
                            copy_k_stack(a)
                        if f is not None:
                            if fl == 1:
                                gelu_inner(f, 0)
                                gelu_out(f, 0)
                            if fl == 2:
                                glu_hidden(f, 0)
                            make_gates(f)
                        for s in range(STEPS + 3):
                            more = f is not None and s + 1 < experts(fl)
                            if a is not None and s < STEPS:
                                reduce_max(a, s)
                                if s % 2:
                                    split_max(a, s // 2)
                            if more and fl == 1:
                                gelu_inner(f, s + 1)
                            if a is not None and s < STEPS and s % 2:
                                add_max(a, s // 2)
                            if more and fl == 2:
                                glu_hidden(f, s + 1)
                            if f is not None and s < experts(fl):
                                add_expert(f, s)
                            if more and fl == 1:
                                gelu_out(f, s + 1)
                            if f is not None and s == EXPERTS:
                                if fl in (1, 3):
                                    add_output_bias(f)
                                expert_sum(f)
                        if a is not None:
                            heads_out(a)
                            attention_sum(a)

            nc.sync.sem_clear(range(first_loop_sem.num, last_loop_sem.num + 1))
            nc.all_engine_barrier()


def _layers_of(inputs):
    import numpy as _np

    def a(name):
        return _np.asarray(inputs[name])

    def t(name):
        return a(name).T

    m0, m1 = a("mask_BxSxS2_ik1"), a("mask_Bx1xSxS2_ik0")[:, 0]
    return {
        "x": a("x"),
        "ctx_t": a("ctx_1024").transpose(0, 2, 1),
        "mask00": m0, "mask01": m0.transpose(0, 2, 1),
        "mask10": m1, "mask11": m1.transpose(0, 2, 1),
        "gates": _np.concatenate([a("g_xattn"), a("g_ffn")]),
        "wq": _np.stack([t("L0_xattn_Wq"), t("L1_xattn_w_q"), t("L2_xattn_Wq"), t("L3_xattn_wq")]),
        "wk": _np.stack([t("L0_xattn_Wk"), t("L1_xattn_w_k"), t("L2_xattn_Wk"), t("L3_xattn_wk")]),
        "wv": _np.stack([t("L0_xattn_Wv"), t("L1_xattn_w_v"), t("L2_xattn_Wv"), t("L3_xattn_wv")]),
        "wo": _np.stack([t("L0_xattn_Wo"), t("L1_xattn_w_o"), t("L2_xattn_Wo"), t("L3_xattn_wo")]),
        "bq0": a("L0_xattn_bq"), "bk0": a("L0_xattn_bk"), "bv0": a("L0_xattn_bv"), "bo0": a("L0_xattn_bo"),
        "bq3": a("L3_xattn_bq"), "bk3": a("L3_xattn_bk"), "bv3": a("L3_xattn_bv"), "bo3": a("L3_xattn_bo"),
        "bo2": a("L2_xattn_bo"), "time_decay": a("L3_xattn_time_decay").reshape(1),
        "router": _np.stack([a("L0_ffn_Wr"), t("L1_ffn_router_w"), a("L2_ffn_router_w"), a("L3_ffn_Wr")]),
        "route_bias2": a("L2_ffn_expert_bias"), "route_bias3": a("L3_ffn_br"),
        "up_w0": a("L0_ffn_W1"), "down_w0": a("L0_ffn_W2"),
        "up_w1": a("L1_ffn_w_fc"), "down_w1": a("L1_ffn_w_proj"),
        "up_w3": a("L3_ffn_W1"), "down_w3": a("L3_ffn_W2"),
        "hid_bias1": a("L1_ffn_b_fc").reshape(EXPERTS * CH, P).T, "out_bias1": a("L1_ffn_b_proj"),
        "hid_bias3": a("L3_ffn_b1").reshape(EXPERTS * CH, P).T, "out_bias3": a("L3_ffn_b2"),
        "glu_w1": a("L2_ffn_w1"), "glu_w2": a("L2_ffn_w2"), "glu_w3": a("L2_ffn_w3"),
        "sglu_w1": a("L2_ffn_sw1"), "sglu_w2": a("L2_ffn_sw2"), "sglu_w3": a("L2_ffn_sw3"),
    }


def kernel(**inputs):
    import numpy as _np
    import concourse.bacc as _bacc
    from concourse import mybir as _mybir
    from concourse.bass_utils import run_bass_kernel_spmd as _run

    nc = _bacc.Bacc("TRN2", target_bir_lowering=False, num_devices=1)
    arrays, ins = {}, {}
    for name, value in _layers_of(inputs).items():
        value = _np.ascontiguousarray(value)
        arrays[f"in_{name}"] = value
        ins[name] = nc.dram_tensor(f"in_{name}", value.shape, _mybir.dt.from_np(value.dtype), kind="ExternalInput").ap()
    out = nc.dram_tensor("out_0", (BATCH, S, D), F32, kind="ExternalOutput").ap()
    flamingo_layers(nc, ins, out)
    r = _run(nc, [arrays], core_ids=[0])
    return r.results[0]["out_0"]
```

```python
import concourse.bass as bass
from concourse import mybir
from contextlib import ExitStack

F32 = mybir.dt.float32
F32R = mybir.dt.float32r
BF16 = mybir.dt.bfloat16
I32 = mybir.dt.int32
U32 = mybir.dt.uint32
ALU = mybir.AluOpType
ACT = mybir.ActivationFunctionType
AX = mybir.AxisListType.X

P = 128
LAYERS, BATCH, S, D = 4, 4, 256, 128
LANES = BATCH
LAG = 2
TT = S // P
HEADS, DK = 16, 8
GROUPS, GH = 4, 4
STEPS = HEADS // 2
EXPERTS, FF = 8, 512
CH = FF // P
PHASES = LAYERS * LANES
BIG = float(2 ** 100)
EPS = 1e-5
WINDOW = 4
BAND = P + WINDOW
GELU_A = 0.044715
GELU_C = 0.7978845608028654
GATE_LINKS = (12, 12, 10, 8)
UP_LAYERS = (0, 1, 3)
UP_RING = 2
VW = P + DK


def window(layer, tile):
    return (tile * (S - BAND), BAND) if layer == 2 else (0, S)


def experts(layer):
    return EXPERTS + 1 if layer == 2 else EXPERTS


def experts_before(n):
    return sum(experts(m // LANES) for m in range(n))


def split_phases(n):
    return sum(m // LANES in UP_LAYERS for m in range(n))


def flamingo_layers(nc, ins, out):
    ctx = ExitStack()
    with ctx:
        def sb(name, shape, dt=F32):
            return ctx.enter_context(nc.sbuf_tensor(name, shape, dt))

        def pb(name, shape, dt=F32):
            return ctx.enter_context(nc.psum_tensor(name, shape, dt))

        def sem(name):
            return ctx.enter_context(nc.semaphore(name))

        wq = sb("wq", [P, LAYERS, D])
        wk = sb("wk", [P, LAYERS, D])
        wv = sb("wv", [P, LAYERS, D])
        wo = sb("wo", [P, LAYERS, D])
        up_hi = sb("up_hi", [P, EXPERTS, FF], F32R)
        up_lo = sb("up_lo", [P, EXPERTS, FF], F32R)
        up_in = sb("up_in", [P, UP_RING, FF])
        down_a, down_b = sb("down_a", [P, EXPERTS, CH, D]), sb("down_b", [P, EXPERTS, CH, D])
        down_w = {0: down_a, 1: down_b, 3: down_a}
        glu_w1 = sb("glu_w1", [P, EXPERTS + 1, D])
        glu_w3 = sb("glu_w3", [P, EXPERTS + 1, D])
        glu_w2 = sb("glu_w2", [P, EXPERTS + 1, D])
        router = sb("router", [P, LAYERS, EXPERTS])
        col_bias = {n: sb(n, [P, 1]) for n in ("bq0", "bk0", "bq3", "bk3")}
        bv = {l: sb(f"bv{l}", [P, D]) for l in (0, 3)}
        bo = {l: sb(f"bo{l}", [P, D]) for l in (0, 2, 3)}
        hid_bias = {l: sb(f"hid_bias{l}", [P, EXPERTS, CH]) for l in (1, 3)}
        out_bias = {l: sb(f"out_bias{l}", [P, D]) for l in (1, 3)}
        route_bias = {l: sb(f"route_bias{l}", [P, EXPERTS]) for l in (2, 3)}
        gates = sb("gates", [P, 2 * LAYERS])
        tanh_g = sb("tanh_g", [P, 2 * LAYERS])
        time_decay = sb("time_decay", [P, 1])

        ident = sb("ident", [P, P])
        ident_r = sb("ident_r", [P, P], F32R)
        ident_b = sb("ident_b", [P, P], BF16)
        spread_two = {"q": sb("spread_q_high", [P, GROUPS, P], F32R), "k": sb("spread_k_high", [P, GROUPS, P], F32R)}
        spread_one = {"q": sb("spread_q_low", [P, GROUPS, P], F32R), "k": sb("spread_k_low", [P, GROUPS, P], F32R)}
        ones_rows = sb("ones_rows", [P, 1])
        minus_half = sb("minus_half", [P, TT])
        iota8 = sb("iota8", [P, EXPERTS])
        decay = sb("decay", [P, TT, S])
        decay_hi = sb("decay_hi", [P, TT, S], F32R)
        decay_lo = sb("decay_lo", [P, TT, S], F32R)
        band = sb("band", [P, TT, BAND], BF16)

        x = [sb(f"x{b}", [P, TT, D]) for b in range(LANES)]
        ctx_t = [sb(f"ctx_t{b}", [P, S]) for b in range(LANES)]
        mask = [[sb(f"mask{b}{o}", [P, TT, S], BF16) for o in range(2)] for b in range(LANES)]

        q_stack = sb("q_stack", [P, GROUPS, S], F32R)
        k_stack = sb("k_stack", [P, GROUPS, S], F32R)
        qm_stack = sb("qm_stack", [P, 2, S], F32R)
        qkv_hi = {n: sb(f"{n}_hi", [P, S], F32R)[:, :] for n in "qk"}
        qkv_lo = {n: sb(f"{n}_lo", [P, S], F32R)[:, :] for n in "qk"}
        v_tmp = sb("v_tmp", [P, TT, D])
        v_cols = sb("v_cols", [P, TT, 2, (HEADS // 2) * VW])
        row_max = sb("row_max", [P, HEADS, TT])
        max_parts = sb("max_parts", [P, TT, GH, 32], F32R)
        probs = sb("probs", [P, 2, 2, TT, S])
        inv_sum = sb("inv_sum", [P // 2, 2 * S])[:, :]
        heads_t = sb("heads_t", [P, S])[:, :]
        x_res = sb("x_res", [P, TT, D])
        iota_i = probs[:, 0, 0, :, :].bitcast(I32)
        dist, dist_neg = probs[:, 0, 1, :, :], probs[:, 1, 0, :, :]

        normed_hi, normed_lo = sb("normed_hi", [P, S], F32R), sb("normed_lo", [P, S], F32R)
        hidden = sb("hidden", [P, 2, CH, S])
        pre_act = sb("pre_act", [P, 2, 2, S])
        gelu_t = sb("gelu_t", [P, 2, 2, S])
        acc = sb("acc", [P, TT, D])
        logit = sb("logit", [P, TT, EXPERTS])
        logit_max = sb("logit_max", [P, TT])
        shifted = sb("shifted", [P, TT, EXPERTS])
        exp_l = sb("exp_l", [P, TT, EXPERTS])
        exp_sum = sb("exp_sum", [P, TT])
        exp_inv = sb("exp_inv", [P, TT])
        prob = sb("prob", [P, TT, EXPERTS])
        choice = sb("choice", [P, TT, EXPERTS])
        top8 = sb("top8", [P, TT, 8])
        top_idx = sb("top_idx", [P, TT, 8], U32)
        top_f = sb("top_f", [P, TT, 8])
        pick1 = sb("pick1", [P, TT, EXPERTS])
        pick2 = sb("pick2", [P, TT, EXPERTS])
        picked = sb("picked", [P, TT, EXPERTS])
        gate_raw = sb("gate_raw", [P, TT, EXPERTS])
        gate_sum = sb("gate_sum", [P, TT])
        gate_inv = sb("gate_inv", [P, TT])
        gate_pad = sb("gate_pad", [P, TT, P])
        gate_use = sb("gate_use", [P, TT, EXPERTS])
        gate_t = gelu_t[:, 0, 0, :]
        mask_in = [pre_act[:, i, :, :].bitcast(I32) for i in range(2)]

        smax = pb("smax", [P, 2, 512])
        sexp = pb("sexp", [P, 2, 512])
        cbank = pb("cbank", [P, 512])
        ybank = pb("ybank", [P, 512])
        hbank = pb("hbank", [P, 2, 512])

        w_attn, w_small = sem("w_attn"), sem("w_small")
        w_glu = sem("w_glu")
        up_loaded = [sem(f"up_loaded{i}") for i in range(UP_RING)]
        up_rounded, up_split = sem("up_rounded"), sem("up_split")
        w_down = {l: sem(f"w_down{l}") for l in range(LAYERS)}
        zeroed, ident_made, spread_made, const_made = sem("zeroed"), sem("ident_made"), sem("spread_made"), sem("const_made")
        iota_made, dist_made, decay_made, tanh_made, v_set = (
            sem("iota_made"), sem("dist_made"), sem("decay_made"), sem("tanh_made"), sem("v_set"))

        class Norm:

            def __init__(self, tag):
                self.stats = sb(f"{tag}_stats", [P, TT, 6])
                self.mean_var = sb(f"{tag}_mean_var", [P, TT, 2])
                self.var_eps = sb(f"{tag}_var_eps", [P, TT])
                self.rstd = sb(f"{tag}_rstd", [P, TT])
                self.normed = sb(f"{tag}_normed", [P, TT, D])
                self.normed_t = sb(f"{tag}_normed_t", [P, S])
                self.stats_done = sem(f"{tag}_stats_done")
                self.aggr_done = sem(f"{tag}_aggr_done")
                self.eps_added = sem(f"{tag}_eps_added")
                self.rstd_done = sem(f"{tag}_rstd_done")
                self.normed_done = sem(f"{tag}_normed_done")
                self.turned = sem(f"{tag}_turned")
                self.turned_sb = sem(f"{tag}_turned_sb")

        an, fn = Norm("attn"), Norm("ffn")
        x_loaded = [sem(f"x_loaded{b}") for b in range(LANES)]
        ctx_loaded = [sem(f"ctx_loaded{b}") for b in range(LANES)]
        x_new = [sem(f"x_new{b}") for b in range(LANES)]
        mask_loaded = [sem("mask_loaded0"), sem("mask_loaded1")]
        mask_made, stored = sem("mask_made"), sem("stored")
        k_proj, v_proj, q_proj = sem("k_proj"), sem("v_proj"), sem("q_proj")
        k_hi, k_lo, q_hi, q_lo, v_ready = sem("k_hi_s"), sem("k_lo_s"), sem("q_hi_s"), sem("q_lo_s"), sem("v_ready")
        k_spread, q_spread, k_ready, q_ready = sem("k_spread"), sem("q_spread"), sem("k_ready"), sem("q_ready")
        max_psum, max_red, max_hi, max_lo = sem("max_psum"), sem("max_red"), sem("max_hi"), sem("max_lo")
        max_turned, qm_ready, exp_psum, exp_done, pv_done = (
            sem("max_turned"), sem("qm_ready"), sem("exp_psum"), sem("exp_done"), sem("pv_done"))
        inv_done, heads_ready, attn_out, res_ready = sem("inv_done"), sem("heads_ready"), sem("attn_out"), sem("res_ready")
        logits_psum, gate_step, gate_max, gate_shifted = (
            sem("logits_psum"), sem("gate_step"), sem("gate_max"), sem("gate_shifted"))
        exp_l_done, gate_chain, gate_ready = sem("exp_l_done"), sem("gate_chain"), sem("gate_ready")
        up_psum, hid_ready, y_psum, y_acc = sem("up_psum"), sem("hid_ready"), sem("y_psum"), sem("y_acc")
        pre_ready, sq_ready, inner_ready, tanh_ready = sem("pre_ready"), sem("sq_ready"), sem("inner_ready"), sem("tanh_ready")
        glu_tanh, glu_silu = sem("glu_tanh"), sem("glu_silu")
        gate_turned, gate_t_ready, bias_psum, bias_added = (
            sem("gate_turned"), sem("gate_t_ready"), sem("bias_psum"), sem("bias_added"))
        v_placed, turned_hi, turned_lo = sem("v_placed"), sem("turned_hi"), sem("turned_lo")

        def v_view(lo):
            return v_cols[:, :, :, :].rearrange("p t u (j c) -> p t u j c", c=VW)[:, :, :, :, lo:lo + DK]

        def score_bias(eng_mm, bank, lane, layer):
            if layer == 3:
                eng_mm(bank, ident_r[:, :], decay_hi[:, :, :].rearrange("p t n -> p (t n)"), start=True, stop=False,
                       skip_group_check=True)
                eng_mm(bank, ident_r[:, :], decay_lo[:, :, :].rearrange("p t n -> p (t n)"), start=False, stop=False,
                       skip_group_check=True)
            elif layer == 2:
                for t in range(TT):
                    lo, w = window(layer, t)
                    eng_mm(bank[:, t * S + lo:t * S + lo + w], ident_b[:, :], band[:, t, :],
                           start=(t == 0), stop=False, skip_group_check=True)
            else:
                m = mask[lane][1]
                eng_mm(bank, ident_b[:, :], m[:, :, :].rearrange("p t n -> p (t n)"), start=True, stop=False,
                       skip_group_check=True)

        small = [
            (router[:, :, :], ins["router"].rearrange("l p e -> p l e")),
            (gates[:, :], ins["gates"].partition_broadcast(P)),
            (time_decay[:, :], ins["time_decay"].partition_broadcast(P)),
        ]
        for n in ("bq0", "bk0", "bq3", "bk3"):
            small.append((col_bias[n][:, :], ins[n].rearrange("(p a) -> p a", a=1)))
        for l in (0, 3):
            small.append((bv[l][:, :], ins[f"bv{l}"].partition_broadcast(P)))
        for l in (0, 2, 3):
            small.append((bo[l][:, :], ins[f"bo{l}"].partition_broadcast(P)))
        for l in (2, 3):
            small.append((route_bias[l][:, :], ins[f"route_bias{l}"].partition_broadcast(P)))
        for l in (1, 3):
            small.append((hid_bias[l][:, :, :], ins[f"hid_bias{l}"].rearrange("p (e c) -> p e c", c=CH)))
            small.append((out_bias[l][0:EXPERTS, :], ins[f"out_bias{l}"]))
        SMALL = 16 * len(small)

        with nc.Block(no_gpsimd_drain=True) as block:
            @block.sync
            def _(sp):
                sp.dma_start(x[0][:, :, :], ins["x"][0].rearrange("(t p) n -> p t n", p=P)).then_inc(x_loaded[0], 16)
                sp.dma_start(ctx_t[0][:, :], ins["ctx_t"][0]).then_inc(ctx_loaded[0], 16)
                for w, name in ((wk, "wk"), (wv, "wv"), (wq, "wq"), (wo, "wo")):
                    sp.dma_start(w[:, :, :], ins[name].rearrange("l p n -> p l n")).then_inc(w_attn, 16)
                sp.wait_ge(zeroed, 2)
                for dst, src in small:
                    sp.dma_start(dst, src).then_inc(w_small, 16)
                for b in range(1, LANES):
                    sp.dma_start(x[b][:, :, :], ins["x"][b].rearrange("(t p) n -> p t n", p=P)).then_inc(x_loaded[b], 16)
                    sp.dma_start(ctx_t[b][:, :], ins["ctx_t"][b]).then_inc(ctx_loaded[b], 16)

            @block.scalar
            def _(act):
                act.wait_ge(w_small, SMALL)
                act.activation(tanh_g[:, :], gates[:, :], ACT.Tanh).then_inc(tanh_made, 1)

            @block.gpsimd
            def _(pool):
                for l in (1, 3):
                    pool.memset(out_bias[l][:, :], 0.0).then_inc(zeroed, 1)
                pool.memset(ident[:, :], 1.0).then_inc(ident_made, 1)
                pool.wait_ge(ident_made, 1)
                pool.affine_select(out=ident[:, :], in_=ident[:, :], compare_op=ALU.is_equal, fill=0.0, base=0,
                                   pattern=[[-1, P]], channel_multiplier=1).then_inc(ident_made, 1)
                pool.iota(iota_i, [[P, TT], [-1, S]], base=0, channel_multiplier=1).then_inc(iota_made, 1)
                pool.wait_ge(ident_made, 2)
                pool.tensor_copy(ident_r[:, :], ident[:, :]).then_inc(ident_made, 1)
                pool.tensor_copy(ident_b[:, :], ident[:, :]).then_inc(ident_made, 1)
                pool.memset(minus_half[:, :], -0.5).then_inc(const_made, 1)
                for e in range(EXPERTS):
                    pool.memset(iota8[:, e:e + 1], float(e)).then_inc(const_made, 1)
                pool.memset(gate_pad[:, :, :], 0.0).then_inc(const_made, 1)
                pool.wait_ge(w_attn, 64)
                pool.wait_ge(w_small, SMALL)
                pool.tensor_scalar(wq[:, :, :], wq[:, :, :], DK ** -0.5, None, ALU.mult).then_inc(const_made, 1)
                for n in ("bq0", "bq3"):
                    pool.tensor_scalar(col_bias[n][:, :], col_bias[n][:, :], DK ** -0.5, None, ALU.mult)\
                        .then_inc(const_made, 1)
                pool.wait_ge(tanh_made, 1)
                for l in (0, 2, 3):
                    pool.tensor_scalar(bo[l][:, :], bo[l][:, :], tanh_g[:, l:l + 1], None, ALU.mult)\
                        .then_inc(const_made, 1)

            @block.vector
            def _(dve):
                for t in (spread_two["q"], spread_two["k"], spread_one["q"], spread_one["k"]):
                    dve.memset(t[:, :, :].bitcast(F32), 0.0).then_inc(v_set, 1)
                dve.memset(max_parts[:, :, :, :].bitcast(F32), 0.0).then_inc(v_set, 1)
                dve.memset(v_cols[:, :, :, :], 0.0).then_inc(v_set, 1)
                dve.wait_ge(v_set, 6)
                dve.memset(v_view(P // 2)[:, 0, :, :, :], 1.0).then_inc(v_set, 1)
                dve.memset(v_view(P // 2)[:, 1, :, :, :], 1.0).then_inc(v_set, 1)
                dve.wait_ge(ident_made, 3)
                for g in range(GROUPS):
                    src = ident[:, g * 32:(g + 1) * 32].rearrange("p (h d) -> p h d", d=DK)
                    for t, copies in ((spread_two["q"], (0, 1)), (spread_one["q"], (2,)),
                                      (spread_two["k"], (0, 2)), (spread_one["k"], (1,))):
                        for c in copies:
                            dst = t[:, g, :].rearrange("p (h r) -> p h r", r=32)[:, :, c * DK:(c + 1) * DK]
                            dve.tensor_copy(dst, src).then_inc(spread_made, 1)
                rows = ident[:, :].rearrange("p (h r) -> p h r", r=32)[:, :, 3 * DK:3 * DK + 2]
                dve.tensor_reduce(ones_rows[:, :], rows, mybir.AxisListType.XY, ALU.add).then_inc(spread_made, 1)
                dve.wait_ge(iota_made, 1)
                dve.tensor_copy(dist, iota_i).then_inc(dist_made, 1)
                dve.wait_ge(dist_made, 1)
                dve.tensor_scalar(dist_neg, dist, -1.0, None, ALU.mult).then_inc(dist_made, 1)
                dve.wait_ge(dist_made, 2)
                dve.tensor_tensor(dist, dist, dist_neg, ALU.max).then_inc(dist_made, 1)
                dve.wait_ge(dist_made, 3)
                for t in range(TT):
                    lo, n = window(2, t)
                    dve.tensor_scalar(band[:, t, :], dist[:, t, lo:lo + n], float(WINDOW), -BIG, ALU.is_gt, ALU.mult)\
                       .then_inc(decay_made, 1)
                dve.wait_ge(w_small, SMALL)
                dve.tensor_scalar(dist_neg, dist, time_decay[:, 0:1], -1.0, ALU.mult, ALU.mult)\
                   .then_inc(dist_made, 1)
                dve.wait_ge(dist_made, 4)
                dve.tensor_copy(decay[:, :, :], dist_neg).then_inc(decay_made, 1)
                dve.tensor_copy(decay_hi[:, :, :], dist_neg).then_inc(dist_made, 1)
                dve.wait_ge(dist_made, 5)
                dve.tensor_tensor(decay_lo[:, :, :], dist_neg, decay_hi[:, :, :].bitcast(F32), ALU.subtract)\
                   .then_inc(decay_made, 1)


        def x_ready(n, kind):
            return (x_loaded[n % LANES], 16) if n < LANES and kind == 0 else (x_new[n % LANES], 2 * (n // LANES) + kind)

        def masks_for(n):
            return 2 * (n + 1)

        def biased(n):
            return sum(m // LANES in (1, 3) for m in range(n))

        def phases(slot):
            a = slot if slot < PHASES else None
            f = slot - LAG if slot >= LAG else None
            nxt = slot + 1 if slot + 1 < PHASES else None
            prev = slot - 1 if 1 <= slot <= PHASES else None
            return a, f, nxt, prev

        with nc.Block(no_gpsimd_drain=True) as block:
            @block.sync
            def _(sp):
                def load_mask(i):
                    m, b, o = i // (2 * LANES), i // 2 % LANES, i % 2
                    if i >= 2:
                        sp.wait_ge(mask_made, i - 1)
                    sp.dma_start(mask_in[i % 2], ins[f"mask{m}{o}"][b].rearrange("(t p) n -> p t n", p=P))\
                      .then_inc(mask_loaded[i % 2], 16)

                def load_up(j):
                    if j >= UP_RING:
                        sp.wait_ge(up_split, j - UP_RING + 1)
                    sp.dma_start(up_in[:, j % UP_RING, :], ins[f"up_w{UP_LAYERS[j // EXPERTS]}"][j % EXPERTS])\
                      .then_inc(up_loaded[j % UP_RING], 16)

                def load_down(l):
                    sp.dma_start(down_w[l][:, :, :, :], ins[f"down_w{l}"].rearrange("e (c p) n -> p e c n", p=P))\
                      .then_inc(w_down[l], 16)

                for i in range(2 * LANES):
                    load_mask(i)
                for j in range(UP_RING):
                    load_up(j)
                load_down(0)
                for j in range(UP_RING, EXPERTS):
                    load_up(j)
                load_down(1)
                for w, name in ((glu_w1, "glu_w1"), (glu_w3, "glu_w3")):
                    sp.dma_start(w[:, 0:EXPERTS, :], ins[name].rearrange("e p n -> p e n")).then_inc(w_glu, 16)
                    sp.dma_start(w[:, EXPERTS, :], ins["s" + name]).then_inc(w_glu, 16)
                sp.dma_start(glu_w2[:, 0:EXPERTS, :], ins["glu_w2"].rearrange("e p n -> p e n")).then_inc(w_down[2], 16)
                sp.dma_start(glu_w2[:, EXPERTS, :], ins["sglu_w2"]).then_inc(w_down[2], 16)
                for i in range(2 * LANES, 4 * LANES):
                    load_mask(i)
                for j in range(EXPERTS, 2 * EXPERTS + UP_RING):
                    load_up(j)
                sp.wait_ge(y_psum, experts_before(LANES))
                load_down(3)
                for j in range(2 * EXPERTS + UP_RING, 3 * EXPERTS):
                    load_up(j)
                for b in range(LANES):
                    sp.wait_ge(x_new[b], 2 * LAYERS)
                    sp.dma_start(out[b].rearrange("(t p) n -> p t n", p=P), x[b][:, :, :]).then_inc(stored, 16)
                sp.wait_ge(stored, 16 * LANES)

            @block.gpsimd
            def _(pool):
                def make_masks(n):
                    b = n % LANES
                    if n >= LANES:
                        pool.wait_ge(max_red, STEPS * (b + 1))
                        pool.wait_ge(exp_psum, STEPS * (b + 1))
                    for o in range(2):
                        i = 2 * n + o
                        pool.wait_ge(mask_loaded[i % 2], 16 * (i // 2 + 1))
                        if n >= LANES:
                            pool.wait_ge(mask_made, 2 * b + o + 1)
                        pool.tensor_scalar(mask[b][o][:, :, :], mask_in[i % 2], 0.0, -BIG,
                                           ALU.is_equal, ALU.mult).then_inc(mask_made, 1)

                def split_up(j):
                    i, e = j // EXPERTS, j % EXPERTS
                    pool.wait_ge(up_loaded[j % UP_RING], 16 * (j // UP_RING + 1))
                    if i:
                        before = UP_LAYERS[i - 1] * LANES + LANES - 1
                        pool.wait_ge(up_psum, 2 * (experts_before(before) + e + 1))
                    pool.tensor_copy(up_hi[:, e, :], up_in[:, j % UP_RING, :]).then_inc(up_rounded, 1)
                    pool.wait_ge(up_rounded, j + 1)
                    pool.tensor_tensor(up_lo[:, e, :], up_in[:, j % UP_RING, :], up_hi[:, e, :].bitcast(F32),
                                       ALU.subtract).then_inc(up_split, 1)

                def rstd(ln, n):
                    pool.wait_ge(ln.aggr_done, TT * (n + 1))
                    pool.tensor_scalar(ln.var_eps[:, :], ln.mean_var[:, :, 1], EPS, None, ALU.add)\
                        .then_inc(ln.eps_added, 1)
                    pool.wait_ge(ln.eps_added, n + 1)
                    pool.tensor_tensor(ln.rstd[:, :], ln.var_eps[:, :], minus_half[:, :], ALU.pow)\
                        .then_inc(ln.rstd_done, 1)

                def residual_with_bias(n):
                    layer, b = n // LANES, n % LANES
                    if layer == 1:
                        return
                    pool.wait_ge(*x_ready(n, 0))
                    if n:
                        pool.wait_ge(x_new[(n - 1) % LANES], 2 * ((n - 1) // LANES) + 1)
                    for t in range(TT):
                        last = pool.tensor_tensor(x_res[:, t, :], x[b][:, t, :], bo[layer][:, :], ALU.add)
                    last.then_inc(res_ready, 1)

                def gelu_square(n, e):
                    for u in range(2):
                        c = 2 * (EXPERTS * (n - LANES) + e) + u + 1
                        pool.wait_ge(pre_ready, c)
                        if c > 2:
                            pool.wait_ge(hid_ready, 2 * (experts_before(n) + e - 1) + u + 1)
                        pool.tensor_tensor(gelu_t[:, u, :, :], pre_act[:, u, :, :], pre_act[:, u, :, :], ALU.mult)\
                            .then_inc(sq_ready, 1)

                def place_v(n):
                    pool.wait_ge(v_ready, n + 1)
                    if n:
                        pool.wait_ge(pv_done, STEPS * n)
                    for t in range(TT):
                        last = pool.tensor_copy(v_view(0)[:, t, :, :, :],
                                                v_tmp[:, t, :].rearrange("p (u j d) -> p u j d", u=2, d=DK))
                    last.then_inc(v_placed, 1)

                rstd(an, 0)
                make_masks(0)
                place_v(0)
                splits = {}
                for j in range(EXPERTS):
                    for i, first in enumerate(((0, 6), (LANES + LAG - 1, 1), (2 * LANES + LAG, 1))):
                        slot, s = first[0] + (first[1] + j) // (STEPS + 3), (first[1] + j) % (STEPS + 3)
                        splits[slot, s] = EXPERTS * i + j
                for slot in range(PHASES + LAG):
                    a, f, nxt, prev = phases(slot)
                    gelu = f is not None and f // LANES == 1
                    if gelu:
                        gelu_square(f, 0)
                    for s in range(STEPS + 3):
                        if gelu and s + 1 < EXPERTS:
                            gelu_square(f, s + 1)
                        if slot == 0 and s < LANES - 1:
                            make_masks(s + 1)
                        if slot in range(1, LANES + 1) and s == 2:
                            make_masks(LANES + slot - 1)
                        if a is not None and s == 3:
                            residual_with_bias(a)
                        if (slot, s) in splits:
                            split_up(splits[slot, s])
                        if s == 5 and prev is not None:
                            rstd(fn, prev)
                        if s == 5 and nxt is not None:
                            rstd(an, nxt)
                    if nxt is not None:
                        place_v(nxt)

            @block.tensor
            def _(pe):
                def mm(o, lhs, rhs, **kw):
                    return nc.tensor.matmul(o, lhs, rhs, **kw)

                def kv_project(n):
                    layer, b = n // LANES, n % LANES
                    pe.wait_ge(w_attn, 64)
                    pe.wait_ge(ctx_loaded[b], 16)
                    if n:
                        pe.wait_ge(qm_ready, GROUPS * n)
                    mm(smax[:, 1, 0:S], wk[:, layer, :], ctx_t[b][:, :], start=True, stop=True).then_inc(k_proj, 1)
                    for t in range(TT):
                        last = mm(smax[:, 1, S + t * D:S + (t + 1) * D], ctx_t[b][:, t * P:(t + 1) * P], wv[:, layer, :],
                                  start=True, stop=True)
                    last.then_inc(v_proj, 1)

                def turn(ln, n, bank):
                    pe.wait_ge(ident_made, 2)
                    pe.wait_ge(ln.normed_done, TT * (n + 1))
                    for t in range(TT):
                        last = nc.tensor.transpose(bank[:, t * P:(t + 1) * P], ln.normed[:, t, :], ident[:, :])
                    last.then_inc(ln.turned, 1)

                def q_project(n):
                    pe.wait_ge(an.turned_sb, n + 1)
                    mm(smax[:, 0, S:2 * S], wq[:, n // LANES, :], an.normed_t[:, :], start=True, stop=True)\
                        .then_inc(q_proj, 1)

                def spread(n, which, bank, parts_done, done):
                    pe.wait_ge(parts_done, n + 1)
                    flat = bank[:, :, :].rearrange("p a n -> p (a n)")
                    for g in range(GROUPS):
                        o = flat[:, g * S:(g + 1) * S]
                        mm(o, spread_two[which][:, g, :], qkv_hi[which], start=True, stop=False)
                        last = mm(o, spread_one[which][:, g, :], qkv_lo[which], start=False, stop=True)
                    last.then_inc(done, 1)

                def spread_k(n):
                    pe.wait_ge(q_lo, n + 1)
                    pe.wait_ge(v_ready, n + 1)
                    spread(n, "k", smax, k_lo, k_spread)

                def spread_q(n):
                    if n:
                        pe.wait_ge(exp_done, STEPS * n)
                    spread(n, "q", sexp, q_lo, q_spread)

                def strip(h):
                    return slice(32 * (h % GH), 32 * (h % GH) + 32)

                def max_scores(n, s):
                    if s == 0:
                        pe.wait_ge(k_ready, n + 1)
                        pe.wait_ge(q_ready, n + 1)
                    else:
                        pe.wait_ge(max_red, STEPS * n + s)
                        if s % 2 == 0:
                            pe.wait_ge(qm_ready, GROUPS * n + s // 2)
                    for j in range(2):
                        h = 2 * s + j
                        for t in range(TT):
                            last = mm(smax[:, j, t * S:(t + 1) * S], q_stack[strip(h), h // GH, t * P:(t + 1) * P],
                                      k_stack[strip(h), h // GH, :], start=(t == 0), stop=(t == TT - 1),
                                      skip_group_check=True)
                    last.then_inc(max_psum, 1)

                def turn_max(n, g):
                    pe.wait_ge(max_lo, GROUPS * n + g + 1)
                    for t in range(TT):
                        last = mm(smax[:, 0, t * P:(t + 1) * P], max_parts[:, t, :, :].rearrange("p h r -> p (h r)"),
                                  ident_r[:, :], start=True, stop=True)
                    last.then_inc(max_turned, 1)

                def exp_scores(n, s):
                    layer, b = n // LANES, n % LANES
                    if layer < 2:
                        pe.wait_ge(mask_made, masks_for(n))
                    pe.wait_ge(qm_ready, GROUPS * n + s // 2 + 1)
                    if s:
                        pe.wait_ge(exp_done, STEPS * n + s)
                    for j in range(2):
                        h = 2 * s + j
                        score_bias(mm, sexp[:, j, :], b, layer)
                        for t in range(TT):
                            last = mm(sexp[:, j, t * S:(t + 1) * S], k_stack[strip(h), h // GH, t * P:(t + 1) * P],
                                      qm_stack[strip(h), h // GH % 2, :], start=False, stop=(t == TT - 1),
                                      skip_group_check=True)
                    last.then_inc(exp_psum, 1)

                def times_v(n, s):
                    layer = n // LANES
                    pe.wait_ge(exp_done, STEPS * n + s + 1)
                    if s == 0:
                        pe.wait_ge(v_placed, n + 1)
                        if n:
                            pe.wait_ge(x_new[(n - 1) % LANES], 2 * ((n - 1) // LANES) + 1)
                    for j in range(2):
                        h = 2 * s + j
                        u, hj = h // (HEADS // 2), h % (HEADS // 2)
                        for t in range(TT):
                            lo, w = window(layer, t)
                            last = mm(cbank[:, u * S + lo:u * S + lo + w], v_cols[:, t, u, hj * P:(hj + 1) * P],
                                      probs[:, s % 2, j, t, 0:w], start=(hj == 0 and t == 0),
                                      stop=(hj == HEADS // 2 - 1 and t == TT - 1), skip_group_check=True)
                    last.then_inc(pv_done, 1)

                def out_project(n):
                    pe.wait_ge(heads_ready, 2 * (n + 1))
                    for t in range(TT):
                        last = mm(cbank[:, t * D:(t + 1) * D], heads_t[:, t * P:(t + 1) * P], wo[:, n // LANES, :],
                                  start=True, stop=True)
                    last.then_inc(attn_out, 1)

                def logits(n):
                    pe.wait_ge(fn.turned_sb, n + 1)
                    pe.wait_ge(w_small, SMALL)
                    for t in range(TT):
                        last = mm(ybank[:, S + t * EXPERTS:S + (t + 1) * EXPERTS], fn.normed_t[:, t * P:(t + 1) * P],
                                  router[:, n // LANES, :], start=True, stop=True)
                    last.then_inc(logits_psum, 1)

                def up(n, e):
                    layer, done = n // LANES, experts_before(n) + e
                    if layer == 2:
                        pe.wait_ge(w_glu, 64)
                    else:
                        pe.wait_ge(up_split, EXPERTS * UP_LAYERS.index(layer) + e + 1)
                        pe.wait_ge(turned_hi, split_phases(n) + 1)
                        pe.wait_ge(turned_lo, split_phases(n) + 1)
                    for u in range(2):
                        if done:
                            if layer == 1 and e:
                                pe.wait_ge(pre_ready, 2 * (EXPERTS * (n - LANES) + e - 1) + u + 1)
                            else:
                                pe.wait_ge(hid_ready, 2 * done if layer == 2 or e == 0 else 2 * (done - 1) + u + 1)
                        if e == 0 and n and (n - 1) // LANES in (1, 3):
                            pe.wait_ge(gate_t_ready, biased(n))
                        if layer == 2:
                            last = mm(hbank[:, u, 0:S], (glu_w1, glu_w3)[u][:, e, :], fn.normed_t[:, :],
                                      start=True, stop=True)
                        else:
                            for c in range(2):
                                o, cols = hbank[:, u, c * S:(c + 1) * S], slice((2 * u + c) * P, (2 * u + c + 1) * P)
                                mm(o, up_hi[:, e, cols], normed_hi[:, :], start=True, stop=False)
                                mm(o, up_hi[:, e, cols], normed_lo[:, :], start=False, stop=False)
                                last = mm(o, up_lo[:, e, cols], normed_hi[:, :], start=False, stop=True)
                        last.then_inc(up_psum, 1)

                def down(n, e):
                    layer, done = n // LANES, experts_before(n) + e
                    pe.wait_ge(w_down[layer], 32 if layer == 2 else 16)
                    pe.wait_ge(hid_ready, 2 * (done + 1))
                    if e == 0:
                        pe.wait_ge(gate_step, n + 1)
                    else:
                        pe.wait_ge(y_acc, done)
                    for t in range(TT):
                        o = ybank[:, t * D:(t + 1) * D]
                        if layer == 2:
                            last = mm(o, hidden[:, done % 2, 0, t * P:(t + 1) * P], glu_w2[:, e, :], start=True, stop=True)
                        else:
                            for c in range(CH):
                                last = mm(o, hidden[:, done % 2, c, t * P:(t + 1) * P], down_w[layer][:, e, c, :],
                                          start=(c == 0), stop=(c == CH - 1))
                    last.then_inc(y_psum, 1)

                def output_bias(n):
                    layer = n // LANES
                    pe.wait_ge(gate_ready, n + 1)
                    pe.wait_ge(hid_ready, 2 * experts_before(n + 1))
                    for t in range(TT):
                        last = nc.tensor.transpose(hbank[:, 0, t * P:(t + 1) * P], gate_pad[:, t, :], ident[:, :])
                    last.then_inc(gate_turned, 1)
                    pe.wait_ge(gate_t_ready, biased(n) + 1)
                    pe.wait_ge(y_acc, experts_before(n + 1))
                    for t in range(TT):
                        last = mm(ybank[:, t * D:(t + 1) * D], gate_t[:, t * P:(t + 1) * P], out_bias[layer][:, :],
                                  start=True, stop=True)
                    last.then_inc(bias_psum, 1)

                kv_project(0)
                turn(an, 0, smax[:, 0, :])
                q_project(0)
                spread_k(0)
                spread_q(0)
                for slot in range(PHASES + LAG):
                    a, f, nxt, prev = phases(slot)
                    if f is not None:
                        if f:
                            pe.wait_ge(x_new[(f - 1) % LANES], 2 * ((f - 1) // LANES) + 2)
                        turn(fn, f, ybank)
                    if a is not None:
                        max_scores(a, 0)
                    if f is not None:
                        logits(f)
                        up(f, 0)
                    for s in range(STEPS + 3):
                        if a is not None and 1 <= s < STEPS:
                            max_scores(a, s)
                        if prev is not None and s == 1:
                            out_project(prev)
                        if f is not None and s + 1 < experts(f // LANES):
                            up(f, s + 1)
                        if a is not None and s < STEPS and s % 2:
                            turn_max(a, s // 2)
                        if a is not None and 2 <= s < STEPS + 2:
                            exp_scores(a, s - 2)
                        if f is not None and s < experts(f // LANES):
                            down(f, s)
                        if f is not None and s == EXPERTS and f // LANES in (1, 3):
                            output_bias(f)
                        if nxt is not None:
                            if s == STEPS:
                                kv_project(nxt)
                                turn(an, nxt, smax[:, 0, :])
                            if s == STEPS + 1:
                                q_project(nxt)
                            if s == STEPS + 2:
                                spread_k(nxt)
                        if a is not None and s >= 3:
                            times_v(a, s - 3)
                    if nxt is not None:
                        spread_q(nxt)

            @block.scalar
            def _(act):
                def high_part(n, which, proj, done, src):
                    layer = n // LANES
                    act.wait_ge(proj, n + 1)
                    if which == "k":
                        act.wait_ge(v_proj, n + 1)
                    if n:
                        act.wait_ge(q_spread if which == "q" else k_spread, n)
                    if layer in (0, 3):
                        i = act.activation(qkv_hi[which], src, ACT.Identity, bias=col_bias[f"b{which}{layer}"][:, :])
                    else:
                        i = act.activation(qkv_hi[which], src, ACT.Copy)
                    i.then_inc(done, 1)

                def copy_turned(ln, n, bank):
                    act.wait_ge(ln.turned, n + 1)
                    act.activation(ln.normed_t[:, :], bank[:, 0:S], ACT.Copy).then_inc(ln.turned_sb, 1)

                def copy_turned_high(n):
                    if n // LANES != 2:
                        act.wait_ge(fn.turned, n + 1)
                        act.activation(normed_hi[:, :], ybank[:, 0:S], ACT.Copy).then_inc(turned_hi, 1)

                def copy_q_stack(n):
                    act.wait_ge(q_spread, n + 1)
                    act.activation(q_stack[:, :, :].rearrange("p g n -> p (g n)"),
                                   sexp[:, :, :].rearrange("p a n -> p (a n)"), ACT.Copy).then_inc(q_ready, 1)

                def exp_logits(n):
                    act.wait_ge(gate_step, n + 1)
                    act.wait_ge(gate_shifted, n + 1)
                    act.activation(exp_l[:, :, :], shifted[:, :, :], ACT.Exp).then_inc(exp_l_done, 1)

                def exponentials(n, s):
                    layer = n // LANES
                    act.wait_ge(exp_psum, STEPS * n + s + 1)
                    if STEPS * n + s >= 2:
                        act.wait_ge(pv_done, STEPS * n + s - 1)
                    if layer == 2:
                        for t in range(TT):
                            lo, w = window(layer, t)
                            last = act.activation(probs[:, s % 2, :, t, 0:w], sexp[:, :, t * S + lo:t * S + lo + w], ACT.Exp)
                    else:
                        last = act.activation(probs[:, s % 2, :, :, :].rearrange("p j t n -> p (j t n)"),
                                              sexp[:, :, :].rearrange("p j n -> p (j n)"), ACT.Exp)
                    last.then_inc(exp_done, 1)

                def hidden_units(n, e):
                    layer, done = n // LANES, experts_before(n) + e
                    for u in range(2):
                        act.wait_ge(up_psum, 2 * done + u + 1)
                        if layer == 0:
                            if done >= 2:
                                act.wait_ge(y_psum, done - 1)
                            act.activation(hidden[:, done % 2, 2 * u:2 * u + 2, :].rearrange("p c n -> p (c n)"),
                                           hbank[:, u, :], ACT.Relu).then_inc(hid_ready, 1)
                        elif layer == 3:
                            act.wait_ge(y_psum, done - 1)
                            for c in range(2):
                                last = act.activation(hidden[:, done % 2, 2 * u + c, :], hbank[:, u, c * S:(c + 1) * S],
                                                      ACT.Relu, bias=hid_bias[3][:, e, 2 * u + c:2 * u + c + 1])
                            last.then_inc(hid_ready, 1)
                        elif layer == 1:
                            if e or n > LANES:
                                act.wait_ge(hid_ready, 2 * (done - 1) + u + 1)
                            else:
                                act.wait_ge(mask_made, 4 * LANES)
                            for c in range(2):
                                last = act.activation(pre_act[:, u, c, :], hbank[:, u, c * S:(c + 1) * S],
                                                      ACT.Identity, bias=hid_bias[1][:, e, 2 * u + c:2 * u + c + 1])
                            last.then_inc(pre_ready, 1)
                        elif u == 0:
                            if done > experts_before(2 * LANES):
                                act.wait_ge(hid_ready, 2 * done)
                            act.activation(pre_act[:, 0, 0, :], hbank[:, 0, 0:S], ACT.Tanh, scale=0.5)\
                               .then_inc(glu_tanh, 1)

                def gelu_tanh(n, e):
                    for u in range(2):
                        act.wait_ge(inner_ready, 2 * (EXPERTS * (n - LANES) + e) + u + 1)
                        act.activation(gelu_t[:, u, :, :], gelu_t[:, u, :, :], ACT.Tanh, scale=GELU_C * GELU_A)\
                           .then_inc(tanh_ready, 1)

                def copy_gates(n):
                    act.wait_ge(gate_turned, biased(n) + 1)
                    act.activation(gate_t, hbank[:, 0, 0:S], ACT.Copy).then_inc(gate_t_ready, 1)

                high_part(0, "k", k_proj, k_hi, smax[:, 1, 0:S])
                copy_turned(an, 0, smax[:, 0, :])
                high_part(0, "q", q_proj, q_hi, smax[:, 0, S:2 * S])
                copy_q_stack(0)
                for slot in range(PHASES + LAG):
                    a, f, nxt, prev = phases(slot)
                    if f is not None:
                        copy_turned_high(f)
                        copy_turned(fn, f, ybank)
                        hidden_units(f, 0)
                        if f // LANES == 1:
                            gelu_tanh(f, 0)
                        exp_logits(f)
                    for s in range(STEPS + 3):
                        more = f is not None and s + 1 < experts(f // LANES)
                        if more:
                            hidden_units(f, s + 1)
                        if a is not None and 2 <= s < STEPS + 2:
                            exponentials(a, s - 2)
                        if more and f // LANES == 1:
                            gelu_tanh(f, s + 1)
                        if f is not None and s == EXPERTS and f // LANES in (1, 3):
                            copy_gates(f)
                        if nxt is not None:
                            if s == STEPS:
                                copy_turned(an, nxt, smax[:, 0, :])
                                high_part(nxt, "k", k_proj, k_hi, smax[:, 1, 0:S])
                            if s == STEPS + 1:
                                high_part(nxt, "q", q_proj, q_hi, smax[:, 0, S:2 * S])
                            if s == STEPS + 2:
                                copy_q_stack(nxt)

            @block.vector
            def _(dve):
                def statistics(ln, n, kind):
                    dve.wait_ge(*x_ready(n, kind))
                    for t in range(TT):
                        dve.bn_stats(ln.stats[:, t, :], x[n % LANES][:, t, :]).then_inc(ln.stats_done, 1)
                    dve.wait_ge(ln.stats_done, TT * (n + 1))
                    for t in range(TT):
                        dve.bn_aggr(ln.mean_var[:, t, :], ln.stats[:, t, :]).then_inc(ln.aggr_done, 1)

                def normalise(ln, n):
                    dve.wait_ge(ln.rstd_done, n + 1)
                    if n:
                        dve.wait_ge(ln.turned, n)
                    for t in range(TT):
                        dve.tensor_scalar(ln.normed[:, t, :], x[n % LANES][:, t, :], ln.mean_var[:, t, 0:1],
                                          ln.rstd[:, t:t + 1], ALU.subtract, ALU.mult).then_inc(ln.normed_done, 1)

                def turned_low_part(n):
                    if n // LANES != 2:
                        dve.wait_ge(turned_hi, split_phases(n) + 1)
                        dve.wait_ge(fn.turned_sb, n + 1)
                        dve.tensor_tensor(normed_lo[:, :], fn.normed_t[:, :], normed_hi[:, :].bitcast(F32), ALU.subtract)\
                           .then_inc(turned_lo, 1)

                def low_part(n, which, hi_done, done, src):
                    layer = n // LANES
                    dve.wait_ge(hi_done, n + 1)
                    bias = col_bias[f"b{which}{layer}"][:, :] if layer in (0, 3) else 0.0
                    dve.scalar_tensor_tensor(out=qkv_lo[which], in0=src, scalar=bias,
                                             in1=qkv_hi[which].bitcast(F32), op0=ALU.add, op1=ALU.subtract)\
                       .then_inc(done, 1)

                def take_v(n):
                    layer = n // LANES
                    dve.wait_ge(v_proj, n + 1)
                    if n:
                        dve.wait_ge(v_placed, n)
                    src = smax[:, 1, S:2 * S].rearrange("p (t n) -> p t n", t=TT)
                    if layer in (0, 3):
                        i = dve.tensor_tensor(v_tmp[:, :, :], src, bv[layer][:, :].unsqueeze(1).broadcast_to([P, TT, D]),
                                              ALU.add)
                    else:
                        i = dve.tensor_copy(v_tmp[:, :, :], src)
                    i.then_inc(v_ready, 1)

                def copy_k_stack(n):
                    dve.wait_ge(k_spread, n + 1)
                    if n:
                        dve.wait_ge(exp_psum, STEPS * n)
                    dve.tensor_scalar(k_stack[:, :, :].rearrange("p g n -> p (g n)"),
                                      smax[:, :, :].rearrange("p a n -> p (a n)"), ones_rows[:, 0:1], None,
                                      ALU.add).then_inc(k_ready, 1)

                def reduce_max(n, s):
                    layer, b = n // LANES, n % LANES
                    if layer < 2 and s == 0:
                        dve.wait_ge(mask_made, masks_for(n))
                    dve.wait_ge(max_psum, STEPS * n + s + 1)
                    if s == 0 and n:
                        dve.wait_ge(max_lo, GROUPS * n)
                    for j in range(2):
                        for t in range(TT):
                            lo, w = window(layer, t)
                            bias = {0: mask[b][0], 1: mask[b][0], 2: band, 3: decay}[layer][:, t, :]
                            scores = smax[:, j, t * S + lo:t * S + lo + w]
                            last = dve.tensor_tensor_reduce(scores, scores, bias, 1.0, -3.0e38, ALU.add, ALU.max,
                                                            row_max[:, 2 * s + j, t:t + 1])
                    last.then_inc(max_red, 1)

                def split_max(n, g):
                    dve.wait_ge(max_red, STEPS * n + 2 * g + 2)
                    if GROUPS * n + g:
                        dve.wait_ge(max_turned, GROUPS * n + g)
                    src = row_max[:, GH * g:GH * g + GH, :].rearrange("p h t -> p t h")
                    hi, lo = max_parts[:, :, :, 3 * DK], max_parts[:, :, :, 3 * DK + 1]
                    dve.tensor_scalar(hi, src, -1.0, None, ALU.mult).then_inc(max_hi, 1)
                    dve.wait_ge(max_hi, GROUPS * n + g + 1)
                    dve.scalar_tensor_tensor(out=lo, in0=src, scalar=-1.0, in1=hi.bitcast(F32),
                                             op0=ALU.mult, op1=ALU.subtract).then_inc(max_lo, 1)

                def add_max(n, g):
                    dve.wait_ge(max_turned, GROUPS * n + g + 1)
                    if GROUPS * n + g >= 2:
                        dve.wait_ge(exp_psum, STEPS * n + 2 * g - 2)
                    dve.tensor_tensor(qm_stack[:, g % 2, :], smax[:, 0, 0:S], q_stack[:, g, :].bitcast(F32), ALU.add)\
                       .then_inc(qm_ready, 1)

                def heads_out(n):
                    dve.wait_ge(pv_done, STEPS * (n + 1))
                    dve.reciprocal(inv_sum, cbank[P // 2:P, :]).then_inc(inv_done, 1)
                    dve.wait_ge(inv_done, n + 1)
                    for u in range(2):
                        dve.tensor_tensor(heads_t[u * P // 2:(u + 1) * P // 2, :], cbank[0:P // 2, u * S:(u + 1) * S],
                                          inv_sum[:, u * S:(u + 1) * S], ALU.mult).then_inc(heads_ready, 1)

                def attention_sum(n):
                    layer, b = n // LANES, n % LANES
                    dve.wait_ge(attn_out, n + 1)
                    src = x[b]
                    if layer != 1:
                        dve.wait_ge(res_ready, n + 1 if n < LANES else n + 1 - LANES)
                        src = x_res
                    dve.scalar_tensor_tensor(out=x[b][:, :, :].rearrange("p t n -> p (t n)"), in0=cbank[:, 0:S],
                                             scalar=tanh_g[:, layer:layer + 1],
                                             in1=src[:, :, :].rearrange("p t n -> p (t n)"),
                                             op0=ALU.mult, op1=ALU.add).then_inc(x_new[b], 1)

                def bc(ap):
                    return ap.unsqueeze(2).broadcast_to([P, TT, EXPERTS])

                def read_logits(n):
                    layer = n // LANES
                    dve.wait_ge(logits_psum, n + 1)
                    src = ybank[:, S:S + TT * EXPERTS].rearrange("p (t e) -> p t e", t=TT)
                    if layer == 3:
                        b3 = route_bias[3][:, :].unsqueeze(1).broadcast_to([P, TT, EXPERTS])
                        i = dve.tensor_tensor(logit[:, :, :], src, b3, ALU.add)
                    else:
                        i = dve.tensor_copy(logit[:, :, :], src)
                    i.then_inc(gate_step, 1)
                    dve.wait_ge(gate_step, n + 1)
                    dve.tensor_reduce(logit_max[:, :], logit[:, :, :], AX, ALU.max).then_inc(gate_max, 1)
                    dve.wait_ge(gate_max, n + 1)
                    dve.tensor_tensor(shifted[:, :, :], logit[:, :, :], bc(logit_max[:, :]), ALU.subtract)\
                       .then_inc(gate_shifted, 1)

                def make_gates(n):
                    layer = n // LANES
                    steps = [sum(GATE_LINKS[m // LANES] for m in range(n))]

                    def done(i):
                        i.then_inc(gate_chain, 1)
                        steps[0] += 1
                        dve.wait_ge(gate_chain, steps[0])

                    dve.wait_ge(exp_l_done, n + 1)
                    done(dve.tensor_reduce(exp_sum[:, :], exp_l[:, :, :], AX, ALU.add))
                    done(dve.reciprocal(exp_inv[:, :], exp_sum[:, :]))
                    done(dve.tensor_tensor(prob[:, :, :], exp_l[:, :, :], bc(exp_inv[:, :]), ALU.mult))
                    if layer == 2:
                        b2 = route_bias[2][:, :].unsqueeze(1).broadcast_to([P, TT, EXPERTS])
                        done(dve.tensor_tensor(choice[:, :, :], prob[:, :, :], b2, ALU.add))
                    key = choice if layer == 2 else prob
                    dve.max(top8[:, 0, :], key[:, 0, :])
                    done(dve.max(top8[:, 1, :], key[:, 1, :]))
                    dve.max_index(top_idx[:, 0, :], top8[:, 0, :], key[:, 0, :])
                    done(dve.max_index(top_idx[:, 1, :], top8[:, 1, :], key[:, 1, :]))
                    done(dve.tensor_copy(top_f[:, :, :], top_idx[:, :, :]))
                    i8 = iota8[:, :].unsqueeze(1).broadcast_to([P, TT, EXPERTS])
                    if layer == 3:
                        done(dve.tensor_tensor(picked[:, :, :], i8, bc(top_f[:, :, 0]), ALU.is_equal))
                    else:
                        dve.tensor_tensor(pick1[:, :, :], i8, bc(top_f[:, :, 0]), ALU.is_equal)
                        done(dve.tensor_tensor(pick2[:, :, :], i8, bc(top_f[:, :, 1]), ALU.is_equal))
                        done(dve.tensor_tensor(picked[:, :, :], pick1[:, :, :], pick2[:, :, :], ALU.add))
                    gate = gate_pad[:, :, 0:EXPERTS]
                    if layer >= 2:
                        done(dve.tensor_tensor(gate, picked[:, :, :], prob[:, :, :], ALU.mult))
                    else:
                        done(dve.tensor_tensor(gate_raw[:, :, :], picked[:, :, :], prob[:, :, :], ALU.mult))
                        done(dve.tensor_reduce(gate_sum[:, :], gate_raw[:, :, :], AX, ALU.add))
                        done(dve.reciprocal(gate_inv[:, :], gate_sum[:, :]))
                        done(dve.tensor_tensor(gate, gate_raw[:, :, :], bc(gate_inv[:, :]), ALU.mult))
                    dve.tensor_scalar(gate_use[:, :, :], gate, 0.5 if layer in (1, 2) else 1.0, None, ALU.mult)\
                       .then_inc(gate_ready, 1)
                    assert steps[0] == sum(GATE_LINKS[m // LANES] for m in range(n + 1))

                def gelu_inner(n, e):
                    for u in range(2):
                        dve.wait_ge(sq_ready, 2 * (EXPERTS * (n - LANES) + e) + u + 1)
                        dve.scalar_tensor_tensor(out=gelu_t[:, u, :, :], in0=gelu_t[:, u, :, :], scalar=1.0 / GELU_A,
                                                 in1=pre_act[:, u, :, :], op0=ALU.add, op1=ALU.mult)\
                           .then_inc(inner_ready, 1)

                def gelu_out(n, e):
                    done = experts_before(n) + e
                    for u in range(2):
                        dve.wait_ge(tanh_ready, 2 * (EXPERTS * (n - LANES) + e) + u + 1)
                        dve.wait_ge(y_psum, done - 1)
                        dve.scalar_tensor_tensor(out=hidden[:, done % 2, 2 * u:2 * u + 2, :], in0=gelu_t[:, u, :, :],
                                                 scalar=1.0, in1=pre_act[:, u, :, :], op0=ALU.add, op1=ALU.mult)\
                           .then_inc(hid_ready, 1)

                def glu_hidden(n, e):
                    done = experts_before(n) + e
                    dve.wait_ge(glu_tanh, done - experts_before(2 * LANES) + 1)
                    dve.scalar_tensor_tensor(out=gelu_t[:, 0, 0, :], in0=pre_act[:, 0, 0, :], scalar=1.0,
                                             in1=hbank[:, 0, 0:S], op0=ALU.add, op1=ALU.mult).then_inc(hid_ready, 1)
                    dve.wait_ge(hid_ready, 2 * done + 1)
                    dve.wait_ge(up_psum, 2 * done + 2)
                    dve.wait_ge(y_psum, done - 1)
                    dve.tensor_tensor(hidden[:, done % 2, 0, :], hbank[:, 1, 0:S], gelu_t[:, 0, 0, :], ALU.mult)\
                       .then_inc(hid_ready, 1)

                def add_expert(n, e):
                    layer, done = n // LANES, experts_before(n) + e
                    dve.wait_ge(y_psum, done + 1)
                    if e == 0:
                        dve.wait_ge(gate_ready, n + 1)
                    else:
                        dve.wait_ge(y_acc, done)
                    for t in range(TT):
                        o, y = acc[:, t, :], ybank[:, t * D:(t + 1) * D]
                        g = 0.5 if e == EXPERTS else gate_use[:, t, e:e + 1]
                        if e == 0:
                            last = dve.tensor_scalar(o, y, g, None, ALU.mult)
                        else:
                            last = dve.scalar_tensor_tensor(out=o, in0=y, scalar=g, in1=o, op0=ALU.mult, op1=ALU.add)
                    last.then_inc(y_acc, 1)

                def add_output_bias(n):
                    k = biased(n) + 1
                    dve.wait_ge(bias_psum, k)
                    dve.wait_ge(y_acc, experts_before(n + 1))
                    dve.tensor_tensor(acc[:, :, :].rearrange("p t n -> p (t n)"), ybank[:, 0:S],
                                      acc[:, :, :].rearrange("p t n -> p (t n)"), ALU.add).then_inc(bias_added, 1)
                    dve.wait_ge(bias_added, k)

                def expert_sum(n):
                    layer, b = n // LANES, n % LANES
                    dve.wait_ge(y_acc, experts_before(n + 1))
                    dve.scalar_tensor_tensor(out=x[b][:, :, :], in0=acc[:, :, :],
                                             scalar=tanh_g[:, LAYERS + layer:LAYERS + layer + 1], in1=x[b][:, :, :],
                                             op0=ALU.mult, op1=ALU.add).then_inc(x_new[b], 1)

                statistics(an, 0, 0)
                normalise(an, 0)
                low_part(0, "k", k_hi, k_lo, smax[:, 1, 0:S])
                take_v(0)
                low_part(0, "q", q_hi, q_lo, smax[:, 0, S:2 * S])
                copy_k_stack(0)
                for slot in range(PHASES + LAG):
                    a, f, nxt, prev = phases(slot)
                    fl = f // LANES if f is not None else None
                    if f is not None:
                        turned_low_part(f)
                    if a is not None:
                        reduce_max(a, 0)
                    if f is not None:
                        read_logits(f)
                    if fl == 1:
                        gelu_inner(f, 0)
                    if prev is not None:
                        heads_out(prev)
                    if fl == 1:
                        gelu_out(f, 0)
                    if fl == 2:
                        glu_hidden(f, 0)
                    for s in range(STEPS + 3):
                        more = f is not None and s + 1 < experts(fl)
                        if a is not None and s < STEPS:
                            if s:
                                reduce_max(a, s)
                            if s % 2:
                                split_max(a, s // 2)
                        if more and fl == 1:
                            gelu_inner(f, s + 1)
                        if a is not None and s < STEPS and s % 2:
                            add_max(a, s // 2)
                        if more and fl == 2:
                            glu_hidden(f, s + 1)
                        if s == 0 and f is not None:
                            make_gates(f)
                        if s == 1 and prev is not None:
                            attention_sum(prev)
                        if f is not None and s < experts(fl):
                            add_expert(f, s)
                        if more and fl == 1:
                            gelu_out(f, s + 1)
                        if f is not None and s == EXPERTS:
                            if fl in (1, 3):
                                add_output_bias(f)
                            expert_sum(f)
                        if s == 5 and nxt is not None:
                            statistics(an, nxt, 0)
                        if s == 5 and prev is not None:
                            statistics(fn, prev, 1)
                        if s == 6 and nxt is not None:
                            normalise(an, nxt)
                        if s == 6 and prev is not None:
                            normalise(fn, prev)
                        if nxt is not None:
                            if s == STEPS:
                                low_part(nxt, "k", k_hi, k_lo, smax[:, 1, 0:S])
                                take_v(nxt)
                            if s == STEPS + 1:
                                low_part(nxt, "q", q_hi, q_lo, smax[:, 0, S:2 * S])
                            if s == STEPS + 2:
                                copy_k_stack(nxt)


def _layers_of(inputs):
    import numpy as _np

    def a(name):
        return _np.asarray(inputs[name])

    def t(name):
        return a(name).T

    m0, m1 = a("mask_BxSxS2_ik1"), a("mask_Bx1xSxS2_ik0")[:, 0]
    return {
        "x": a("x"),
        "ctx_t": a("ctx_1024").transpose(0, 2, 1),
        "mask00": m0, "mask01": m0.transpose(0, 2, 1),
        "mask10": m1, "mask11": m1.transpose(0, 2, 1),
        "gates": _np.concatenate([a("g_xattn"), a("g_ffn")]),
        "wq": _np.stack([t("L0_xattn_Wq"), t("L1_xattn_w_q"), t("L2_xattn_Wq"), t("L3_xattn_wq")]),
        "wk": _np.stack([t("L0_xattn_Wk"), t("L1_xattn_w_k"), t("L2_xattn_Wk"), t("L3_xattn_wk")]),
        "wv": _np.stack([t("L0_xattn_Wv"), t("L1_xattn_w_v"), t("L2_xattn_Wv"), t("L3_xattn_wv")]),
        "wo": _np.stack([t("L0_xattn_Wo"), t("L1_xattn_w_o"), t("L2_xattn_Wo"), t("L3_xattn_wo")]),
        "bq0": a("L0_xattn_bq"), "bk0": a("L0_xattn_bk"), "bv0": a("L0_xattn_bv"), "bo0": a("L0_xattn_bo"),
        "bq3": a("L3_xattn_bq"), "bk3": a("L3_xattn_bk"), "bv3": a("L3_xattn_bv"), "bo3": a("L3_xattn_bo"),
        "bo2": a("L2_xattn_bo"), "time_decay": a("L3_xattn_time_decay").reshape(1),
        "router": _np.stack([a("L0_ffn_Wr"), t("L1_ffn_router_w"), a("L2_ffn_router_w"), a("L3_ffn_Wr")]),
        "route_bias2": a("L2_ffn_expert_bias"), "route_bias3": a("L3_ffn_br"),
        "up_w0": a("L0_ffn_W1"), "down_w0": a("L0_ffn_W2"),
        "up_w1": a("L1_ffn_w_fc"), "down_w1": a("L1_ffn_w_proj"),
        "up_w3": a("L3_ffn_W1"), "down_w3": a("L3_ffn_W2"),
        "hid_bias1": a("L1_ffn_b_fc").reshape(EXPERTS * CH, P).T, "out_bias1": a("L1_ffn_b_proj"),
        "hid_bias3": a("L3_ffn_b1").reshape(EXPERTS * CH, P).T, "out_bias3": a("L3_ffn_b2"),
        "glu_w1": a("L2_ffn_w1"), "glu_w2": a("L2_ffn_w2"), "glu_w3": a("L2_ffn_w3"),
        "sglu_w1": a("L2_ffn_sw1"), "sglu_w2": a("L2_ffn_sw2"), "sglu_w3": a("L2_ffn_sw3"),
    }


def kernel(**inputs):
    import numpy as _np
    import concourse.bacc as _bacc
    from concourse import mybir as _mybir
    from concourse.bass_utils import run_bass_kernel_spmd as _run

    nc = _bacc.Bacc("TRN2", target_bir_lowering=False, num_devices=1)
    arrays, ins = {}, {}
    for name, value in _layers_of(inputs).items():
        value = _np.ascontiguousarray(value)
        arrays[f"in_{name}"] = value
        ins[name] = nc.dram_tensor(f"in_{name}", value.shape, _mybir.dt.from_np(value.dtype), kind="ExternalInput").ap()
    out = nc.dram_tensor("out_0", (BATCH, S, D), F32, kind="ExternalOutput").ap()
    flamingo_layers(nc, ins, out)
    r = _run(nc, [arrays], core_ids=[0])
    return r.results[0]["out_0"]
```

```python
import concourse.bass as bass
from concourse import mybir
from contextlib import ExitStack

F32 = mybir.dt.float32
F32R = mybir.dt.float32r
BF16 = mybir.dt.bfloat16
I32 = mybir.dt.int32
U32 = mybir.dt.uint32
ALU = mybir.AluOpType
ACT = mybir.ActivationFunctionType
AX = mybir.AxisListType.X

P = 128
LAYERS, BATCH, S, D = 4, 4, 256, 128
LANES = BATCH
LAG = 2
TT = S // P
HEADS, DK = 16, 8
GROUPS, GH = 4, 4
STEPS = HEADS // 2
SLOT_STEPS = STEPS + 2
EXPERTS, FF = 8, 512
CH = FF // P
PHASES = LAYERS * LANES
BIG = float(2 ** 100)
EPS = 1e-5
WINDOW = 4
RIM = 32
BAND = P + RIM
GELU_A = 0.044715
GELU_C = 0.7978845608028654
GATE_LINKS = (12, 12, 10, 8)
CHOICE_LINKS = (6, 6, 7, 6)
UP_LAYERS = (0, 1, 3)
PROBS = 3
UP_RING = 2
VC = 1 + 3 * DK
HH = HEADS // 2


def window(layer, tile):
    return (tile * (S - BAND), BAND) if layer == 2 else (0, S)


def experts(layer):
    return EXPERTS + 1 if layer == 2 else EXPERTS


def experts_before(n):
    return sum(experts(m // LANES) for m in range(n))


def split_phases(n):
    return sum(m // LANES in UP_LAYERS for m in range(n))


def flamingo_layers(nc, ins, out):
    ctx = ExitStack()
    with ctx:
        def sb(name, shape, dt=F32):
            return ctx.enter_context(nc.sbuf_tensor(name, shape, dt))

        def pb(name, shape, dt=F32):
            return ctx.enter_context(nc.psum_tensor(name, shape, dt))

        def sem(name):
            return ctx.enter_context(nc.semaphore(name))

        wq = sb("wq", [P, LAYERS, D])
        wk = sb("wk", [P, LAYERS, D])
        wv = sb("wv", [P, LAYERS, D])
        wo = sb("wo", [P, LAYERS, D])
        up_hi = sb("up_hi", [P, EXPERTS, FF], F32R)
        up_lo = sb("up_lo", [P, EXPERTS, FF], F32R)
        up_in = sb("up_in", [P, UP_RING, FF])
        down_a, down_b = sb("down_a", [P, EXPERTS, CH, D]), sb("down_b", [P, EXPERTS, CH, D])
        down_w = {0: down_a, 1: down_b, 3: down_a}
        glu_w1 = sb("glu_w1", [P, EXPERTS + 1, D])
        glu_w3 = sb("glu_w3", [P, EXPERTS + 1, D])
        glu_w2 = sb("glu_w2", [P, EXPERTS + 1, D])
        router = sb("router", [P, LAYERS, EXPERTS])
        col_bias = {n: sb(n, [P, 1]) for n in ("bq0", "bk0", "bq3", "bk3")}
        bv = {l: sb(f"bv{l}", [P, D]) for l in (0, 3)}
        bo = {l: sb(f"bo{l}", [P, D]) for l in (0, 2, 3)}
        hid_bias = {l: sb(f"hid_bias{l}", [P, EXPERTS, CH]) for l in (1, 3)}
        out_bias = {l: sb(f"out_bias{l}", [P, D]) for l in (1, 3)}
        route_bias = {l: sb(f"route_bias{l}", [P, EXPERTS]) for l in (2, 3)}
        gates = sb("gates", [P, 2 * LAYERS])
        tanh_g = sb("tanh_g", [P, 2 * LAYERS])
        time_decay = sb("time_decay", [P, 1])

        ident = sb("ident", [P, P])
        ident_r = sb("ident_r", [P, P], F32R)
        ident_b = sb("ident_b", [P, P], BF16)
        spread_two = {"q": sb("spread_q_high", [P, GROUPS, P], F32R), "k": sb("spread_k_high", [P, GROUPS, P], F32R)}
        spread_one = {"q": sb("spread_q_low", [P, GROUPS, P], F32R), "k": sb("spread_k_low", [P, GROUPS, P], F32R)}
        ones_rows = sb("ones_rows", [P, 1])
        minus_half = sb("minus_half", [P, TT])
        iota8 = sb("iota8", [P, EXPERTS])
        decay = sb("decay", [P, TT, S])
        decay_hi = sb("decay_hi", [P, TT, S], F32R)
        decay_lo = sb("decay_lo", [P, TT, S], F32R)
        band = sb("band", [P, TT, BAND], BF16)

        x = [sb(f"x{b}", [P, TT, D]) for b in range(LANES)]
        ctx_t = [sb(f"ctx_t{b}", [P, S]) for b in range(LANES)]
        mask = [[sb(f"mask{b}{o}", [P, TT, S], BF16) for o in range(2)] for b in range(LANES)]

        q_stack = sb("q_stack", [P, GROUPS, S], F32R)
        k_stack = sb("k_stack", [P, 2, GROUPS, S], F32R)
        qm_stack = sb("qm_stack", [P, 2, S], F32R)
        qkv_hi = {n: sb(f"{n}_hi", [P, S], F32R)[:, :] for n in "qk"}
        qkv_lo = {n: sb(f"{n}_lo", [P, S], F32R)[:, :] for n in "qk"}
        v_tmp = sb("v_tmp", [P, TT, D])
        v_cols = sb("v_cols", [P, 2, TT, HEADS, VC], BF16)
        row_max = sb("row_max", [P, HEADS, TT])
        max_parts = sb("max_parts", [P, TT, GH, 32], F32R)
        probs = sb("probs", [P, PROBS, 2, TT, S])
        rest = sb("rest", [P, 2, 2, TT, S])
        low = sb("low", [P, 2, 2, TT, S], BF16)
        sums = sb("sums", [P, 2, TT * HH, VC])
        part_sum = sb("part_sum", [P, TT * HH, DK])
        inv_sum = sb("inv_sum", [P, TT * HH])
        heads_tok = sb("heads_tok", [P, TT, D])
        heads_t = sb("heads_t", [P, S])[:, :]
        x_res = sb("x_res", [P, TT, D])

        normed_hi, normed_lo = sb("normed_hi", [P, S], F32R), sb("normed_lo", [P, S], F32R)
        hidden = sb("hidden", [P, 2, CH, S])
        iota_i = hidden[:, 0, 0:TT, :].bitcast(I32)
        dist, dist_neg = hidden[:, 0, TT:2 * TT, :], hidden[:, 1, 0:TT, :]
        pre_act = sb("pre_act", [P, 2, 2, S])
        gelu_t = sb("gelu_t", [P, 2, 2, S])
        acc = sb("acc", [P, TT, D])
        logit = sb("logit", [P, TT, EXPERTS])
        logit_max = sb("logit_max", [P, TT])
        shifted = sb("shifted", [P, TT, EXPERTS])
        exp_l = sb("exp_l", [P, TT, EXPERTS])
        exp_sum = sb("exp_sum", [P, TT])
        exp_inv = sb("exp_inv", [P, TT])
        prob = sb("prob", [P, TT, EXPERTS])
        choice = sb("choice", [P, TT, EXPERTS])
        top8 = sb("top8", [P, TT, 8])
        top_idx = sb("top_idx", [P, TT, 8], U32)
        top_f = sb("top_f", [P, TT, 8])
        pick1 = sb("pick1", [P, TT, EXPERTS])
        pick2 = sb("pick2", [P, TT, EXPERTS])
        picked = sb("picked", [P, TT, EXPERTS])
        gate_raw = sb("gate_raw", [P, TT, EXPERTS])
        gate_sum = sb("gate_sum", [P, TT])
        gate_inv = sb("gate_inv", [P, TT])
        gate_pad = sb("gate_pad", [P, TT, P])
        gate_use = sb("gate_use", [P, TT, EXPERTS])
        gate_t = gelu_t[:, 0, 0, :]
        mask_in = [pre_act[:, i, :, :].bitcast(I32) for i in range(2)]

        smax = pb("smax", [P, 2, 512])
        sexp = pb("sexp", [P, 2, 512])
        cbank = pb("cbank", [P, 512])
        ybank = pb("ybank", [P, 512])
        hbank = pb("hbank", [P, 2, 512])

        w_attn, w_out, w_first, w_small = sem("w_attn"), sem("w_out"), sem("w_first"), sem("w_small")
        w_glu = sem("w_glu")
        up_loaded = [sem(f"up_loaded{i}") for i in range(UP_RING)]
        up_rounded, up_split = sem("up_rounded"), sem("up_split")
        w_down = {l: sem(f"w_down{l}") for l in range(LAYERS)}
        zeroed, ident_made, spread_made, const_made = sem("zeroed"), sem("ident_made"), sem("spread_made"), sem("const_made")
        iota_made, dist_made, decay_made, tanh_made, v_set = (
            sem("iota_made"), sem("dist_made"), sem("decay_made"), sem("tanh_made"), sem("v_set"))

        class Norm:

            def __init__(self, tag):
                self.stats = sb(f"{tag}_stats", [P, TT, 6])
                self.mean_var = sb(f"{tag}_mean_var", [P, TT, 2])
                self.var_eps = sb(f"{tag}_var_eps", [P, TT])
                self.rstd = sb(f"{tag}_rstd", [P, TT])
                self.normed = sb(f"{tag}_normed", [P, TT, D])
                self.normed_t = sb(f"{tag}_normed_t", [P, S])
                self.stats_done = sem(f"{tag}_stats_done")
                self.aggr_done = sem(f"{tag}_aggr_done")
                self.eps_added = sem(f"{tag}_eps_added")
                self.rstd_done = sem(f"{tag}_rstd_done")
                self.normed_done = sem(f"{tag}_normed_done")
                self.turned = sem(f"{tag}_turned")
                self.turned_sb = sem(f"{tag}_turned_sb")

        an, fn = Norm("attn"), Norm("ffn")
        x_loaded = [sem(f"x_loaded{b}") for b in range(LANES)]
        ctx_loaded = [sem(f"ctx_loaded{b}") for b in range(LANES)]
        x_new = [sem(f"x_new{b}") for b in range(LANES)]
        mask_loaded = [sem("mask_loaded0"), sem("mask_loaded1")]
        mask_made, stored = sem("mask_made"), sem("stored")
        k_proj, v_proj, q_proj = sem("k_proj"), sem("v_proj"), sem("q_proj")
        k_hi, k_lo, q_hi, q_lo, v_ready = sem("k_hi_s"), sem("k_lo_s"), sem("q_hi_s"), sem("q_lo_s"), sem("v_ready")
        k_spread, q_spread, k_ready, q_ready = sem("k_spread"), sem("q_spread"), sem("k_ready"), sem("q_ready")
        max_psum, max_red, max_hi, max_lo = sem("max_psum"), sem("max_red"), sem("max_hi"), sem("max_lo")
        max_turned, qm_ready, exp_psum, exp_done, pv_done = (
            sem("max_turned"), sem("qm_ready"), sem("exp_psum"), sem("exp_done"), sem("pv_done"))
        heads_ready, attn_out, res_ready = sem("heads_ready"), sem("attn_out"), sem("res_ready")
        rest_ready, rest_half_ready = sem("rest_ready"), sem("rest_half_ready")
        low_ready, sums_copied = sem("low_ready"), sem("sums_copied")
        heads_chain, heads_made, heads_turned, v_chain = (
            sem("heads_chain"), sem("heads_made"), sem("heads_turned"), sem("v_chain"))
        logits_psum, gate_step, gate_max, gate_shifted = (
            sem("logits_psum"), sem("gate_step"), sem("gate_max"), sem("gate_shifted"))
        exp_l_done, gate_chain, gate_ready = sem("exp_l_done"), sem("gate_chain"), sem("gate_ready")
        up_psum, hid_ready, y_psum, y_acc = sem("up_psum"), sem("hid_ready"), sem("y_psum"), sem("y_acc")
        pre_ready, inner_ready, tanh_ready = sem("pre_ready"), sem("inner_ready"), sem("tanh_ready")
        glu_tanh = sem("glu_tanh")
        gate_turned, gate_t_ready, bias_psum, bias_added = (
            sem("gate_turned"), sem("gate_t_ready"), sem("bias_psum"), sem("bias_added"))
        q_scaled, bo_scaled = sem("q_scaled"), sem("bo_scaled")
        v_placed, turned_hi, turned_lo = sem("v_placed"), sem("turned_hi"), sem("turned_lo")

        def upper(ap):
            return ap.bitcast(BF16).rearrange("p (n two) -> p n two", two=2)[:, :, 1]

        def score_bias(eng_mm, bank, lane, layer):
            if layer == 3:
                eng_mm(bank, ident_r[:, :], decay_hi[:, :, :].rearrange("p t n -> p (t n)"), start=True, stop=False,
                       skip_group_check=True)
                eng_mm(bank, ident_r[:, :], decay_lo[:, :, :].rearrange("p t n -> p (t n)"), start=False, stop=False,
                       skip_group_check=True)
            elif layer == 2:
                for t in range(TT):
                    lo, w = window(layer, t)
                    eng_mm(bank[:, t * S + lo:t * S + lo + w], ident_b[:, :], band[:, t, :],
                           start=(t == 0), stop=False, skip_group_check=True)
            else:
                m = mask[lane][1]
                eng_mm(bank, ident_b[:, :], m[:, :, :].rearrange("p t n -> p (t n)"), start=True, stop=False,
                       skip_group_check=True)

        first = [(col_bias[n][:, :], ins[n].rearrange("(p a) -> p a", a=1)) for n in ("bq0", "bk0")]
        first.append((bv[0][:, :], ins["bv0"].partition_broadcast(P)))
        small = [
            (gates[:, :], ins["gates"].partition_broadcast(P)),
            (router[:, :, :], ins["router"].rearrange("l p e -> p l e")),
            (time_decay[:, :], ins["time_decay"].partition_broadcast(P)),
        ]
        for l in (0, 2, 3):
            small.append((bo[l][:, :], ins[f"bo{l}"].partition_broadcast(P)))
        for n in ("bq3", "bk3"):
            small.append((col_bias[n][:, :], ins[n].rearrange("(p a) -> p a", a=1)))
        small.append((bv[3][:, :], ins["bv3"].partition_broadcast(P)))
        for l in (2, 3):
            small.append((route_bias[l][:, :], ins[f"route_bias{l}"].partition_broadcast(P)))
        for l in (1, 3):
            small.append((hid_bias[l][:, :, :], ins[f"hid_bias{l}"].rearrange("p (e c) -> p e c", c=CH)))
            small.append((out_bias[l][0:EXPERTS, :], ins[f"out_bias{l}"]))
        FIRST, SMALL = 16 * len(first), 16 * len(small)

        def x_ready(n, kind):
            return (x_loaded[n % LANES], 16) if n < LANES and kind == 0 else (x_new[n % LANES], 2 * (n // LANES) + kind)

        def masks_for(n):
            return 2 * (n + 1)

        splits = {}
        for i, (slot, s) in enumerate(((0, 2), (LANES + LAG - 1, 2), (2 * LANES + LAG, 1))):
            for e in range(EXPERTS):
                splits[slot + (s + e) // SLOT_STEPS, (s + e) % SLOT_STEPS] = EXPERTS * i + e

        def each_window(n, s, heads, op):
            k = STEPS * n + s
            if n // LANES != 2:
                j = slice(heads[0], heads[-1] + 1)
                return op(lambda x: x[:, k % (PROBS if x is probs else 2), j, :, :].rearrange("p j t n -> p (j t n)"))
            for j in heads:
                for t in range(TT):
                    last = op(lambda x: x[:, k % (PROBS if x is probs else 2), j, t, 0:BAND])
            return last

        def biased(n):
            return sum(m // LANES in (1, 3) for m in range(n))

        def phases(slot):
            a = slot if slot < PHASES else None
            f = slot - LAG if slot >= LAG else None
            nxt = slot + 1 if slot + 1 < PHASES else None
            prev = slot - 1 if 1 <= slot <= PHASES else None
            return a, f, nxt, prev

        with nc.Block(no_gpsimd_drain=True) as block:
            @block.sync
            def _(sp):
                def load_mask(i):
                    m, b, o = i // (2 * LANES), i // 2 % LANES, i % 2
                    if i >= 2:
                        sp.wait_ge(mask_made, i - 1)
                    sp.dma_start(mask_in[i % 2], ins[f"mask{m}{o}"][b].rearrange("(t p) n -> p t n", p=P))\
                      .then_inc(mask_loaded[i % 2], 16)

                def load_up(j):
                    if j >= UP_RING:
                        sp.wait_ge(up_split, j - UP_RING + 1)
                    sp.dma_start(up_in[:, j % UP_RING, :], ins[f"up_w{UP_LAYERS[j // EXPERTS]}"][j % EXPERTS])\
                      .then_inc(up_loaded[j % UP_RING], 16)

                def load_down(l):
                    sp.dma_start(down_w[l][:, :, :, :], ins[f"down_w{l}"].rearrange("e (c p) n -> p e c n", p=P))\
                      .then_inc(w_down[l], 16)

                def load_lane(b):
                    sp.dma_start(x[b][:, :, :], ins["x"][b].rearrange("(t p) n -> p t n", p=P)).then_inc(x_loaded[b], 16)
                    sp.dma_start(ctx_t[b][:, :], ins["ctx_t"][b]).then_inc(ctx_loaded[b], 16)

                load_lane(0)
                for w, name in ((wk, "wk"), (wv, "wv"), (wq, "wq")):
                    sp.dma_start(w[:, :, :], ins[name].rearrange("l p n -> p l n")).then_inc(w_attn, 16)
                for dst, src in first:
                    sp.dma_start(dst, src).then_inc(w_first, 16)
                for i in range(2):
                    load_mask(i)
                sp.dma_start(wo[:, :, :], ins["wo"].rearrange("l p n -> p l n")).then_inc(w_out, 16)
                sp.wait_ge(zeroed, 2)
                for dst, src in small:
                    sp.dma_start(dst, src).then_inc(w_small, 16)
                for b in range(1, LANES):
                    load_lane(b)
                for i in range(2, 2 * LANES):
                    load_mask(i)
                for j in range(UP_RING):
                    load_up(j)
                load_down(0)
                for j in range(UP_RING, EXPERTS):
                    load_up(j)
                load_down(1)
                for w, name in ((glu_w1, "glu_w1"), (glu_w3, "glu_w3")):
                    sp.dma_start(w[:, 0:EXPERTS, :], ins[name].rearrange("e p n -> p e n")).then_inc(w_glu, 16)
                    sp.dma_start(w[:, EXPERTS, :], ins["s" + name]).then_inc(w_glu, 16)
                sp.dma_start(glu_w2[:, 0:EXPERTS, :], ins["glu_w2"].rearrange("e p n -> p e n")).then_inc(w_down[2], 16)
                sp.dma_start(glu_w2[:, EXPERTS, :], ins["sglu_w2"]).then_inc(w_down[2], 16)
                for i in range(2 * LANES, 4 * LANES):
                    load_mask(i)
                for j in range(EXPERTS, 2 * EXPERTS + UP_RING):
                    load_up(j)
                sp.wait_ge(y_psum, experts_before(LANES))
                load_down(3)
                for j in range(2 * EXPERTS + UP_RING, 3 * EXPERTS):
                    load_up(j)
                for b in range(LANES):
                    sp.wait_ge(x_new[b], 2 * LAYERS)
                    sp.dma_start(out[b].rearrange("(t p) n -> p t n", p=P), x[b][:, :, :]).then_inc(stored, 16)
                sp.wait_ge(stored, 16 * LANES)

            @block.gpsimd
            def _(pool):
                def make_masks(n):
                    b = n % LANES
                    if n >= LANES:
                        pool.wait_ge(max_red, STEPS * (b + 1))
                        pool.wait_ge(exp_psum, STEPS * (b + 1))
                    for o in range(2):
                        i = 2 * n + o
                        pool.wait_ge(mask_loaded[i % 2], 16 * (i // 2 + 1))
                        if n >= LANES:
                            pool.wait_ge(mask_made, 2 * b + o + 1)
                        pool.tensor_scalar(mask[b][o][:, :, :], mask_in[i % 2], 0.0, -BIG,
                                           ALU.is_equal, ALU.mult).then_inc(mask_made, 1)

                def rstd(ln, n):
                    pool.wait_ge(ln.aggr_done, TT * (n + 1))
                    pool.tensor_scalar(ln.var_eps[:, :], ln.mean_var[:, :, 1], EPS, None, ALU.add)\
                        .then_inc(ln.eps_added, 1)
                    pool.wait_ge(ln.eps_added, n + 1)
                    pool.tensor_tensor(ln.rstd[:, :], ln.var_eps[:, :], minus_half[:, :], ALU.pow)\
                        .then_inc(ln.rstd_done, 1)

                def residual_with_bias(n):
                    layer, b = n // LANES, n % LANES
                    if layer == 1:
                        return
                    pool.wait_ge(*x_ready(n, 0))
                    if n:
                        pool.wait_ge(x_new[(n - 1) % LANES], 2 * ((n - 1) // LANES) + 1)
                    for t in range(TT):
                        last = pool.tensor_tensor(x_res[:, t, :], x[b][:, t, :], bo[layer][:, :], ALU.add)
                    last.then_inc(res_ready, 1)

                def place_v(n):
                    pool.wait_ge(v_ready, n + 1)
                    if n >= 2:
                        pool.wait_ge(pv_done, STEPS * (n - 1))
                    src = v_tmp[:, :, :].rearrange("p t (h d) -> p (t h) d", d=DK)
                    cols = v_cols[:, n % 2, :, :, :].rearrange("p t h c -> p (t h) c")
                    parts = [cols[:, :, 1 + i * DK:1 + (i + 1) * DK] for i in range(3)]
                    pool.tensor_copy(parts[0], src).then_inc(v_chain, 1)
                    pool.wait_ge(v_chain, 3 * n + 1)
                    pool.tensor_tensor(src, src, parts[0], ALU.subtract).then_inc(v_chain, 1)
                    pool.wait_ge(v_chain, 3 * n + 2)
                    pool.tensor_copy(parts[1], src).then_inc(v_chain, 1)
                    pool.wait_ge(v_chain, 3 * n + 3)
                    pool.tensor_tensor(parts[2], src, parts[1], ALU.subtract).then_inc(v_placed, 1)

                def rest_probs(n, s):
                    k = STEPS * n + s
                    pool.wait_ge(exp_done, k + 1)
                    if k >= 2:
                        pool.wait_ge(pv_done, k - 1)
                    last = each_window(n, s, (1,), lambda o: pool.tensor_tensor(o(rest), o(probs), upper(o(probs)),
                                                                                ALU.subtract))
                    last.then_inc(rest_half_ready, 1)

                def low_probs(n, s):
                    k = STEPS * n + s
                    pool.wait_ge(rest_ready, k + 1)
                    pool.wait_ge(rest_half_ready, k + 1)
                    if k >= 2:
                        pool.wait_ge(pv_done, k - 1)
                    last = each_window(n, s, (0, 1), lambda o: pool.tensor_tensor(o(low), o(rest), upper(o(rest)), ALU.subtract))
                    last.then_inc(low_ready, 1)

                pool.memset(ident[:, :], 1.0).then_inc(ident_made, 1)
                pool.memset(minus_half[:, :], -0.5).then_inc(const_made, 1)
                pool.wait_ge(ident_made, 1)
                pool.affine_select(out=ident[:, :], in_=ident[:, :], compare_op=ALU.is_equal, fill=0.0, base=0,
                                   pattern=[[-1, P]], channel_multiplier=1).then_inc(ident_made, 1)
                for l in (1, 3):
                    pool.memset(out_bias[l][:, :], 0.0).then_inc(zeroed, 1)
                pool.wait_ge(ident_made, 2)
                pool.tensor_copy(ident_r[:, :], ident[:, :]).then_inc(ident_made, 1)
                pool.wait_ge(w_attn, 48)
                pool.tensor_scalar(wq[:, 0, :], wq[:, 0, :], DK ** -0.5, None, ALU.mult).then_inc(q_scaled, 1)
                pool.wait_ge(w_first, FIRST)
                pool.tensor_scalar(col_bias["bq0"][:, :], col_bias["bq0"][:, :], DK ** -0.5, None, ALU.mult)\
                    .then_inc(q_scaled, 1)
                pool.wait_ge(const_made, 1)
                rstd(an, 0)
                make_masks(0)
                pool.tensor_copy(ident_b[:, :], ident[:, :]).then_inc(ident_made, 1)
                place_v(0)
                for e in range(EXPERTS):
                    pool.memset(iota8[:, e:e + 1], float(e)).then_inc(const_made, 1)
                pool.memset(gate_pad[:, :, :], 0.0).then_inc(const_made, 1)
                pool.iota(iota_i, [[P, TT], [-1, S]], base=0, channel_multiplier=1).then_inc(iota_made, 1)
                for slot in range(PHASES + LAG):
                    a, f, nxt, prev = phases(slot)
                    for s in range(SLOT_STEPS):
                        if prev is not None and s == 0:
                            rest_probs(prev, STEPS - 1)
                            low_probs(prev, STEPS - 1)
                        if s == 0 and 0 < slot < PHASES:
                            place_v(a)
                        if a is not None and s >= 3:
                            rest_probs(a, s - 3)
                            low_probs(a, s - 3)
                        if slot == 0 and s < LANES - 1:
                            make_masks(s + 1)
                        if slot == 0 and s == 5:
                            pool.wait_ge(w_small, SMALL)
                            pool.tensor_scalar(wq[:, 1:LAYERS, :], wq[:, 1:LAYERS, :], DK ** -0.5, None, ALU.mult)\
                                .then_inc(q_scaled, 1)
                            pool.tensor_scalar(col_bias["bq3"][:, :], col_bias["bq3"][:, :], DK ** -0.5, None, ALU.mult)\
                                .then_inc(q_scaled, 1)
                            pool.wait_ge(tanh_made, 1)
                            for l in (0, 2, 3):
                                pool.tensor_scalar(bo[l][:, :], bo[l][:, :], tanh_g[:, l:l + 1], None, ALU.mult)\
                                    .then_inc(bo_scaled, 1)
                            pool.wait_ge(bo_scaled, 3)
                        if slot in range(1, LANES + 1) and s == 2:
                            make_masks(LANES + slot - 1)
                        if a is not None and s == 6:
                            residual_with_bias(a)
                        if s == 5 and nxt is not None:
                            rstd(an, nxt)
                        if s == 6 and prev is not None:
                            rstd(fn, prev)

            @block.tensor
            def _(pe):
                def mm(o, lhs, rhs, **kw):
                    return nc.tensor.matmul(o, lhs, rhs, **kw)

                def kv_project(n):
                    layer, b = n // LANES, n % LANES
                    pe.wait_ge(w_attn, 48)
                    pe.wait_ge(ctx_loaded[b], 16)
                    if n:
                        pe.wait_ge(qm_ready, GROUPS * n)
                    mm(smax[:, 1, 0:S], wk[:, layer, :], ctx_t[b][:, :], start=True, stop=True).then_inc(k_proj, 1)
                    for t in range(TT):
                        last = mm(smax[:, 1, S + t * D:S + (t + 1) * D], ctx_t[b][:, t * P:(t + 1) * P], wv[:, layer, :],
                                  start=True, stop=True)
                    last.then_inc(v_proj, 1)

                def turn(ln, n, bank):
                    pe.wait_ge(ident_made, 2)
                    pe.wait_ge(ln.normed_done, TT * (n + 1))
                    for t in range(TT):
                        last = nc.tensor.transpose(bank[:, t * P:(t + 1) * P], ln.normed[:, t, :], ident[:, :])
                    last.then_inc(ln.turned, 1)

                def q_project(n):
                    pe.wait_ge(an.turned_sb, n + 1)
                    pe.wait_ge(q_scaled, 1 if n < LANES else 4)
                    mm(smax[:, 0, S:2 * S], wq[:, n // LANES, :], an.normed_t[:, :], start=True, stop=True)\
                        .then_inc(q_proj, 1)

                def spread(n, which, bank, parts_done, done):
                    pe.wait_ge(spread_made, 6 * GROUPS + 1)
                    pe.wait_ge(parts_done, n + 1)
                    flat = bank[:, :, :].rearrange("p a n -> p (a n)")
                    for g in range(GROUPS):
                        o = flat[:, g * S:(g + 1) * S]
                        mm(o, spread_two[which][:, g, :], qkv_hi[which], start=True, stop=False)
                        last = mm(o, spread_one[which][:, g, :], qkv_lo[which], start=False, stop=True)
                    last.then_inc(done, 1)

                def spread_k(n):
                    pe.wait_ge(q_lo, n + 1)
                    pe.wait_ge(v_ready, n + 1)
                    spread(n, "k", smax, k_lo, k_spread)

                def spread_q(n):
                    pe.wait_ge(k_ready, n + 1)
                    spread(n, "q", smax, q_lo, q_spread)

                def strip(h):
                    return slice(32 * (h % GH), 32 * (h % GH) + 32)

                def max_scores(n, s):
                    if s == 0:
                        pe.wait_ge(k_ready, n + 1)
                        pe.wait_ge(q_ready, n + 1)
                    else:
                        pe.wait_ge(max_red, STEPS * n + s)
                        if s % 2 == 0:
                            pe.wait_ge(qm_ready, GROUPS * n + s // 2)
                    for j in range(2):
                        h = 2 * s + j
                        for t in range(TT):
                            last = mm(smax[:, j, t * S:(t + 1) * S], q_stack[strip(h), h // GH, t * P:(t + 1) * P],
                                      k_stack[strip(h), n % 2, h // GH, :], start=(t == 0), stop=(t == TT - 1),
                                      skip_group_check=True)
                    last.then_inc(max_psum, 1)

                def turn_max(n, g):
                    pe.wait_ge(ident_made, 3)
                    pe.wait_ge(max_lo, GROUPS * n + g + 1)
                    for t in range(TT):
                        last = mm(smax[:, 0, t * P:(t + 1) * P], max_parts[:, t, :, :].rearrange("p h r -> p (h r)"),
                                  ident_r[:, :], start=True, stop=True)
                    last.then_inc(max_turned, 1)

                def exp_scores(n, s):
                    layer, b = n // LANES, n % LANES
                    pe.wait_ge(ident_made, 4)
                    if layer < 2:
                        pe.wait_ge(mask_made, masks_for(n))
                    else:
                        pe.wait_ge(decay_made, TT + 3)
                    pe.wait_ge(qm_ready, GROUPS * n + s // 2 + 1)
                    if n or s:
                        pe.wait_ge(exp_done, STEPS * n + s)
                    for j in range(2):
                        h = 2 * s + j
                        score_bias(mm, sexp[:, j, :], b, layer)
                        for t in range(TT):
                            last = mm(sexp[:, j, t * S:(t + 1) * S], k_stack[strip(h), n % 2, h // GH, t * P:(t + 1) * P],
                                      qm_stack[strip(h), h // GH % 2, :], start=False, stop=(t == TT - 1),
                                      skip_group_check=True)
                    last.then_inc(exp_psum, 1)

                def times_v(n, s):
                    layer, k = n // LANES, STEPS * n + s
                    pe.wait_ge(low_ready, k + 1)
                    if s == 0:
                        pe.wait_ge(v_placed, n + 1)
                        pe.wait_ge(v_set, 7)
                        if n:
                            pe.wait_ge(x_new[(n - 1) % LANES], 2 * ((n - 1) // LANES) + 1)
                    if s == HH // 2:
                        pe.wait_ge(sums_copied, 2 * n + 1)
                    for j in range(2):
                        h = 2 * s + j
                        for tq in range(TT):
                            for tk in (tq, 1 - tq):
                                lo, w = window(layer, tk)
                                first, last_q = max(lo, tq * P), min(lo + w, (tq + 1) * P)
                                col = (tq * HH + h % HH) * VC
                                out_rows = slice(first - tq * P, last_q - tq * P)
                                held = slice(first - lo, last_q - lo)
                                for i, part in enumerate((upper(probs[:, k % PROBS, j, tk, :]), upper(rest[:, k % 2, j, tk, :]),
                                                          low[:, k % 2, j, tk, :])):
                                    cols = 1 + (3 - i) * DK
                                    last = mm(cbank[out_rows, col:col + cols], part[:, held],
                                              v_cols[:, n % 2, tk, h, 0:cols],
                                              start=(h % HH == 0 and tq == 0 and tk == 0 and i == 0),
                                              stop=(tk == 1 - tq and i == 2), skip_group_check=True)
                    last.then_inc(pv_done, 1)

                def turn_heads(n):
                    pe.wait_ge(heads_made, 2 * (n + 1))
                    pe.wait_ge(sums_copied, 2 * (n + 1))
                    for t in range(TT):
                        last = nc.tensor.transpose(cbank[:, t * P:(t + 1) * P], heads_tok[:, t, :], ident[:, :])
                    last.then_inc(heads_turned, 1)

                def out_project(n):
                    pe.wait_ge(heads_ready, n + 1)
                    pe.wait_ge(w_out, 16)
                    for t in range(TT):
                        last = mm(cbank[:, S + t * D:S + (t + 1) * D], heads_t[:, t * P:(t + 1) * P], wo[:, n // LANES, :],
                                  start=True, stop=True)
                    last.then_inc(attn_out, 1)

                def logits(n):
                    pe.wait_ge(fn.turned_sb, n + 1)
                    pe.wait_ge(w_small, SMALL)
                    for t in range(TT):
                        last = mm(hbank[:, 1, S + t * EXPERTS:S + (t + 1) * EXPERTS], fn.normed_t[:, t * P:(t + 1) * P],
                                  router[:, n // LANES, :], start=True, stop=True)
                    last.then_inc(logits_psum, 1)

                def up(n, e):
                    layer, done = n // LANES, experts_before(n) + e
                    if layer == 2:
                        pe.wait_ge(w_glu, 64)
                    else:
                        pe.wait_ge(up_split, EXPERTS * UP_LAYERS.index(layer) + e + 1)
                        pe.wait_ge(turned_hi, split_phases(n) + 1)
                        pe.wait_ge(turned_lo, split_phases(n) + 1)
                    if e == 0:
                        pe.wait_ge(gate_step, n + 1)
                    for u in range(2):
                        if done:
                            if layer == 1 and e:
                                pe.wait_ge(pre_ready, 2 * (EXPERTS * (n - LANES) + e - 1) + u + 1)
                            else:
                                pe.wait_ge(hid_ready, 2 * done if layer == 2 or e == 0 else 2 * (done - 1) + u + 1)
                        if e == 0 and n and (n - 1) // LANES in (1, 3):
                            pe.wait_ge(gate_t_ready, biased(n))
                        if layer == 2:
                            last = mm(hbank[:, u, 0:S], (glu_w1, glu_w3)[u][:, e, :], fn.normed_t[:, :],
                                      start=True, stop=True)
                        else:
                            for c in range(2):
                                o, cols = hbank[:, u, c * S:(c + 1) * S], slice((2 * u + c) * P, (2 * u + c + 1) * P)
                                mm(o, up_hi[:, e, cols], normed_hi[:, :], start=True, stop=False)
                                mm(o, up_hi[:, e, cols], normed_lo[:, :], start=False, stop=False)
                                last = mm(o, up_lo[:, e, cols], normed_hi[:, :], start=False, stop=True)
                        last.then_inc(up_psum, 1)

                def down(n, e):
                    layer, done = n // LANES, experts_before(n) + e
                    pe.wait_ge(w_down[layer], 32 if layer == 2 else 16)
                    pe.wait_ge(hid_ready, 2 * (done + 1))
                    if e:
                        pe.wait_ge(y_acc, done)
                    elif n:
                        pe.wait_ge(x_new[(n - 1) % LANES], 2 * ((n - 1) // LANES) + 2)
                    for t in range(TT):
                        o = ybank[:, t * D:(t + 1) * D]
                        if layer == 2:
                            last = mm(o, hidden[:, done % 2, 0, t * P:(t + 1) * P], glu_w2[:, e, :], start=True, stop=True)
                        else:
                            for c in range(CH):
                                last = mm(o, hidden[:, done % 2, c, t * P:(t + 1) * P], down_w[layer][:, e, c, :],
                                          start=(c == 0), stop=(c == CH - 1))
                    last.then_inc(y_psum, 1)

                def turn_gates(n):
                    pe.wait_ge(gate_ready, n + 1)
                    pe.wait_ge(hid_ready, 2 * experts_before(n + 1))
                    for t in range(TT):
                        last = nc.tensor.transpose(hbank[:, 0, t * P:(t + 1) * P], gate_pad[:, t, :], ident[:, :])
                    last.then_inc(gate_turned, 1)

                def output_bias(n):
                    layer = n // LANES
                    pe.wait_ge(gate_t_ready, biased(n) + 1)
                    pe.wait_ge(y_acc, experts_before(n + 1))
                    for t in range(TT):
                        last = mm(ybank[:, t * D:(t + 1) * D], gate_t[:, t * P:(t + 1) * P], out_bias[layer][:, :],
                                  start=True, stop=True)
                    last.then_inc(bias_psum, 1)

                def sum_step(slot, s):
                    a, _, _, prev = phases(slot)
                    if prev is not None and s < 2:
                        times_v(prev, STEPS - 2 + s)
                    if a is not None and 4 <= s <= STEPS:
                        times_v(a, s - 4)

                kv_project(0)
                turn(an, 0, smax[:, 0, :])
                q_project(0)
                spread_k(0)
                spread_q(0)
                for slot in range(PHASES + LAG):
                    a, f, nxt, prev = phases(slot)
                    if f is not None:
                        up(f, 0)
                    for s in range(SLOT_STEPS):
                        layer = f // LANES if f is not None else None
                        more = f is not None and s + 1 < experts(layer)
                        if a is not None and s < STEPS:
                            max_scores(a, s)
                        if nxt is not None and s == STEPS:
                            kv_project(nxt)
                            turn(an, nxt, smax[:, 0, :])
                        if nxt is not None and s == STEPS + 1:
                            spread_k(nxt)
                        if f is not None and 1 <= s <= experts(f // LANES):
                            down(f, s - 1)
                        if nxt is not None and s == STEPS:
                            q_project(nxt)
                        turn_next = a is not None and s < STEPS and s % 2
                        if turn_next and layer == 1:
                            turn_max(a, s // 2)
                        if more and layer != 2:
                            up(f, s + 1)
                        if prev is not None and s == STEPS + 1:
                            if f is not None:
                                pe.wait_ge(hid_ready, 2 * experts_before(prev))
                            turn(fn, prev, hbank[:, 1, :])
                        if s == EXPERTS + 1 and layer in (1, 3):
                            turn_gates(f)
                        if prev is not None and s == 2:
                            turn_heads(prev)
                        if prev is not None and s == 3:
                            out_project(prev)
                        if layer not in (2, None):
                            sum_step(slot, s)
                            if turn_next and layer != 1:
                                turn_max(a, s // 2)
                        if a is not None and 2 <= s < STEPS + 2:
                            exp_scores(a, s - 2)
                        if layer in (2, None):
                            if turn_next and layer is None:
                                turn_max(a, s // 2)
                            sum_step(slot, s)
                            if turn_next and layer == 2:
                                turn_max(a, s // 2)
                            if more:
                                up(f, s + 1)
                        if prev is not None and s == STEPS + 1:
                            logits(prev)
                        if nxt is not None and s == STEPS + 1:
                            spread_q(nxt)
                        if s == EXPERTS + 1 and layer in (1, 3):
                            output_bias(f)
                        if a is not None and s == STEPS + 1:
                            times_v(a, s - 4)

            @block.scalar
            def _(act):
                def high_part(n, which, proj, done, src):
                    layer = n // LANES
                    act.wait_ge(proj, n + 1)
                    if which == "k":
                        act.wait_ge(v_proj, n + 1)
                    if n:
                        act.wait_ge(q_spread if which == "q" else k_spread, n)
                    if layer == 3:
                        act.wait_ge(q_scaled, 4)
                    if layer in (0, 3):
                        i = act.activation(qkv_hi[which], src, ACT.Identity, bias=col_bias[f"b{which}{layer}"][:, :])
                    else:
                        i = act.activation(qkv_hi[which], src, ACT.Copy)
                    i.then_inc(done, 1)

                def copy_turned(ln, n, bank):
                    act.wait_ge(ln.turned, n + 1)
                    act.activation(ln.normed_t[:, :], bank[:, 0:S], ACT.Copy).then_inc(ln.turned_sb, 1)

                def copy_turned_high(n):
                    if n // LANES != 2:
                        act.wait_ge(fn.turned, n + 1)
                        act.activation(normed_hi[:, :], hbank[:, 1, 0:S], ACT.Copy).then_inc(turned_hi, 1)

                def copy_q_stack(n):
                    act.wait_ge(q_spread, n + 1)
                    act.activation(q_stack[:, :, :].rearrange("p g n -> p (g n)"),
                                   smax[:, :, :].rearrange("p a n -> p (a n)"), ACT.Copy).then_inc(q_ready, 1)

                def exp_logits(n):
                    act.wait_ge(gate_step, n + 1)
                    act.wait_ge(gate_shifted, n + 1)
                    act.activation(exp_l[:, :, :], shifted[:, :, :], ACT.Exp).then_inc(exp_l_done, 1)

                def exponentials(n, s):
                    layer, k = n // LANES, STEPS * n + s
                    act.wait_ge(exp_psum, k + 1)
                    if k >= PROBS:
                        act.wait_ge(pv_done, k + 1 - PROBS)
                    if layer == 2:
                        for t in range(TT):
                            lo, w = window(layer, t)
                            last = act.activation(probs[:, k % PROBS, :, t, 0:w], sexp[:, :, t * S + lo:t * S + lo + w], ACT.Exp)
                    else:
                        last = act.activation(probs[:, k % PROBS, :, :, :].rearrange("p j t n -> p (j t n)"),
                                              sexp[:, :, :].rearrange("p j n -> p (j n)"), ACT.Exp)
                    last.then_inc(exp_done, 1)

                def high_up(j):
                    i, e = j // EXPERTS, j % EXPERTS
                    act.wait_ge(up_loaded[j % UP_RING], 16 * (j // UP_RING + 1))
                    if i:
                        before = UP_LAYERS[i - 1] * LANES + LANES - 1
                        act.wait_ge(up_psum, 2 * (experts_before(before) + e + 1))
                    act.activation(up_hi[:, e, :], up_in[:, j % UP_RING, :], ACT.Copy).then_inc(up_rounded, 1)

                def copy_sums(n, u):
                    act.wait_ge(pv_done, STEPS * n + (u + 1) * HH // 2)
                    if n:
                        act.wait_ge(heads_made, 2 * n)
                    act.activation(sums[:, u, :, :].rearrange("p a c -> p (a c)"), cbank[:, 0:TT * HH * VC], ACT.Copy)\
                       .then_inc(sums_copied, 1)

                def copy_heads(n):
                    act.wait_ge(heads_turned, n + 1)
                    act.activation(heads_t, cbank[:, 0:S], ACT.Copy).then_inc(heads_ready, 1)

                def hidden_units(n, e):
                    layer, done = n // LANES, experts_before(n) + e
                    for u in range(2):
                        act.wait_ge(up_psum, 2 * done + u + 1)
                        if layer == 0:
                            if done >= 2:
                                act.wait_ge(y_psum, done - 1)
                            elif u == 0:
                                act.wait_ge(decay_made, TT + 3)
                            act.activation(hidden[:, done % 2, 2 * u:2 * u + 2, :].rearrange("p c n -> p (c n)"),
                                           hbank[:, u, :], ACT.Relu).then_inc(hid_ready, 1)
                        elif layer == 3:
                            act.wait_ge(y_psum, done - 1)
                            for c in range(2):
                                last = act.activation(hidden[:, done % 2, 2 * u + c, :], hbank[:, u, c * S:(c + 1) * S],
                                                      ACT.Relu, bias=hid_bias[3][:, e, 2 * u + c:2 * u + c + 1])
                            last.then_inc(hid_ready, 1)
                        elif layer == 1:
                            if e or n > LANES:
                                act.wait_ge(hid_ready, 2 * (done - 1) + u + 1)
                            else:
                                act.wait_ge(mask_made, 4 * LANES)
                            for to, func in ((pre_act, ACT.Identity), (gelu_t, ACT.Square)):
                                for c in range(2):
                                    last = act.activation(to[:, u, c, :], hbank[:, u, c * S:(c + 1) * S],
                                                          func, bias=hid_bias[1][:, e, 2 * u + c:2 * u + c + 1])
                            last.then_inc(pre_ready, 1)
                        elif u == 0:
                            if done > experts_before(2 * LANES):
                                act.wait_ge(hid_ready, 2 * done)
                            act.activation(pre_act[:, 0, 0, :], hbank[:, 0, 0:S], ACT.Tanh, scale=0.5)\
                               .then_inc(glu_tanh, 1)

                def gelu_tanh(n, e):
                    for u in range(2):
                        act.wait_ge(inner_ready, 2 * (EXPERTS * (n - LANES) + e) + u + 1)
                        act.activation(gelu_t[:, u, :, :], gelu_t[:, u, :, :], ACT.Tanh, scale=GELU_C * GELU_A)\
                           .then_inc(tanh_ready, 1)

                def copy_gates(n):
                    act.wait_ge(gate_turned, biased(n) + 1)
                    act.activation(gate_t, hbank[:, 0, 0:S], ACT.Copy).then_inc(gate_t_ready, 1)

                act.wait_ge(w_first, FIRST)
                high_part(0, "k", k_proj, k_hi, smax[:, 1, 0:S])
                copy_turned(an, 0, smax[:, 0, :])
                act.wait_ge(q_scaled, 2)
                high_part(0, "q", q_proj, q_hi, smax[:, 0, S:2 * S])
                copy_q_stack(0)
                act.wait_ge(w_small, SMALL)
                act.activation(tanh_g[:, :], gates[:, :], ACT.Tanh).then_inc(tanh_made, 1)
                for slot in range(PHASES + LAG):
                    a, f, nxt, prev = phases(slot)
                    if f is not None:
                        hidden_units(f, 0)
                    for s in range(SLOT_STEPS):
                        if f is not None and f // LANES == 1 and s < EXPERTS:
                            gelu_tanh(f, s)
                        if nxt is not None and s == STEPS:
                            copy_turned(an, nxt, smax[:, 0, :])
                            high_part(nxt, "k", k_proj, k_hi, smax[:, 1, 0:S])
                            high_part(nxt, "q", q_proj, q_hi, smax[:, 0, S:2 * S])
                        if prev is not None and s == 2:
                            copy_heads(prev)
                        if prev is not None and s == 1:
                            copy_sums(prev, 1)
                        if a is not None and s == 3 + HH // 2:
                            copy_sums(a, 0)
                        glu = f is not None and f // LANES == 2 and s <= STEPS
                        if glu and 2 <= s and a is not None:
                            exponentials(a, s - 2)
                        if f is not None and s + 1 < experts(f // LANES):
                            hidden_units(f, s + 1)
                        if prev is not None and s == STEPS + 1:
                            copy_turned_high(prev)
                            copy_turned(fn, prev, hbank[:, 1, :])
                        if f is not None and s == EXPERTS + 1 and f // LANES in (1, 3):
                            copy_gates(f)
                        if a is not None and 2 <= s and not glu:
                            exponentials(a, s - 2)
                        if (slot, s) in splits:
                            high_up(splits[slot, s])
                        if nxt is not None and s == STEPS + 1:
                            copy_q_stack(nxt)
                        if prev is not None and s == STEPS + 1:
                            exp_logits(prev)

            @block.vector
            def _(dve):
                def statistics(ln, n, kind):
                    dve.wait_ge(*x_ready(n, kind))
                    for t in range(TT):
                        dve.bn_stats(ln.stats[:, t, :], x[n % LANES][:, t, :]).then_inc(ln.stats_done, 1)
                    dve.wait_ge(ln.stats_done, TT * (n + 1))
                    for t in range(TT):
                        dve.bn_aggr(ln.mean_var[:, t, :], ln.stats[:, t, :]).then_inc(ln.aggr_done, 1)

                def normalise(ln, n):
                    dve.wait_ge(ln.rstd_done, n + 1)
                    if n:
                        dve.wait_ge(ln.turned, n)
                    for t in range(TT):
                        dve.tensor_scalar(ln.normed[:, t, :], x[n % LANES][:, t, :], ln.mean_var[:, t, 0:1],
                                          ln.rstd[:, t:t + 1], ALU.subtract, ALU.mult).then_inc(ln.normed_done, 1)

                def turned_low_part(n):
                    if n // LANES != 2:
                        dve.wait_ge(turned_hi, split_phases(n) + 1)
                        dve.wait_ge(fn.turned_sb, n + 1)
                        dve.tensor_tensor(normed_lo[:, :], fn.normed_t[:, :], normed_hi[:, :].bitcast(F32), ALU.subtract)\
                           .then_inc(turned_lo, 1)

                def low_part(n, which, hi_done, done, src):
                    layer = n // LANES
                    dve.wait_ge(hi_done, n + 1)
                    bias = col_bias[f"b{which}{layer}"][:, :] if layer in (0, 3) else 0.0
                    dve.scalar_tensor_tensor(out=qkv_lo[which], in0=src, scalar=bias,
                                             in1=qkv_hi[which].bitcast(F32), op0=ALU.add, op1=ALU.subtract)\
                       .then_inc(done, 1)

                def take_v(n):
                    layer = n // LANES
                    dve.wait_ge(v_proj, n + 1)
                    if n:
                        dve.wait_ge(v_placed, n)
                    src = smax[:, 1, S:2 * S].rearrange("p (t n) -> p t n", t=TT)
                    if layer in (0, 3):
                        i = dve.tensor_tensor(v_tmp[:, :, :], src, bv[layer][:, :].unsqueeze(1).broadcast_to([P, TT, D]),
                                              ALU.add)
                    else:
                        i = dve.tensor_copy(v_tmp[:, :, :], src)
                    i.then_inc(v_ready, 1)

                def copy_k_stack(n):
                    dve.wait_ge(k_spread, n + 1)
                    if n >= 2:
                        dve.wait_ge(exp_psum, STEPS * (n - 1))
                    dve.tensor_scalar(k_stack[:, n % 2, :, :].rearrange("p g n -> p (g n)"),
                                      smax[:, :, :].rearrange("p a n -> p (a n)"), ones_rows[:, 0:1], None,
                                      ALU.add).then_inc(k_ready, 1)

                def make_decay():
                    dve.wait_ge(iota_made, 1)
                    dve.tensor_copy(dist, iota_i).then_inc(dist_made, 1)
                    dve.wait_ge(dist_made, 1)
                    dve.tensor_scalar(dist_neg, dist, -1.0, None, ALU.mult).then_inc(dist_made, 1)
                    dve.wait_ge(dist_made, 2)
                    dve.tensor_tensor(dist, dist, dist_neg, ALU.max).then_inc(dist_made, 1)
                    dve.wait_ge(dist_made, 3)
                    for t in range(TT):
                        lo, n = window(2, t)
                        dve.tensor_scalar(band[:, t, :], dist[:, t, lo:lo + n], float(WINDOW), -BIG, ALU.is_gt, ALU.mult)\
                           .then_inc(decay_made, 1)
                    dve.wait_ge(w_small, SMALL)
                    dve.tensor_scalar(dist_neg, dist, time_decay[:, 0:1], -1.0, ALU.mult, ALU.mult)\
                       .then_inc(dist_made, 1)
                    dve.wait_ge(dist_made, 4)
                    dve.tensor_copy(decay[:, :, :], dist_neg).then_inc(decay_made, 1)
                    dve.tensor_copy(decay_hi[:, :, :], dist_neg).then_inc(decay_made, 1)
                    dve.wait_ge(decay_made, TT + 2)
                    dve.tensor_tensor(decay_lo[:, :, :], dist_neg, decay_hi[:, :, :].bitcast(F32), ALU.subtract)\
                       .then_inc(decay_made, 1)
                    dve.wait_ge(decay_made, TT + 3)

                def reduce_max(n, s):
                    layer, b = n // LANES, n % LANES
                    if layer < 2 and s == 0:
                        dve.wait_ge(mask_made, masks_for(n))
                    dve.wait_ge(max_psum, STEPS * n + s + 1)
                    if s == 0 and n:
                        dve.wait_ge(max_lo, GROUPS * n)
                    for j in range(2):
                        for t in range(TT):
                            lo, w = window(layer, t)
                            bias = {0: mask[b][0], 1: mask[b][0], 2: band, 3: decay}[layer][:, t, :]
                            scores = smax[:, j, t * S + lo:t * S + lo + w]
                            last = dve.tensor_tensor_reduce(scores, scores, bias, 1.0, -3.0e38, ALU.add, ALU.max,
                                                            row_max[:, 2 * s + j, t:t + 1])
                    last.then_inc(max_red, 1)

                def split_max(n, g):
                    dve.wait_ge(max_red, STEPS * n + 2 * g + 2)
                    if GROUPS * n + g:
                        dve.wait_ge(max_turned, GROUPS * n + g)
                    src = row_max[:, GH * g:GH * g + GH, :].rearrange("p h t -> p t h")
                    hi, lo = max_parts[:, :, :, 3 * DK], max_parts[:, :, :, 3 * DK + 1]
                    dve.tensor_scalar(hi, src, -1.0, None, ALU.mult).then_inc(max_hi, 1)
                    dve.wait_ge(max_hi, GROUPS * n + g + 1)
                    dve.scalar_tensor_tensor(out=lo, in0=src, scalar=-1.0, in1=hi.bitcast(F32),
                                             op0=ALU.mult, op1=ALU.subtract).then_inc(max_lo, 1)

                def add_max(n, g):
                    dve.wait_ge(max_turned, GROUPS * n + g + 1)
                    if GROUPS * n + g >= 2:
                        dve.wait_ge(exp_psum, STEPS * n + 2 * g - 2)
                    dve.tensor_tensor(qm_stack[:, g % 2, :], smax[:, 0, 0:S], q_stack[:, g, :].bitcast(F32), ALU.add)\
                       .then_inc(qm_ready, 1)

                def low_up(j):
                    i, e = j // EXPERTS, j % EXPERTS
                    dve.wait_ge(up_rounded, j + 1)
                    dve.tensor_tensor(up_lo[:, e, :], up_in[:, j % UP_RING, :], up_hi[:, e, :].bitcast(F32),
                                      ALU.subtract).then_inc(up_split, 1)

                def rest_probs(n, s):
                    k = STEPS * n + s
                    dve.wait_ge(exp_done, k + 1)
                    if k >= 2:
                        dve.wait_ge(pv_done, k - 1)
                        dve.wait_ge(low_ready, k - 1)
                    last = each_window(n, s, (0,), lambda o: dve.tensor_tensor(o(rest), o(probs), upper(o(probs)), ALU.subtract))
                    last.then_inc(rest_ready, 1)

                def heads_out(n, u):
                    i = 2 * n + u
                    dve.wait_ge(sums_copied, i + 1)
                    if n:
                        dve.wait_ge(heads_turned, n)
                    one, v1, v2, v3 = (sums[:, u, :, lo:hi] for lo, hi in ((0, 1), (1, 9), (9, 17), (17, 25)))
                    if i:
                        dve.wait_ge(heads_made, i)
                    dve.tensor_tensor(part_sum[:, :, :], v2, v3, ALU.add).then_inc(heads_chain, 1)
                    dve.reciprocal(inv_sum[:, :], one.rearrange("p a c -> p (a c)")).then_inc(heads_chain, 1)
                    dve.wait_ge(heads_chain, 3 * i + 1)
                    dve.tensor_tensor(part_sum[:, :, :], part_sum[:, :, :], v1, ALU.add).then_inc(heads_chain, 1)
                    dve.wait_ge(heads_chain, 3 * i + 3)
                    dst = heads_tok[:, :, u * D // 2:(u + 1) * D // 2].rearrange("p t (h d) -> p t h d", d=DK)
                    dve.tensor_tensor(dst, part_sum[:, :, :].rearrange("p (t h) d -> p t h d", t=TT),
                                      inv_sum[:, :].rearrange("p (t h) -> p t h", t=TT).unsqueeze(3)
                                      .broadcast_to([P, TT, HH, DK]), ALU.mult).then_inc(heads_made, 1)

                def attention_sum(n):
                    layer, b = n // LANES, n % LANES
                    dve.wait_ge(attn_out, n + 1)
                    src = x[b]
                    if layer != 1:
                        dve.wait_ge(res_ready, n + 1 if n < LANES else n + 1 - LANES)
                        src = x_res
                    dve.scalar_tensor_tensor(out=x[b][:, :, :].rearrange("p t n -> p (t n)"), in0=cbank[:, S:2 * S],
                                             scalar=tanh_g[:, layer:layer + 1],
                                             in1=src[:, :, :].rearrange("p t n -> p (t n)"),
                                             op0=ALU.mult, op1=ALU.add).then_inc(x_new[b], 1)

                def bc(ap):
                    return ap.unsqueeze(2).broadcast_to([P, TT, EXPERTS])

                def read_logits(n):
                    layer = n // LANES
                    dve.wait_ge(logits_psum, n + 1)
                    src = hbank[:, 1, S:S + TT * EXPERTS].rearrange("p (t e) -> p t e", t=TT)
                    if layer == 3:
                        b3 = route_bias[3][:, :].unsqueeze(1).broadcast_to([P, TT, EXPERTS])
                        i = dve.tensor_tensor(logit[:, :, :], src, b3, ALU.add)
                    else:
                        i = dve.tensor_copy(logit[:, :, :], src)
                    i.then_inc(gate_step, 1)
                    dve.wait_ge(gate_step, n + 1)
                    dve.tensor_reduce(logit_max[:, :], logit[:, :, :], AX, ALU.max).then_inc(gate_max, 1)
                    dve.wait_ge(gate_max, n + 1)
                    dve.tensor_tensor(shifted[:, :, :], logit[:, :, :], bc(logit_max[:, :]), ALU.subtract)\
                       .then_inc(gate_shifted, 1)

                def chained(before):
                    steps = [before]

                    def done(i):
                        i.then_inc(gate_chain, 1)
                        steps[0] += 1
                        dve.wait_ge(gate_chain, steps[0])

                    return steps, done

                def choose_experts(n):
                    layer = n // LANES
                    steps, done = chained(sum(GATE_LINKS[m // LANES] for m in range(n)))
                    dve.wait_ge(exp_l_done, n + 1)
                    done(dve.tensor_reduce(exp_sum[:, :], exp_l[:, :, :], AX, ALU.add))
                    done(dve.reciprocal(exp_inv[:, :], exp_sum[:, :]))
                    done(dve.tensor_tensor(prob[:, :, :], exp_l[:, :, :], bc(exp_inv[:, :]), ALU.mult))
                    if layer == 2:
                        b2 = route_bias[2][:, :].unsqueeze(1).broadcast_to([P, TT, EXPERTS])
                        done(dve.tensor_tensor(choice[:, :, :], prob[:, :, :], b2, ALU.add))
                    key = choice if layer == 2 else prob
                    dve.max(top8[:, 0, :], key[:, 0, :])
                    done(dve.max(top8[:, 1, :], key[:, 1, :]))
                    dve.max_index(top_idx[:, 0, :], top8[:, 0, :], key[:, 0, :])
                    done(dve.max_index(top_idx[:, 1, :], top8[:, 1, :], key[:, 1, :]))
                    done(dve.tensor_copy(top_f[:, :, :], top_idx[:, :, :]))
                    assert steps[0] == sum(GATE_LINKS[m // LANES] for m in range(n)) + CHOICE_LINKS[layer]

                def make_gates(n):
                    layer = n // LANES
                    steps, done = chained(sum(GATE_LINKS[m // LANES] for m in range(n)) + CHOICE_LINKS[layer])
                    i8 = iota8[:, :].unsqueeze(1).broadcast_to([P, TT, EXPERTS])
                    if layer == 3:
                        done(dve.tensor_tensor(picked[:, :, :], i8, bc(top_f[:, :, 0]), ALU.is_equal))
                    else:
                        dve.tensor_tensor(pick1[:, :, :], i8, bc(top_f[:, :, 0]), ALU.is_equal)
                        done(dve.tensor_tensor(pick2[:, :, :], i8, bc(top_f[:, :, 1]), ALU.is_equal))
                        done(dve.tensor_tensor(picked[:, :, :], pick1[:, :, :], pick2[:, :, :], ALU.add))
                    gate = gate_pad[:, :, 0:EXPERTS]
                    if layer >= 2:
                        done(dve.tensor_tensor(gate, picked[:, :, :], prob[:, :, :], ALU.mult))
                    else:
                        done(dve.tensor_tensor(gate_raw[:, :, :], picked[:, :, :], prob[:, :, :], ALU.mult))
                        done(dve.tensor_reduce(gate_sum[:, :], gate_raw[:, :, :], AX, ALU.add))
                        done(dve.reciprocal(gate_inv[:, :], gate_sum[:, :]))
                        done(dve.tensor_tensor(gate, gate_raw[:, :, :], bc(gate_inv[:, :]), ALU.mult))
                    dve.tensor_scalar(gate_use[:, :, :], gate, 0.5 if layer in (1, 2) else 1.0, None, ALU.mult)\
                       .then_inc(gate_ready, 1)
                    assert steps[0] == sum(GATE_LINKS[m // LANES] for m in range(n + 1))

                def gelu_inner(n, e):
                    for u in range(2):
                        dve.wait_ge(pre_ready, 2 * (EXPERTS * (n - LANES) + e) + u + 1)
                        dve.scalar_tensor_tensor(out=gelu_t[:, u, :, :], in0=gelu_t[:, u, :, :], scalar=1.0 / GELU_A,
                                                 in1=pre_act[:, u, :, :], op0=ALU.add, op1=ALU.mult)\
                           .then_inc(inner_ready, 1)

                def gelu_out(n, e):
                    done = experts_before(n) + e
                    for u in range(2):
                        dve.wait_ge(tanh_ready, 2 * (EXPERTS * (n - LANES) + e) + u + 1)
                        dve.wait_ge(y_psum, done - 1)
                        dve.scalar_tensor_tensor(out=hidden[:, done % 2, 2 * u:2 * u + 2, :], in0=gelu_t[:, u, :, :],
                                                 scalar=1.0, in1=pre_act[:, u, :, :], op0=ALU.add, op1=ALU.mult)\
                           .then_inc(hid_ready, 1)

                def glu_hidden(n, e):
                    done = experts_before(n) + e
                    dve.wait_ge(glu_tanh, done - experts_before(2 * LANES) + 1)
                    dve.scalar_tensor_tensor(out=gelu_t[:, 0, 0, :], in0=pre_act[:, 0, 0, :], scalar=1.0,
                                             in1=hbank[:, 0, 0:S], op0=ALU.add, op1=ALU.mult).then_inc(hid_ready, 1)
                    dve.wait_ge(hid_ready, 2 * done + 1)
                    dve.wait_ge(up_psum, 2 * done + 2)
                    dve.wait_ge(y_psum, done - 1)
                    dve.tensor_tensor(hidden[:, done % 2, 0, :], hbank[:, 1, 0:S], gelu_t[:, 0, 0, :], ALU.mult)\
                       .then_inc(hid_ready, 1)

                def add_expert(n, e):
                    layer, done = n // LANES, experts_before(n) + e
                    dve.wait_ge(y_psum, done + 1)
                    if e == 0:
                        dve.wait_ge(gate_ready, n + 1)
                    else:
                        dve.wait_ge(y_acc, done)
                    for t in range(TT):
                        o, y = acc[:, t, :], ybank[:, t * D:(t + 1) * D]
                        g = 0.5 if e == EXPERTS else gate_use[:, t, e:e + 1]
                        if e == 0:
                            last = dve.tensor_scalar(o, y, g, None, ALU.mult)
                        else:
                            last = dve.scalar_tensor_tensor(out=o, in0=y, scalar=g, in1=o, op0=ALU.mult, op1=ALU.add)
                    last.then_inc(y_acc, 1)

                def add_output_bias(n):
                    k = biased(n) + 1
                    dve.wait_ge(bias_psum, k)
                    dve.wait_ge(y_acc, experts_before(n + 1))
                    dve.tensor_tensor(acc[:, :, :].rearrange("p t n -> p (t n)"), ybank[:, 0:S],
                                      acc[:, :, :].rearrange("p t n -> p (t n)"), ALU.add).then_inc(bias_added, 1)
                    dve.wait_ge(bias_added, k)

                def expert_sum(n):
                    layer, b = n // LANES, n % LANES
                    dve.wait_ge(y_acc, experts_before(n + 1))
                    dve.scalar_tensor_tensor(out=x[b][:, :, :], in0=acc[:, :, :],
                                             scalar=tanh_g[:, LAYERS + layer:LAYERS + layer + 1], in1=x[b][:, :, :],
                                             op0=ALU.mult, op1=ALU.add).then_inc(x_new[b], 1)

                for t in (spread_two["q"], spread_two["k"], spread_one["q"], spread_one["k"]):
                    dve.memset(t[:, :, :].bitcast(F32), 0.0).then_inc(v_set, 1)
                statistics(an, 0, 0)
                dve.memset(max_parts[:, :, :, :].bitcast(F32), 0.0).then_inc(v_set, 1)
                for i in range(2):
                    dve.memset(v_cols[:, i, :, :, 0], 1.0).then_inc(v_set, 1)
                dve.wait_ge(v_set, 7)
                dve.wait_ge(ident_made, 2)
                for g in range(GROUPS):
                    src = ident[:, g * 32:(g + 1) * 32].rearrange("p (h d) -> p h d", d=DK)
                    for t, copies in ((spread_two["q"], (0, 1)), (spread_one["q"], (2,)),
                                      (spread_two["k"], (0, 2)), (spread_one["k"], (1,))):
                        for c in copies:
                            dst = t[:, g, :].rearrange("p (h r) -> p h r", r=32)[:, :, c * DK:(c + 1) * DK]
                            dve.tensor_copy(dst, src).then_inc(spread_made, 1)
                rows = ident[:, :].rearrange("p (h r) -> p h r", r=32)[:, :, 3 * DK:3 * DK + 2]
                dve.tensor_reduce(ones_rows[:, :], rows, mybir.AxisListType.XY, ALU.add).then_inc(spread_made, 1)
                normalise(an, 0)
                dve.wait_ge(w_first, FIRST)
                dve.wait_ge(q_scaled, 2)
                dve.wait_ge(spread_made, 6 * GROUPS + 1)
                low_part(0, "k", k_hi, k_lo, smax[:, 1, 0:S])
                take_v(0)
                low_part(0, "q", q_hi, q_lo, smax[:, 0, S:2 * S])
                copy_k_stack(0)
                for slot in range(PHASES + LAG):
                    a, f, nxt, prev = phases(slot)
                    fl = f // LANES if f is not None else None
                    if fl == 2:
                        glu_hidden(f, 0)
                    if prev is not None:
                        rest_probs(prev, STEPS - 1)
                    if f is not None and fl != 2:
                        choose_experts(f)
                    if fl == 1:
                        gelu_inner(f, 0)
                    for s in range(SLOT_STEPS):
                        if fl == 2 and 1 <= s < experts(2):
                            glu_hidden(f, s)
                        if a is not None and s < STEPS:
                            reduce_max(a, s)
                            if s % 2:
                                split_max(a, s // 2)
                        if fl == 1 and 1 <= s < EXPERTS:
                            gelu_inner(f, s)
                        if fl == 1 and s == 0:
                            gelu_out(f, 0)
                        if fl == 2 and s == 0:
                            choose_experts(f)
                        if f is not None and s == 0:
                            make_gates(f)
                        if nxt is not None and s == STEPS:
                            low_part(nxt, "k", k_hi, k_lo, smax[:, 1, 0:S])
                            take_v(nxt)
                        if nxt is not None and s == STEPS + 1:
                            copy_k_stack(nxt)
                        if f is not None and 1 <= s <= experts(fl):
                            add_expert(f, s - 1)
                        if (slot, s - 1) in splits:
                            low_up(splits[slot, s - 1])
                        if s == 0 and (slot - 1, SLOT_STEPS - 1) in splits:
                            low_up(splits[slot - 1, SLOT_STEPS - 1])
                        if nxt is not None and s == STEPS:
                            low_part(nxt, "q", q_hi, q_lo, smax[:, 0, S:2 * S])
                        if fl == 1 and a is not None and s < STEPS and s % 2:
                            add_max(a, s // 2)
                        if fl == 1 and 1 <= s < EXPERTS:
                            gelu_out(f, s)
                        if a is not None and s >= 3:
                            rest_probs(a, s - 3)
                        if fl != 1 and a is not None and s < STEPS and s % 2:
                            add_max(a, s // 2)
                        if prev is not None and s == STEPS + 1:
                            turned_low_part(prev)
                            read_logits(prev)
                        if slot == 0 and s == STEPS - 1:
                            make_decay()
                        if s == 1 and prev is not None:
                            heads_out(prev, 1)
                        if s == 3 and prev is not None:
                            attention_sum(prev)
                        if a is not None and s == 3 + HH // 2:
                            heads_out(a, 0)
                        if f is not None and s == EXPERTS + 1:
                            if fl in (1, 3):
                                add_output_bias(f)
                            expert_sum(f)
                        if s == 4 and nxt is not None:
                            statistics(an, nxt, 0)
                        if s == 5 and prev is not None:
                            statistics(fn, prev, 1)
                        if s == 6 and nxt is not None:
                            normalise(an, nxt)
                        if s == 7 and prev is not None:
                            normalise(fn, prev)


def _layers_of(inputs):
    import numpy as _np

    def a(name):
        return _np.asarray(inputs[name])

    def t(name):
        return a(name).T

    m0, m1 = a("mask_BxSxS2_ik1"), a("mask_Bx1xSxS2_ik0")[:, 0]
    return {
        "x": a("x"),
        "ctx_t": a("ctx_1024").transpose(0, 2, 1),
        "mask00": m0, "mask01": m0.transpose(0, 2, 1),
        "mask10": m1, "mask11": m1.transpose(0, 2, 1),
        "gates": _np.concatenate([a("g_xattn"), a("g_ffn")]),
        "wq": _np.stack([t("L0_xattn_Wq"), t("L1_xattn_w_q"), t("L2_xattn_Wq"), t("L3_xattn_wq")]),
        "wk": _np.stack([t("L0_xattn_Wk"), t("L1_xattn_w_k"), t("L2_xattn_Wk"), t("L3_xattn_wk")]),
        "wv": _np.stack([t("L0_xattn_Wv"), t("L1_xattn_w_v"), t("L2_xattn_Wv"), t("L3_xattn_wv")]),
        "wo": _np.stack([t("L0_xattn_Wo"), t("L1_xattn_w_o"), t("L2_xattn_Wo"), t("L3_xattn_wo")]),
        "bq0": a("L0_xattn_bq"), "bk0": a("L0_xattn_bk"), "bv0": a("L0_xattn_bv"), "bo0": a("L0_xattn_bo"),
        "bq3": a("L3_xattn_bq"), "bk3": a("L3_xattn_bk"), "bv3": a("L3_xattn_bv"), "bo3": a("L3_xattn_bo"),
        "bo2": a("L2_xattn_bo"), "time_decay": a("L3_xattn_time_decay").reshape(1),
        "router": _np.stack([a("L0_ffn_Wr"), t("L1_ffn_router_w"), a("L2_ffn_router_w"), a("L3_ffn_Wr")]),
        "route_bias2": a("L2_ffn_expert_bias"), "route_bias3": a("L3_ffn_br"),
        "up_w0": a("L0_ffn_W1"), "down_w0": a("L0_ffn_W2"),
        "up_w1": a("L1_ffn_w_fc"), "down_w1": a("L1_ffn_w_proj"),
        "up_w3": a("L3_ffn_W1"), "down_w3": a("L3_ffn_W2"),
        "hid_bias1": a("L1_ffn_b_fc").reshape(EXPERTS * CH, P).T, "out_bias1": a("L1_ffn_b_proj"),
        "hid_bias3": a("L3_ffn_b1").reshape(EXPERTS * CH, P).T, "out_bias3": a("L3_ffn_b2"),
        "glu_w1": a("L2_ffn_w1"), "glu_w2": a("L2_ffn_w2"), "glu_w3": a("L2_ffn_w3"),
        "sglu_w1": a("L2_ffn_sw1"), "sglu_w2": a("L2_ffn_sw2"), "sglu_w3": a("L2_ffn_sw3"),
    }


def kernel(**inputs):
    import numpy as _np
    import concourse.bacc as _bacc
    from concourse import mybir as _mybir
    from concourse.bass_utils import run_bass_kernel_spmd as _run

    nc = _bacc.Bacc("TRN2", target_bir_lowering=False, num_devices=1)
    arrays, ins = {}, {}
    for name, value in _layers_of(inputs).items():
        value = _np.ascontiguousarray(value)
        arrays[f"in_{name}"] = value
        ins[name] = nc.dram_tensor(f"in_{name}", value.shape, _mybir.dt.from_np(value.dtype), kind="ExternalInput").ap()
    out = nc.dram_tensor("out_0", (BATCH, S, D), F32, kind="ExternalOutput").ap()
    flamingo_layers(nc, ins, out)
    r = _run(nc, [arrays], core_ids=[0])
    return r.results[0]["out_0"]
```
